# Optimizing a Trainium2 kernel written in Bass

```python
import numpy as np
import jax
import jax.numpy as jnp

def _softmax(x, axis=-1):
    return jax.nn.softmax(x, axis=axis)

def _gelu(x):
    return jax.nn.gelu(x, approximate=True)

def _silu(x):
    return jax.nn.silu(x)

def _sigmoid(x):
    return jax.nn.sigmoid(x)

def _layernorm(x, axis=-1, eps=1e-05):
    m = jnp.mean(x, axis=axis, keepdims=True)
    v = jnp.var(x, axis=axis, keepdims=True)
    return (x - m) / jnp.sqrt(v + eps)

def _scatter_add(tgt, idx, src, axis=0):
    return tgt.at[idx].add(src)

def _segment_sum(src, seg, n):
    return jax.ops.segment_sum(src, seg, n)
kernel_name = 'mk_lm_tower_d1_tok_ids512_r4_daef56'

def setup_inputs(seed: int=0):
    np.random.seed(seed)
    _w = jnp.asarray

    def _rec_inputs():
        import jax
        import jax.numpy as jnp
        _rk = jax.random.key(seed)
        x = jax.random.randint(jax.random.fold_in(_rk, 1), (16, 256), 0, 24, jnp.int32)
        fside_BS_position = jax.random.uniform(jax.random.fold_in(_rk, 21), (16, 256), jnp.float32, 0.0, 0.999927)
        return (x, fside_BS_position)
    x, fside_BS_position = _rec_inputs()

    def _L0_tok_setup():
        import jax, jax.numpy as jnp
        import numpy as np
        N_CHR = 24
        N_EMB = 128
        DIM = 128
        CHR_JUMP = 2.0
        TOPK = 10
        B, N = (4, 512)
        key = jax.random.key(seed)
        k1, k2, k3 = jax.random.split(key, 3)
        chromosome = jax.random.randint(k1, (B, N), 0, N_CHR, dtype=jnp.int32)
        position = jax.random.uniform(k2, (B, N), dtype=jnp.float32)
        embeddings = jax.random.normal(k3, (N_CHR * N_EMB, DIM), dtype=jnp.float32)
        centers = np.concatenate([np.linspace(0.0, 1.0, N_EMB) + n * CHR_JUMP for n in range(N_CHR)]).astype(np.float32)
        log_variances = jnp.full((N_CHR * N_EMB,), -5.0, dtype=jnp.float32)
        return {'chromosome': chromosome, 'position': position, 'embeddings': embeddings, 'centers': jnp.asarray(centers), 'log_variances': log_variances}
    _L0_tok_all = _L0_tok_setup()
    _L0_tok_in = {k: v for k, v in _L0_tok_all.items() if k in ('embeddings', 'centers', 'log_variances')}
    del _L0_tok_all

    def _L0_attn_setup():
        import jax, jax.numpy as jnp
        import numpy as np
        H, KVH, HD, DN, DR = (8, 2, 64, 32, 32)
        EPS = 1e-06
        ROPE_BASE = 500000.0

        def _rms(x, w):
            return w * (x * jax.lax.rsqrt(jnp.mean(x * x, axis=-1, keepdims=True) + EPS))

        def _rope_tables(T):
            inv_freq = 1.0 / ROPE_BASE ** (np.arange(0, DR, 2, dtype=np.float32) / DR)
            freqs = np.outer(np.arange(T, dtype=np.float32), inv_freq)
            emb = np.concatenate([freqs, freqs], axis=-1)
            return (jnp.asarray(np.cos(emb)), jnp.asarray(np.sin(emb)))

        def _apply_rope(x, cos, sin):
            x1, x2 = jnp.split(x, 2, axis=-1)
            rot = jnp.concatenate([-x2, x1], axis=-1)
            return x * cos[None, None] + rot * sin[None, None]
        key = jax.random.key(seed)
        ks = jax.random.split(key, 10)
        std = 0.02
        mup = (256.0 / 512.0) ** 0.5
        return {'x': jax.random.normal(ks[0], (4, 512, 128), jnp.float32), 'W_DQ': jax.random.normal(ks[1], (128, 64), jnp.float32) * std, 'W_UQ': jax.random.normal(ks[2], (64, H * DN), jnp.float32) * std, 'W_QR': jax.random.normal(ks[3], (64, H * DR), jnp.float32) * std, 'W_DKV': jax.random.normal(ks[4], (128, 128), jnp.float32) * std, 'W_UK': jax.random.normal(ks[5], (128, KVH * DN), jnp.float32) * std, 'W_UV': jax.random.normal(ks[6], (128, KVH * HD), jnp.float32) * std, 'W_KR': jax.random.normal(ks[7], (128, KVH * DR), jnp.float32) * std, 'W_VR': jax.random.normal(ks[8], (128, H * HD), jnp.float32) * std * mup, 'W_O': jax.random.normal(ks[9], (H * HD, 128), jnp.float32) * std * mup, 'q_ln_w': jnp.ones((64,), jnp.float32), 'kv_ln_w': jnp.ones((128,), jnp.float32), 'q_head_norm_w': jnp.ones((HD,), jnp.float32), 'k_head_norm_w': jnp.ones((HD,), jnp.float32)}
    _L0_attn_all = _L0_attn_setup()
    _L0_attn_in = {k: v for k, v in _L0_attn_all.items() if k in ('W_DQ', 'W_UQ', 'W_QR', 'W_DKV', 'W_UK', 'W_UV', 'W_KR', 'W_VR', 'W_O', 'q_ln_w', 'kv_ln_w', 'q_head_norm_w', 'k_head_norm_w')}
    del _L0_attn_all

    def _L0_ffn_setup():
        import jax, jax.numpy as jnp
        import numpy as np
        B, T, DIM = (2, 64, 128)
        E, H, K = (64, 256, 42)
        key = jax.random.key(seed)
        ks = jax.random.split(key, 7)
        s1 = 1.0 / np.sqrt(DIM).astype(np.float32)
        s2 = 1.0 / np.sqrt(H).astype(np.float32)
        return {'x': jax.random.normal(ks[0], (B, T, DIM), jnp.float32), 'w1': jax.random.uniform(ks[1], (E, DIM, H), jnp.float32, -s1, s1), 'b1': jax.random.uniform(ks[2], (E, H), jnp.float32, -s1, s1), 'w2': jax.random.uniform(ks[3], (E, H, DIM), jnp.float32, -s2, s2), 'b2': jax.random.uniform(ks[4], (E, DIM), jnp.float32, -s2, s2), 'router_w': jax.random.uniform(ks[5], (DIM, E), jnp.float32, -s1, s1), 'router_b': jax.random.uniform(ks[6], (E,), jnp.float32, -s1, s1)}
    _L0_ffn_all = _L0_ffn_setup()
    _L0_ffn_in = {k: v for k, v in _L0_ffn_all.items() if k in ('w1', 'b1', 'w2', 'b2', 'router_w', 'router_b')}
    del _L0_ffn_all
    return {'x': x, 'fside_BS_position': fside_BS_position, 'L0_tok_embeddings': _L0_tok_in['embeddings'], 'L0_tok_centers': _L0_tok_in['centers'], 'L0_tok_log_variances': _L0_tok_in['log_variances'], 'L0_attn_W_DQ': _L0_attn_in['W_DQ'], 'L0_attn_W_UQ': _L0_attn_in['W_UQ'], 'L0_attn_W_QR': _L0_attn_in['W_QR'], 'L0_attn_W_DKV': _L0_attn_in['W_DKV'], 'L0_attn_W_UK': _L0_attn_in['W_UK'], 'L0_attn_W_UV': _L0_attn_in['W_UV'], 'L0_attn_W_KR': _L0_attn_in['W_KR'], 'L0_attn_W_VR': _L0_attn_in['W_VR'], 'L0_attn_W_O': _L0_attn_in['W_O'], 'L0_attn_q_ln_w': _L0_attn_in['q_ln_w'], 'L0_attn_kv_ln_w': _L0_attn_in['kv_ln_w'], 'L0_attn_q_head_norm_w': _L0_attn_in['q_head_norm_w'], 'L0_attn_k_head_norm_w': _L0_attn_in['k_head_norm_w'], 'L0_ffn_w1': _L0_ffn_in['w1'], 'L0_ffn_b1': _L0_ffn_in['b1'], 'L0_ffn_w2': _L0_ffn_in['w2'], 'L0_ffn_b2': _L0_ffn_in['b2'], 'L0_ffn_router_w': _L0_ffn_in['router_w'], 'L0_ffn_router_b': _L0_ffn_in['router_b']}

def reference(x, fside_BS_position, L0_tok_embeddings, L0_tok_centers, L0_tok_log_variances, L0_attn_W_DQ, L0_attn_W_UQ, L0_attn_W_QR, L0_attn_W_DKV, L0_attn_W_UK, L0_attn_W_UV, L0_attn_W_KR, L0_attn_W_VR, L0_attn_W_O, L0_attn_q_ln_w, L0_attn_kv_ln_w, L0_attn_q_head_norm_w, L0_attn_k_head_norm_w, L0_ffn_w1, L0_ffn_b1, L0_ffn_w2, L0_ffn_b2, L0_ffn_router_w, L0_ffn_router_b):
    import jax
    import jax.numpy as jnp

    def _L0_tok_ref(chromosome, position, embeddings, centers, log_variances):
        import jax, jax.numpy as jnp
        import numpy as np
        N_CHR = 24
        N_EMB = 128
        DIM = 128
        CHR_JUMP = 2.0
        TOPK = 10
        B, N = (4, 512)
        pos = position + chromosome.astype(position.dtype) * CHR_JUMP
        variances = jnp.exp(log_variances)
        w = jnp.exp(-(pos[..., None] - centers) ** 2 / (2.0 * variances))
        w_top, idx = jax.lax.top_k(w, TOPK)
        w_top = w_top / jnp.sum(w_top, axis=-1, keepdims=True)
        emb = embeddings[idx]
        return jnp.einsum('bnk,bnkd->bnd', w_top, emb)

    def _L0_attn_ref(x, W_DQ, W_UQ, W_QR, W_DKV, W_UK, W_UV, W_KR, W_VR, W_O, q_ln_w, kv_ln_w, q_head_norm_w, k_head_norm_w):
        import jax, jax.numpy as jnp
        import numpy as np
        H, KVH, HD, DN, DR = (8, 2, 64, 32, 32)
        EPS = 1e-06
        ROPE_BASE = 500000.0

        def _rms(x, w):
            return w * (x * jax.lax.rsqrt(jnp.mean(x * x, axis=-1, keepdims=True) + EPS))

        def _rope_tables(T):
            inv_freq = 1.0 / ROPE_BASE ** (np.arange(0, DR, 2, dtype=np.float32) / DR)
            freqs = np.outer(np.arange(T, dtype=np.float32), inv_freq)
            emb = np.concatenate([freqs, freqs], axis=-1)
            return (jnp.asarray(np.cos(emb)), jnp.asarray(np.sin(emb)))

        def _apply_rope(x, cos, sin):
            x1, x2 = jnp.split(x, 2, axis=-1)
            rot = jnp.concatenate([-x2, x1], axis=-1)
            return x * cos[None, None] + rot * sin[None, None]
        B, T, D = x.shape
        cos, sin = _rope_tables(T)
        c_q = _rms(x @ W_DQ, q_ln_w)
        q_nope = (c_q @ W_UQ).reshape(B, T, H, DN).transpose(0, 2, 1, 3)
        q_rope = (c_q @ W_QR).reshape(B, T, H, DR).transpose(0, 2, 1, 3)
        c_kv = _rms(x @ W_DKV, kv_ln_w)
        k_nope = (c_kv @ W_UK).reshape(B, T, KVH, DN).transpose(0, 2, 1, 3)
        v = (c_kv @ W_UV).reshape(B, T, KVH, HD).transpose(0, 2, 1, 3)
        k_rope = (x @ W_KR).reshape(B, T, KVH, DR).transpose(0, 2, 1, 3)
        q_rope = _apply_rope(q_rope, cos, sin)
        k_rope = _apply_rope(k_rope, cos, sin)
        q = jnp.concatenate([q_nope, q_rope], axis=-1)
        k = jnp.concatenate([k_nope, k_rope], axis=-1)
        q = _rms(q, q_head_norm_w)
        k = _rms(k, k_head_norm_w)
        g = H // KVH
        k = jnp.repeat(k, g, axis=1)
        v = jnp.repeat(v, g, axis=1)
        scores = jnp.einsum('bhqd,bhkd->bhqk', q, k) * HD ** (-0.5)
        mask = jnp.tril(jnp.ones((T, T), dtype=bool))
        scores = jnp.where(mask, scores, -jnp.inf)
        attn_w = jax.nn.softmax(scores.astype(jnp.float32), axis=-1).astype(q.dtype)
        attn_out = jnp.einsum('bhqk,bhkd->bhqd', attn_w, v)
        v_res = (x @ W_VR).reshape(B, T, H, HD).transpose(0, 2, 1, 3)
        attn_out = attn_out + v_res
        out = attn_out.transpose(0, 2, 1, 3).reshape(B, T, H * HD)
        return out @ W_O

    def _L0_ffn_ref(x, w1, b1, w2, b2, router_w, router_b):
        import jax, jax.numpy as jnp
        import numpy as np
        B, T, DIM = (2, 64, 128)
        E, H, K = (64, 256, 42)
        Bb, Tt, C = x.shape
        N = Bb * Tt
        logits = x @ router_w + router_b
        probs = jax.nn.softmax(logits, axis=-1)
        top_w, top_idx = jax.lax.top_k(probs, K)
        top_w = jax.nn.softmax(top_w, axis=-1)
        xt = x.reshape(N, C)
        top_w = top_w.reshape(N, K)
        top_idx = top_idx.reshape(N, K)
        comb = jnp.zeros((N, E), x.dtype).at[jnp.arange(N)[:, None], top_idx].set(top_w)
        h = jax.nn.gelu(jnp.einsum('td,edh->teh', xt, w1) + b1, approximate=False)
        y = jnp.einsum('teh,ehd->ted', h, w2) + b2
        out = jnp.einsum('ted,te->td', y, comb)
        return out.reshape(Bb, Tt, C)
    h = _L0_tok_ref(x, fside_BS_position, L0_tok_embeddings, L0_tok_centers, L0_tok_log_variances)
    h = h + _L0_attn_ref(_layernorm(h, axis=-1), L0_attn_W_DQ, L0_attn_W_UQ, L0_attn_W_QR, L0_attn_W_DKV, L0_attn_W_UK, L0_attn_W_UV, L0_attn_W_KR, L0_attn_W_VR, L0_attn_W_O, L0_attn_q_ln_w, L0_attn_kv_ln_w, L0_attn_q_head_norm_w, L0_attn_k_head_norm_w)
    h = h + _L0_ffn_ref(_layernorm(h, axis=-1), L0_ffn_w1, L0_ffn_b1, L0_ffn_w2, L0_ffn_b2, L0_ffn_router_w, L0_ffn_router_b)
    return h

_drawn_inputs = setup_inputs


def setup_inputs(seed=0):
    import zlib

    import numpy as np

    out = dict(_drawn_inputs(seed))
    spreads = {'L0_tok_log_variances': (-5.0, 0.2),
     'L0_attn_q_ln_w': (1.0, 0.6),
     'L0_attn_kv_ln_w': (1.0, 0.6),
     'L0_attn_q_head_norm_w': (1.0, 0.6),
     'L0_attn_k_head_norm_w': (1.0, 0.6)}
    factors = {'L0_ffn_b1': 6.282, 'L0_ffn_b2': 3.278, 'L0_ffn_router_b': 3.076}
    for name, (base, spread) in spreads.items():
        noise = np.random.default_rng([zlib.crc32(name.encode()), seed]).standard_normal(out[name].shape)
        drawn = base * np.exp(spread * noise) if base else spread * noise
        out[name] = jnp.asarray(drawn.astype(out[name].dtype))
    for name, factor in factors.items():
        out[name] = (out[name] * factor).astype(out[name].dtype)
    return out
```

```python
from contextlib import ExitStack

import numpy as np

import concourse.bass as bass
from concourse import mybir

F32 = mybir.dt.float32
F32R = mybir.dt.float32r
I32 = mybir.dt.int32
ACT = mybir.ActivationFunctionType
ALU = mybir.AluOpType
AX = mybir.AxisListType

P = 128
BATCH, SEQ, DIM = 16, 256, 128
TOKENS = BATCH * SEQ
TILES = TOKENS // P
CENTERS = 3072
CHUNKS = CENTERS // P
TOPK = 10
CHR_JUMP = 2.0
HEADS, KV, HD, DN, DR = 8, 2, 64, 32, 32
GROUP = HEADS // KV
LQ, LKV = 64, 128
EXPERTS, HIDDEN, ACTIVE = 64, 256, 42
DROPPED = EXPERTS - ACTIVE
RMS_EPS = 1e-6
LN_EPS = 1e-5
MARK = -3.0e38
MASKED = -1.0e30
GT = 512
SWEEP_TOKENS = 2 * GT
SWEEPS = TOKENS // SWEEP_TOKENS
WRING = 4
C_Q, C_KV, C_KR, C_COLS = 0, LQ, LQ + LKV, LQ + LKV + KV * DR + DIM
C_RES = C_COLS - DIM
NH = HEADS + KV


def after(eng, sem, value):
    if not isinstance(value, int) or value > 0:
        eng.wait_ge(sem, value)


def hold(eng, sem, value):
    eng.wait_ge(sem, value)
    if not isinstance(value, int):
        eng.nop(nofuse=True)


def chained(eng, sem, done):
    count = [done]

    def link(instruction):
        instruction.then_inc(sem, 1)
        count[0] = count[0] + 1
        hold(eng, sem, count[0])

    return link


def in_pairs(eng, step, n, body=2):
    for t in range(body):
        step(t, t)
    with eng.Fori(1, n // body) as i:
        for b in range(body):
            step(i * body + b, b)


def lm_tower(nc, tok, pos, emb, centers, logvar, w_dq, w_uq, w_qr, w_dkv, w_uk, w_uv, w_kr, w_vr, w_o,
             q_ln, kv_ln, q_hn, k_hn, w1, b1, w2, b2_rev, router_rev, router_b_rev, rope_cos, rope_sin, out):
    with ExitStack() as whole:
        def keep(name, shape, dt=F32):
            return whole.enter_context(nc.sbuf_tensor(name, shape, dt))

        h = keep("h", [P, TILES, DIM])
        ident = keep("ident", [P, P])
        pair_ident = keep("pair_ident", [P, EXPERTS])
        ones_row = keep("ones_row", [1, P])
        causal = keep("causal", [P, P])
        npos = keep("npos", [P, TILES])
        w_latent = keep("w_latent", [P, LQ + LKV + KV * DR + DIM])
        w_q = keep("w_q", [LQ, GROUP, KV, HD])
        w_kv = keep("w_kv", [P, KV * DN + KV * HD])
        w_out = keep("w_out", [P, GROUP, DIM])
        k_scale = keep("k_scale", [P, 1])
        cos2 = keep("cos2", [P, SEQ // P, DR])
        sin2 = keep("sin2", [P, SEQ // P, DR])
        mv = keep("mv", [P, TILES, 2])
        rstd = keep("rstd", [P, TILES])

        setup(nc, tok, pos, w_dq, w_uq, w_qr, w_dkv, w_uk, w_uv, w_kr, w_vr, w_o, q_ln, kv_ln, q_hn, k_hn,
              rope_cos, rope_sin, ident, pair_ident, ones_row, causal, npos, w_latent, w_q, w_kv, w_out, k_scale,
              cos2, sin2)
        embed(nc, emb, centers, logvar, h, ident, npos, mv)
        with ExitStack() as mid:
            qk = mid.enter_context(nc.sbuf_tensor("qk", [P, TILES, HEADS + KV, HD], F32))
            v_all = mid.enter_context(nc.sbuf_tensor("v_all", [P, TILES, KV * HD], F32))
            ss = mid.enter_context(nc.sbuf_tensor("ss", [P, TILES, 2], F32))
            hs = mid.enter_context(nc.sbuf_tensor("hs", [P, TILES, HEADS + KV], F32))
            with ExitStack() as first:
                c_raw = first.enter_context(nc.sbuf_tensor("c_raw", [P, TILES, C_COLS], F32))
                project(nc, h, ident, w_latent, mv, rstd, c_raw, ss)
                heads(nc, ident, w_q, w_kv, cos2, sin2, c_raw, ss, qk, v_all, hs)
            attend(nc, h, ident, causal, w_out, k_scale, qk, v_all, hs, mv)
        with ExitStack() as last:
            x_hi = last.enter_context(nc.sbuf_tensor("x_hi", [P, TOKENS], F32R))
            x_lo = last.enter_context(nc.sbuf_tensor("x_lo", [P, TOKENS], F32R))
            comb_t = last.enter_context(nc.sbuf_tensor("comb_t", [P, TOKENS], F32R))
            route(nc, h, ident, ones_row, router_rev, router_b_rev, mv, rstd, x_hi, x_lo, comb_t)
            experts(nc, h, ident, pair_ident, x_hi, x_lo, comb_t, w1, b1, w2, b2_rev, out)


def setup(nc, tok, pos, w_dq, w_uq, w_qr, w_dkv, w_uk, w_uv, w_kr, w_vr, w_o, q_ln, kv_ln, q_hn, k_hn,
          rope_cos, rope_sin, ident, pair_ident, ones_row, causal, npos, w_latent, w_q, w_kv, w_out, k_scale,
          cos2, sin2):
    with ExitStack() as ctx:
        def sb(name, shape, dt=F32):
            return ctx.enter_context(nc.sbuf_tensor(name, shape, dt))

        def sem(name):
            return ctx.enter_context(nc.semaphore(name))

        tok_rows = sb("tok_rows", [TILES, P], I32)
        pos_rows = sb("pos_rows", [TILES, P])
        tok_f = sb("tok_f", [TILES, P])
        abs_rows = sb("abs_rows", [TILES, P])
        wq_in = sb("wq_in", [LQ, GROUP, KV, HD])
        wkv_in = sb("wkv_in", [P, KV * DN + KV * HD])
        vr_in = sb("vr_in", [P, GROUP, KV, HD])
        vr_t = sb("vr_t", [P, GROUP, DIM])
        qln = sb("qln", [LQ, 1])
        kvln = sb("kvln", [P, 1])
        hn = sb("hn", [P, 2])
        ps_pos = ctx.enter_context(nc.psum_tensor("ps_pos", [P, 512], F32))
        ps_vr = ctx.enter_context(nc.psum_tensor("ps_vr", [P, GROUP, P], F32))
        ps_m = ctx.enter_context(nc.psum_tensor("ps_m", [P, 512], F32))
        loads = sem("loads")
        rows_in = sem("rows_in")
        out_in = sem("out_in")
        zeroed = sem("zeroed")
        masks = sem("masks")
        posf = sem("posf")
        abs_ready = sem("abs_ready")
        pos_t = sem("pos_t")
        vr_turned = sem("vr_turned")
        vr_copied = sem("vr_copied")
        m_ready = sem("m_ready")
        block = ctx.enter_context(nc.Block(name="setup"))

        @block.sync
        def _(sp):
            sp.dma_start(tok_rows[:], tok.rearrange("b (t p) -> (b t) p", p=P)).then_inc(rows_in, 16)
            sp.dma_start(pos_rows[:], pos.rearrange("b (t p) -> (b t) p", p=P)).then_inc(rows_in, 16)
            for g in range(KV):
                sp.dma_start(vr_in[:, :, g, :], w_vr[:, g * GROUP * HD:(g + 1) * GROUP * HD]
                             .rearrange("k (j d) -> k j d", d=HD)).then_inc(out_in, 16)
            for g in range(KV):
                sp.dma_start(w_out[g * HD:(g + 1) * HD, :, :],
                             w_o[g * GROUP * HD:(g + 1) * GROUP * HD, :].rearrange("(j d) n -> d j n", d=HD)
                             ).then_inc(out_in, 16)
            sp.dma_start(w_latent[:, 0:LQ], w_dq).then_inc(loads, 16)
            sp.dma_start(w_latent[:, LQ:LQ + LKV], w_dkv).then_inc(loads, 16)
            sp.dma_start(w_latent[:, LQ + LKV:LQ + LKV + KV * DR], w_kr).then_inc(loads, 16)
            for g in range(KV):
                cols = slice(g * GROUP * DN, (g + 1) * GROUP * DN)
                sp.dma_start(wq_in[:, :, g, 0:DN], w_uq[:, cols].rearrange("k (j n) -> k j n", n=DN)
                             ).then_inc(loads, 16)
                sp.dma_start(wq_in[:, :, g, DN:HD], w_qr[:, cols].rearrange("k (j n) -> k j n", n=DR)
                             ).then_inc(loads, 16)
            sp.dma_start(wkv_in[:, 0:KV * DN], w_uk).then_inc(loads, 16)
            sp.dma_start(wkv_in[:, KV * DN:], w_uv).then_inc(loads, 16)
            sp.dma_start(qln[:], q_ln.rearrange("(p a) -> p a", a=1)).then_inc(loads, 16)
            sp.dma_start(kvln[:], kv_ln.rearrange("(p a) -> p a", a=1)).then_inc(loads, 16)
            for g in range(KV):
                sp.dma_start(hn[g * HD:(g + 1) * HD, 0:1], q_hn.rearrange("(p a) -> p a", a=1)).then_inc(loads, 16)
                sp.dma_start(hn[g * HD:(g + 1) * HD, 1:2], k_hn.rearrange("(p a) -> p a", a=1)).then_inc(loads, 16)
            half = DR // 2
            for c in range(2):
                sp.dma_start(cos2[:, :, c * half:(c + 1) * half],
                             rope_cos.rearrange("(t p) d -> p t d", p=P)).then_inc(loads, 16)
                sp.dma_start(sin2[:, :, c * half:(c + 1) * half],
                             rope_sin[c].rearrange("(t p) d -> p t d", p=P)).then_inc(loads, 16)

        n_loads = 3 + 2 * KV + 2 + 2 + 2 * KV + 4

        @block.gpsimd
        def _(pool):
            pool.memset(ident[:], 0.0).then_inc(zeroed, 1)
            pool.memset(pair_ident[:], 0.0).then_inc(zeroed, 1)
            pool.memset(causal[:], 0.0).then_inc(zeroed, 1)
            pool.memset(ones_row[:], 1.0).then_inc(zeroed, 1)
            pool.wait_ge(zeroed, 4)
            pool.affine_select(out=ident[:], in_=ident[:], compare_op=ALU.not_equal, fill=1.0, base=0,
                               pattern=[[-1, P]], channel_multiplier=1).then_inc(masks, 1)
            pool.affine_select(out=causal[:], in_=causal[:], compare_op=ALU.is_ge, fill=MASKED, base=0,
                               pattern=[[-1, P]], channel_multiplier=1).then_inc(masks, 1)
            pool.affine_select(out=pair_ident[:], in_=pair_ident[:], compare_op=ALU.not_equal, fill=1.0, base=0,
                               pattern=[[-1, EXPERTS]], channel_multiplier=1).then_inc(masks, 1)
            pool.wait_ge(masks, 3)
            pool.affine_select(out=pair_ident[:], in_=pair_ident[:], compare_op=ALU.not_equal, fill=1.0,
                               base=-EXPERTS, pattern=[[-1, EXPERTS]], channel_multiplier=1).then_inc(masks, 1)

        @block.vector
        def _(dve):
            dve.wait_ge(rows_in, 32)
            dve.tensor_copy(tok_f[:], tok_rows[:]).then_inc(posf, 1)
            dve.wait_ge(posf, 1)
            dve.scalar_tensor_tensor(out=abs_rows[:], in0=tok_f[:], scalar=CHR_JUMP, in1=pos_rows[:],
                                     op0=ALU.mult, op1=ALU.add).then_inc(abs_ready, 1)
            dve.wait_ge(pos_t, 1)
            dve.tensor_scalar(npos[:], ps_pos[:, 0:TILES], -1.0, None, ALU.mult)
            dve.wait_ge(loads, 16 * n_loads)
            dve.tensor_scalar(w_q[:], wq_in[:], qln[:, 0:1], None, ALU.mult)
            dve.tensor_scalar(w_kv[:], wkv_in[:], kvln[:, 0:1], None, ALU.mult)
            dve.scalar_tensor_tensor(out=k_scale[:], in0=hn[:, 0:1], scalar=float(HD) ** -0.5, in1=hn[:, 1:2],
                                     op0=ALU.mult, op1=ALU.mult)
            dve.wait_ge(vr_turned, 1)
            dve.tensor_copy(vr_t[:], ps_vr[:]).then_inc(vr_copied, 1)
            dve.wait_ge(m_ready, 1)
            dve.tensor_copy(w_latent[:, LQ + LKV + KV * DR:], ps_m[:, 0:DIM])

        @block.tensor
        def _(pe):
            pe.wait_ge(masks, 4)
            pe.wait_ge(abs_ready, 1)
            pe.transpose(ps_pos[:, 0:TILES], abs_rows[:], ident[0:TILES, 0:TILES]).then_inc(pos_t, 1)
            pe.wait_ge(out_in, 16 * 2 * KV)
            for j in range(GROUP):
                last = pe.transpose(ps_vr[:, j, :], vr_in[:, j].rearrange("k g d -> k (g d)"), ident[:])
            last.then_inc(vr_turned, 1)
            pe.wait_ge(vr_copied, 1)
            for j in range(GROUP):
                last = pe.matmul(ps_m[:, 0:DIM], vr_t[:, j, :], w_out[:, j, :], start=(j == 0), stop=(j == GROUP - 1))
            last.then_inc(m_ready, 1)


def embed(nc, emb, centers, logvar, h, ident, npos, mv):
    PARTS = 2
    PC = CHUNKS // PARTS
    with ExitStack() as ctx:
        def sb(name, shape, dt=F32):
            return ctx.enter_context(nc.sbuf_tensor(name, shape, dt))

        def sem(name):
            return ctx.enter_context(nc.semaphore(name))

        cent = sb("cent", [P, CENTERS])
        neg_prec = sb("neg_prec", [P, CENTERS])
        table = sb("table", [P, CHUNKS, DIM])
        z = sb("z", [P, 2, CENTERS])
        marked = sb("marked", [P, CENTERS])
        gauss = sb("gauss", [P, 2, CENTERS])
        gauss_t = sb("gauss_t", [P, PARTS, PC, P])
        top_a = sb("top_a", [P, 8])
        top_b = sb("top_b", [P, 8])
        wsum = sb("wsum", [P, 2])
        rsum = sb("rsum", [P, 2])
        stats = sb("stats", [P, 6])
        mvt = sb("mvt", [P, 2])
        ps_t = [ctx.enter_context(nc.psum_tensor(f"ps_t{k}", [P, PC, P], F32)) for k in range(PARTS)]
        ps_h = ctx.enter_context(nc.psum_tensor("ps_h", [P, 2, 512], F32))
        loads = sem("e_loads")
        table_in = sem("table_in")
        prec_exp = sem("prec_exp")
        prec = sem("prec")
        squared = sem("squared")
        z_ready = sem("z_ready")
        z_read = sem("z_read")
        gauss_ready = sem("gauss_ready")
        sel_step = sem("sel_step")
        fin_step = sem("fin_step")
        chosen = sem("chosen")
        turned = sem("turned")
        copied = sem("copied")
        product = sem("product")
        tile_done = sem("tile_done")
        block = ctx.enter_context(nc.Block(name="embed"))

        @block.sync
        def _(sp):
            sp.dma_start(cent[:], centers.rearrange("(a n) -> a n", a=1).broadcast_to([P, CENTERS])).then_inc(loads, 16)
            sp.dma_start(neg_prec[:], logvar.rearrange("(a n) -> a n", a=1).broadcast_to([P, CENTERS])
                         ).then_inc(loads, 16)
            sp.dma_start(table[:], emb.rearrange("(c p) d -> p c d", p=P)).then_inc(table_in, 16)

        @block.scalar
        def _(act):
            act.wait_ge(loads, 32)
            act.activation(neg_prec[:], neg_prec[:], ACT.Exp, scale=-1.0).then_inc(prec_exp, 1)

            def copy_out(t):
                for k in range(PARTS):
                    act.wait_ge(turned, t * PARTS + (k + 1))
                    after(act, product, t)
                    act.activation(gauss_t[:, k], ps_t[k][:], ACT.Copy).then_inc(copied, 1)

            def step(t, b):
                after(act, z_read, t - 1)
                act.activation(z[:, b % 2, :], cent[:], ACT.Square, bias=npos[:, bass.ds(t, 1)]).then_inc(squared, 1)
                if not isinstance(t, int) or t >= 2:
                    copy_out(t - 2)
                act.wait_ge(z_ready, t + 1)
                act.activation(gauss[:, b % 2, :], z[:, b % 2, :], ACT.Exp).then_inc(gauss_ready, 1)

            in_pairs(act, step, TILES)
            copy_out(TILES - 2)
            copy_out(TILES - 1)

        @block.gpsimd
        def _(pool):
            pool.wait_ge(prec, 1)

            def step(t, b):
                pool.wait_ge(squared, t + 1)
                pool.tensor_tensor(z[:, b % 2, :], z[:, b % 2, :], neg_prec[:], ALU.mult).then_inc(z_ready, 1)

            in_pairs(pool, step, TILES)

        @block.vector
        def _(dve):
            dve.wait_ge(prec_exp, 1)
            dve.tensor_scalar(neg_prec[:], neg_prec[:], -0.5, None, ALU.mult).then_inc(prec, 1)

            def select(t, b):
                link = chained(dve, sel_step, t * 5)
                hold(dve, gauss_ready, t + 1)
                link(dve.max(top_a[:], z[:, b, :]))
                dve.match_replace(marked[:], top_a[:], z[:, b, :], MARK).then_inc(z_read, 1)
                hold(dve, z_read, t + 1)
                link(dve.max(top_b[:], marked[:]))
                link(dve.memset(top_b[:, TOPK - 8:8], MARK))
                link(dve.match_replace(marked[:], top_b[:], marked[:], MARK))
                dve.scalar_tensor_tensor(out=gauss[:, b, :], in0=marked[:], scalar=MARK, in1=gauss[:, b, :],
                                         op0=ALU.is_le, op1=ALU.mult, accum_out=wsum[:, b:b + 1]
                                         ).then_inc(chosen, 1)
                dve.wait_ge(chosen, t + 1)
                link(dve.reciprocal(rsum[:, b:b + 1], wsum[:, b:b + 1]))

            def finish(t, b):
                link = chained(dve, fin_step, t * 3)
                dve.wait_ge(product, t + 1)
                link(dve.tensor_scalar(h[:, t, :], ps_h[:, b, 0:DIM], rsum[:, b:b + 1], None, ALU.mult))
                link(dve.bn_stats(stats[:], h[:, t, :]))
                link(dve.bn_aggr(mvt[:], stats[:]))
                dve.tensor_copy(mv[:, t, :], mvt[:]).then_inc(tile_done, 1)

            def step(t, b):
                select(t, b)
                if not isinstance(t, int) or t >= 1:
                    finish(t - 1, 1 - b)

            in_pairs(dve, step, TILES)
            finish(TILES - 1, (TILES - 1) % 2)

        @block.tensor
        def _(pe):
            pe.wait_ge(table_in, 16)

            def step(t, b):
                pe.wait_ge(chosen, t + 1)
                for k in range(PARTS):
                    after(pe, copied, (t - 1) * PARTS + (k + 1))
                    for c in range(PC):
                        at = (k * PC + c) * P
                        last = pe.transpose(ps_t[k][:, c, :], gauss[:, b, at:at + P], ident[:])
                    last.then_inc(turned, 1)
                after(pe, tile_done, t - 1)
                for k in range(PARTS):
                    pe.wait_ge(copied, t * PARTS + (k + 1))
                    for c in range(PC):
                        last = pe.matmul(ps_h[:, b, 0:DIM], gauss_t[:, k, c, :], table[:, k * PC + c, :],
                                         start=(k == 0 and c == 0), stop=(k == PARTS - 1 and c == PC - 1))
                last.then_inc(product, 1)

            in_pairs(pe, step, TILES)


def project(nc, h, ident, w_latent, mv, rstd, c_raw, ss):
    with ExitStack() as ctx:
        def sb(name, shape, dt=F32):
            return ctx.enter_context(nc.sbuf_tensor(name, shape, dt))

        def sem(name):
            return ctx.enter_context(nc.semaphore(name))

        shifted = sb("p_shifted", [P, TILES])
        root = sb("p_root", [P, TILES])
        xn = sb("xn", [P, 2, DIM])
        x_t = sb("x_t", [P, 2, P])
        junk = sb("junk", [P, LQ + LKV])
        ps_x = ctx.enter_context(nc.psum_tensor("ps_x", [P, 2, 512], F32))
        ps_c = ctx.enter_context(nc.psum_tensor("ps_c", [P, 2, 512], F32))
        var_eps = sem("var_eps")
        rooted = sem("p_rooted")
        rstd_ready = sem("rstd_ready")
        normed = sem("normed")
        turned = sem("p_turned")
        x_copied = sem("x_copied")
        projected = sem("projected")
        c_copied = sem("c_copied")
        squared = sem("p_squared")
        block = ctx.enter_context(nc.Block(name="project"))

        @block.scalar
        def _(act):
            act.wait_ge(var_eps, 1)
            act.activation(root[:], shifted[:], ACT.Sqrt).then_inc(rooted, 1)

            def latents(t, b):
                act.wait_ge(projected, t + 1)
                act.activation(c_raw[:, t, :], ps_c[:, b, 0:C_COLS], ACT.Copy).then_inc(c_copied, 1)
                act.wait_ge(c_copied, t + 1)
                after(act, squared, t)
                act.activation(junk[:, C_Q:C_KV], c_raw[:, t, C_Q:C_KV], ACT.Square, accum_out=ss[:, t, 0:1])
                act.activation(junk[:, C_KV:C_KR], c_raw[:, t, C_KV:C_KR], ACT.Square, accum_out=ss[:, t, 1:2]
                               ).then_inc(squared, 1)

            def step(t, b):
                act.wait_ge(turned, t + 1)
                act.activation(x_t[:, b, :], ps_x[:, b, 0:P], ACT.Copy).then_inc(x_copied, 1)
                if not isinstance(t, int) or t >= 1:
                    latents(t - 1, 1 - b)

            in_pairs(act, step, TILES)
            latents(TILES - 1, 1)

        @block.vector
        def _(dve):
            dve.tensor_scalar(shifted[:], mv[:, :, 1], LN_EPS, None, ALU.add).then_inc(var_eps, 1)
            dve.wait_ge(rooted, 1)
            dve.reciprocal(rstd[:], root[:]).then_inc(rstd_ready, 1)
            dve.wait_ge(rstd_ready, 1)

            def add_residual(t):
                dve.wait_ge(c_copied, t + 1)
                dve.tensor_tensor(h[:, t, :], h[:, t, :], c_raw[:, t, C_RES:C_COLS], ALU.add)

            def step(t, b):
                after(dve, turned, t - 1)
                dve.tensor_scalar(xn[:, b, :], h[:, t, :], mv[:, t, 0:1], rstd[:, bass.ds(t, 1)], ALU.subtract,
                                  ALU.mult).then_inc(normed, 1)
                if not isinstance(t, int) or t >= 2:
                    add_residual(t - 2)

            in_pairs(dve, step, TILES)
            add_residual(TILES - 2)
            add_residual(TILES - 1)

        @block.tensor
        def _(pe):
            def product(t, b):
                pe.wait_ge(x_copied, t + 1)
                after(pe, c_copied, t - 1)
                pe.matmul(ps_c[:, b, 0:C_COLS], x_t[:, b, :], w_latent[:], start=True, stop=True
                          ).then_inc(projected, 1)

            def step(t, b):
                pe.wait_ge(normed, t + 1)
                after(pe, x_copied, t - 1)
                pe.transpose(ps_x[:, b, 0:P], xn[:, b, :], ident[:]).then_inc(turned, 1)
                if not isinstance(t, int) or t >= 1:
                    product(t - 1, 1 - b)

            in_pairs(pe, step, TILES)
            product(TILES - 1, 1)


def heads(nc, ident, w_q, w_kv, cos2, sin2, c_raw, ss, qk, v_all, hs):
    with ExitStack() as ctx:
        def sb(name, shape, dt=F32):
            return ctx.enter_context(nc.sbuf_tensor(name, shape, dt))

        def sem(name):
            return ctx.enter_context(nc.semaphore(name))

        mean_sq = sb("mean_sq", [P, 2, TILES])
        root = sb("h_root", [P, 2, TILES])
        rms = sb("rms", [P, 2, TILES])
        cn = sb("cn", [P, 2, LQ + LKV])
        c_t = sb("c_t", [P, 2, 2 * P])
        turned_cos = sb("turned_cos", [P, NH, DR])
        turned_sin = sb("turned_sin", [P, NH, DR])
        sq = sb("sq", [P, NH, HD])
        ps_ct = ctx.enter_context(nc.psum_tensor("ps_ct", [P, 2, 512], F32))
        ps_q = ctx.enter_context(nc.psum_tensor("ps_q", [P, 2, 512], F32))
        ps_kv = ctx.enter_context(nc.psum_tensor("ps_kv", [P, 2, 512], F32))
        mean_ready = sem("mean_ready")
        rooted = sem("h_rooted")
        rms_ready = sem("rms_ready")
        normed = sem("c_normed")
        turned = sem("c_turned")
        c_copied = sem("ct_copied")
        projected = sem("qkv_projected")
        out_copied = sem("qkv_copied")
        rope_step = sem("rope_step")
        block = ctx.enter_context(nc.Block(name="heads"))
        half = DR // 2

        @block.scalar
        def _(act):
            act.wait_ge(mean_ready, 2)
            act.activation(root[:], mean_sq[:], ACT.Sqrt).then_inc(rooted, 1)

            def copy_out(t, b):
                act.wait_ge(projected, t + 1)
                act.activation(qk[:, t, 0:HEADS, :], ps_q[:, b, :].rearrange("p (n d) -> p n d", d=HD), ACT.Copy)
                act.activation(qk[:, t, HEADS:NH, 0:DN], ps_kv[:, b, 0:KV * DN].rearrange("p (n d) -> p n d", d=DN),
                               ACT.Copy)
                act.activation(v_all[:, t, :], ps_kv[:, b, KV * DN:KV * (DN + HD)], ACT.Copy)
                act.activation(qk[:, t, HEADS:NH, DN:HD], c_raw[:, t, C_KR:C_RES].rearrange("p (n d) -> p n d", d=DR),
                               ACT.Copy).then_inc(out_copied, 1)

            def step(t, b):
                act.wait_ge(turned, t + 1)
                act.activation(c_t[0:LQ, b, 0:P], ps_ct[0:LQ, b, 0:P], ACT.Copy)
                act.activation(c_t[:, b, P:2 * P], ps_ct[:, b, P:2 * P], ACT.Copy).then_inc(c_copied, 1)
                if not isinstance(t, int) or t >= 1:
                    copy_out(t - 1, 1 - b)

            in_pairs(act, step, TILES)
            copy_out(TILES - 1, 1)

        @block.vector
        def _(dve):
            for k, n in enumerate((LQ, LKV)):
                dve.tensor_scalar(mean_sq[:, k, :], ss[:, :, k], 1.0 / n, RMS_EPS, ALU.mult, ALU.add
                                  ).then_inc(mean_ready, 1)
            dve.wait_ge(rooted, 1)
            dve.reciprocal(rms[:], root[:]).then_inc(rms_ready, 1)
            dve.wait_ge(rms_ready, 1)

            def rope(t, b):
                dve.wait_ge(out_copied, t + 1)
                link = chained(dve, rope_step, t * 3)
                x = qk[:, t, :, DN:HD]
                cos = cos2[:, b:b + 1, :].broadcast_to([P, NH, DR])
                sin = sin2[:, b:b + 1, :].broadcast_to([P, NH, DR])
                dve.tensor_tensor(turned_cos[:], x, cos, ALU.mult)
                dve.tensor_tensor(turned_sin[:, :, 0:half], qk[:, t, :, DN + half:HD], sin[:, :, 0:half], ALU.mult)
                link(dve.tensor_tensor(turned_sin[:, :, half:DR], qk[:, t, :, DN:DN + half], sin[:, :, half:DR],
                                       ALU.mult))
                link(dve.tensor_tensor(x, turned_cos[:], turned_sin[:], ALU.add))
                link(dve.tensor_tensor(sq[:], qk[:, t], qk[:, t], ALU.mult))
                dve.tensor_reduce(hs[:, t, :], sq[:], AX.X, ALU.add)

            def step(t, b):
                after(dve, turned, t - 1)
                dve.tensor_scalar(cn[:, b, 0:LQ], c_raw[:, t, C_Q:C_KV], rms[:, 0, bass.ds(t, 1)], None, ALU.mult)
                dve.tensor_scalar(cn[:, b, LQ:], c_raw[:, t, C_KV:C_KR], rms[:, 1, bass.ds(t, 1)], None, ALU.mult
                                  ).then_inc(normed, 1)
                if not isinstance(t, int) or t >= 2:
                    rope(t - 2, b)

            in_pairs(dve, step, TILES)
            rope(TILES - 2, 0)
            rope(TILES - 1, 1)

        @block.tensor
        def _(pe):
            def product(t, b):
                pe.wait_ge(c_copied, t + 1)
                after(pe, out_copied, t - 1)
                pe.matmul(ps_q[:, b, :], c_t[0:LQ, b, 0:P], w_q[:].rearrange("k j g d -> k (j g d)"), start=True,
                          stop=True)
                pe.matmul(ps_kv[:, b, 0:KV * (DN + HD)], c_t[:, b, P:2 * P], w_kv[:], start=True, stop=True
                          ).then_inc(projected, 1)

            def step(t, b):
                pe.wait_ge(normed, t + 1)
                if not isinstance(t, int) or t >= 2:
                    hold(pe, c_copied, t - 1)
                pe.transpose(ps_ct[0:LQ, b, 0:P], cn[:, b, 0:LQ], ident[:])
                pe.transpose(ps_ct[:, b, P:2 * P], cn[:, b, LQ:], ident[:]).then_inc(turned, 1)
                if not isinstance(t, int) or t >= 1:
                    product(t - 1, 1 - b)

            in_pairs(pe, step, TILES)
            product(TILES - 1, 1)


def attend(nc, h, ident, causal, w_out, k_scale, qk, v_all, hs, mv):
    UNITS = 2 * BATCH
    with ExitStack() as ctx:
        def sb(name, shape, dt=F32):
            return ctx.enter_context(nc.sbuf_tensor(name, shape, dt))

        def sem(name):
            return ctx.enter_context(nc.semaphore(name))

        mean_sq = sb("a_mean_sq", [P, TILES, NH])
        rms = sb("a_rms", [P, TILES, NH])
        qkn = sb("qkn", [P, 2, NH, HD])
        v_s = sb("v_s", [P, 2, 2, KV * HD])
        q_t = sb("q_t", [P, GROUP, P])
        k_t = sb("k_t", [P, 2, SEQ])
        sm = sb("sm", [P, 4, HEADS, SEQ])
        neg_max = sb("neg_max", [P, 4, HEADS])
        rowsum = sb("rowsum", [P, 4, HEADS])
        rinv = sb("rinv", [P, 4, HEADS])
        p_t = sb("p_t", [P, 2, HEADS, P])
        o_t = sb("o_t", [P, GROUP, P])
        stats = sb("a_stats", [P, 6])
        mvt = sb("a_mvt", [P, 2])
        ps_s = ctx.enter_context(nc.psum_tensor("ps_s", [P, HEADS, SEQ], F32))
        ps_p = ctx.enter_context(nc.psum_tensor("ps_p", [P, HEADS, P], F32))
        ps_qy = ctx.enter_context(nc.psum_tensor("ps_qy", [P, GROUP, P], F32))
        ps_ko = ctx.enter_context(nc.psum_tensor("ps_ko", [P, GROUP, P], F32))
        mean_ready = sem("a_mean_ready")
        rooted = sem("a_rooted")
        rms_ready = sem("a_rms_ready")
        qk_normed = sem("qk_normed")
        qk_turned = sem("qk_turned")
        qk_copied = sem("qk_copied")
        scored = sem("scored")
        masked = sem("masked")
        max_ready = sem("max_ready")
        exp_done = sem("exp_done")
        rinv_ready = sem("rinv_ready")
        weights_ready = sem("weights_ready")
        p_turned = sem("p_turned")
        p_copied = sem("p_copied")
        mixed = sem("mixed")
        o_copied = sem("o_copied")
        y_ready = sem("y_ready")
        y_added = sem("y_added")
        mv_step = sem("mv_step")
        block = ctx.enter_context(nc.Block(name="attend"))

        def blocks_before(u, r):
            whole = u // 2 if isinstance(u, int) else (u - r % 2) // 2
            return whole * 3 + r % 2

        @block.scalar
        def _(act):
            act.wait_ge(mean_ready, 1)
            act.activation(mean_sq[:], mean_sq[:], ACT.Sqrt).then_inc(rooted, 1)

            def copy_qk(u, r):
                q, s = r % 2, r // 2 % 2
                act.wait_ge(qk_turned, u + 1)
                act.activation(q_t[:], ps_qy[:], ACT.Copy)
                act.activation(k_t[:, s, q * P:(q + 1) * P], ps_ko[:, 0, :], ACT.Copy, scale=k_scale[:, 0:1]
                               ).then_inc(qk_copied, 1)

            def copy_o(u):
                act.wait_ge(mixed, u + 1)
                act.activation(o_t[:], ps_ko[:], ACT.Copy).then_inc(o_copied, 1)

            def exps(u, r):
                keys = (r % 2 + 1) * P
                act.wait_ge(max_ready, u + 1)
                for n in range(HEADS):
                    last = act.activation(sm[:, r, n, 0:keys], sm[:, r, n, 0:keys], ACT.Exp,
                                          bias=neg_max[:, r, n:n + 1], accum_out=rowsum[:, r, n:n + 1])
                last.then_inc(exp_done, 1)

            def step(u, r):
                copy_qk(u, r)
                if not isinstance(u, int) or u >= 2:
                    copy_o(u - 2)
                exps(u, r)

            in_pairs(act, step, UNITS, 4)
            copy_o(UNITS - 2)
            copy_o(UNITS - 1)

        @block.gpsimd
        def _(pool):
            pool.wait_ge(rms_ready, 1)

            def norm_qk(u, r):
                q, s = r % 2, r // 2 % 2
                after(pool, qk_turned, u - 1)
                pool.tensor_tensor(qkn[:, q], qk[:, u], rms[:, bass.ds(u, 1), :].rearrange("p a n -> p (a n)")
                                   .unsqueeze(2).broadcast_to([P, NH, HD]), ALU.mult)
                after(pool, mixed, u - 2 - q)
                pool.tensor_copy(v_s[:, s, q, :], v_all[:, u, :]).then_inc(qk_normed, 1)

            def norm_weights(u, r):
                keys = (r % 2 + 1) * P
                pool.wait_ge(rinv_ready, u + 1)
                pool.tensor_tensor(sm[:, r, :, 0:keys], sm[:, r, :, 0:keys],
                                   rinv[:, r, :].unsqueeze(2).broadcast_to([P, HEADS, keys]), ALU.mult
                                   ).then_inc(weights_ready, 1)

            def step(u, r):
                norm_qk(u, r)
                if not isinstance(u, int) or u >= 1:
                    norm_weights(u - 1, (r - 1) % 4)

            in_pairs(pool, step, UNITS, 4)
            norm_weights(UNITS - 1, 3)

        @block.vector
        def _(dve):
            dve.tensor_scalar(mean_sq[:], hs[:], 1.0 / HD, RMS_EPS, ALU.mult, ALU.add).then_inc(mean_ready, 1)
            dve.wait_ge(rooted, 1)
            dve.reciprocal(rms[:], mean_sq[:]).then_inc(rms_ready, 1)

            def copy_p(u, r, block_count, k):
                dve.wait_ge(p_turned, block_count + 1)
                dve.tensor_copy(p_t[:, k], ps_p[:]).then_inc(p_copied, 1)

            def invert(u, r):
                dve.wait_ge(exp_done, u + 1)
                dve.reciprocal(rinv[:, r, :], rowsum[:, r, :]).then_inc(rinv_ready, 1)

            def mask(u, r):
                q = r % 2
                dve.wait_ge(scored, u + 1)
                if q:
                    dve.tensor_copy(sm[:, r, :, 0:P], ps_s[:, :, 0:P])
                dve.tensor_tensor(sm[:, r, :, q * P:(q + 1) * P], ps_s[:, :, q * P:(q + 1) * P],
                                  causal[:].unsqueeze(1).broadcast_to([P, HEADS, P]), ALU.add).then_inc(masked, 1)
                dve.wait_ge(masked, u + 1)
                dve.tensor_reduce(neg_max[:, r, :], sm[:, r, :, 0:(q + 1) * P], AX.X, ALU.max, negate=True
                                  ).then_inc(max_ready, 1)

            def add_y(u):
                link = chained(dve, mv_step, u * 2)
                dve.wait_ge(y_ready, u + 1)
                dve.tensor_tensor(h[:, u, :], h[:, u, :], ps_qy[:, 0, :], ALU.add).then_inc(y_added, 1)
                hold(dve, y_added, u + 1)
                link(dve.bn_stats(stats[:], h[:, u, :]))
                link(dve.bn_aggr(mvt[:], stats[:]))
                dve.tensor_copy(mv[:, u, :], mvt[:])

            def step(u, r):
                old = not isinstance(u, int) or u >= 2
                if old:
                    first = blocks_before(u - 2, r)
                    copy_p(u - 2, r, first, 0)
                if not isinstance(u, int) or u >= 1:
                    invert(u - 1, (r - 1) % 4)
                if old and r % 2:
                    copy_p(u - 2, r, first + 1, 1)
                mask(u, r)
                if old:
                    add_y(u - 2)

            in_pairs(dve, step, UNITS, 4)
            copy_p(UNITS - 2, 2, blocks_before(UNITS - 2, 0), 0)
            invert(UNITS - 1, 3)
            add_y(UNITS - 2)
            for k in range(2):
                copy_p(UNITS - 1, 3, blocks_before(UNITS - 1, 1) + k, k)
            add_y(UNITS - 1)

        @block.tensor
        def _(pe):
            def turn_p(u, r, count, k):
                if k == 0:
                    pe.wait_ge(weights_ready, u + 1)
                after(pe, p_copied, count)
                for n in range(HEADS):
                    last = pe.transpose(ps_p[:, n, :], sm[:, r, n, k * P:(k + 1) * P], ident[:])
                last.then_inc(p_turned, 1)

            def turn_qk(u, r):
                q = r % 2
                pe.wait_ge(qk_normed, u + 1)
                after(pe, y_added, u - 2)
                after(pe, o_copied, u - 2)
                for j in range(GROUP):
                    pe.transpose(ps_qy[:, j, :], qkn[:, q, KV * j:KV * (j + 1), :].rearrange("p n d -> p (n d)"),
                                 ident[:])
                pe.transpose(ps_ko[:, 0, :], qkn[:, q, HEADS:NH, :].rearrange("p n d -> p (n d)"), ident[:]
                             ).then_inc(qk_turned, 1)

            def mix(u, r, count):
                q, s = r % 2, r // 2 % 2
                pe.wait_ge(p_copied, count + q + 1)
                for g in range(KV):
                    for k in range(q + 1):
                        last = pe.matmul(ps_ko[g * HD:(g + 1) * HD, :, :], v_s[:, s, k, g * HD:(g + 1) * HD],
                                         p_t[:, k, g * GROUP:(g + 1) * GROUP, :], start=(k == 0), stop=(k == q))
                last.then_inc(mixed, 1)

            def score(u, r):
                q, s = r % 2, r // 2 % 2
                pe.wait_ge(qk_copied, u + 1)
                after(pe, masked, u)
                for j in range(GROUP):
                    for g in range(KV):
                        at = slice(g * HD, (g + 1) * HD)
                        last = pe.matmul(ps_s[:, g * GROUP + j, 0:(q + 1) * P], q_t[at, j, :],
                                         k_t[at, s, 0:(q + 1) * P], start=True, stop=True)
                last.then_inc(scored, 1)

            def project_out(u):
                pe.wait_ge(o_copied, u + 1)
                for j in range(GROUP):
                    last = pe.matmul(ps_qy[:, 0, :], o_t[:, j, :], w_out[:, j, :], start=(j == 0),
                                     stop=(j == GROUP - 1))
                last.then_inc(y_ready, 1)

            def step(u, r):
                old = not isinstance(u, int) or u >= 2
                if old:
                    first = blocks_before(u - 2, r)
                    turn_p(u - 2, (r - 2) % 4, first, 0)
                turn_qk(u, r)
                if old and r % 2:
                    turn_p(u - 2, (r - 2) % 4, first + 1, 1)
                if old:
                    pe.wait_ge(qk_copied, u + 1)
                    mix(u - 2, (r - 2) % 4, first)
                score(u, r)
                if old:
                    project_out(u - 2)

            in_pairs(pe, step, UNITS, 4)
            for u in (UNITS - 2, UNITS - 1):
                for k in range(u % 2 + 1):
                    turn_p(u, u % 4, blocks_before(u, u) + k, k)
                after(pe, o_copied, u)
                mix(u, u % 4, blocks_before(u, u))
                after(pe, y_added, u)
                project_out(u)


def route(nc, h, ident, ones_row, router_rev, router_b_rev, mv, rstd, x_hi, x_lo, comb_t):
    with ExitStack() as ctx:
        def sb(name, shape, dt=F32):
            return ctx.enter_context(nc.sbuf_tensor(name, shape, dt))

        def sem(name):
            return ctx.enter_context(nc.semaphore(name))

        rw = sb("rw", [P, EXPERTS])
        rb = sb("rb", [1, EXPERTS])
        shifted = sb("r_shifted", [P, TILES])
        root = sb("r_root", [P, TILES])
        xn = sb("r_xn", [P, 2, DIM])
        x_s = sb("x_s", [P, 2, P])
        neg_max = sb("r_neg_max", [P, 2, 1])
        e1 = sb("e1", [P, 2, EXPERTS])
        s1 = sb("s1", [P, 2, 1])
        r1 = sb("r1", [P, 2, 1])
        neg_r1 = sb("neg_r1", [P, 2, 1])
        neg_p = sb("neg_p", [P, 2, EXPERTS])
        left = sb("left", [P, EXPERTS])
        low = sb("low", [P, 8])
        e2 = sb("e2", [P, 2, EXPERTS])
        top = sb("top", [P, EXPERTS])
        s2 = sb("s2", [P, 1])
        r2 = sb("r2", [P, 1])
        c_hi = sb("c_hi", [P, EXPERTS], F32R)
        c_pair = sb("c_pair", [P, 2, 2 * EXPERTS])
        ps_x = ctx.enter_context(nc.psum_tensor("r_ps_x", [P, 2, 512], F32))
        ps_l = ctx.enter_context(nc.psum_tensor("ps_l", [P, 2, 512], F32))
        ps_c = ctx.enter_context(nc.psum_tensor("r_ps_c", [P, 2, 512], F32))
        loads = sem("r_loads")
        var_eps = sem("r_var_eps")
        rooted = sem("r_rooted")
        rstd_ready = sem("r_rstd_ready")
        normed = sem("r_normed")
        turned = sem("r_turned")
        x_copied = sem("r_x_copied")
        hi_ready = sem("hi_ready")
        x_used = sem("x_used")
        logits = sem("logits")
        max_ready = sem("r_max_ready")
        exp_one = sem("exp_one")
        probs = sem("probs")
        exp_two = sem("exp_two")
        top_step = sem("top_step")
        pair_ready = sem("pair_ready")
        pair_turned = sem("pair_turned")
        pair_copied = sem("pair_copied")
        block = ctx.enter_context(nc.Block(name="route"))

        def cols(t):
            return bass.ds(t * P, P)

        @block.sync
        def _(sp):
            sp.dma_start(rw[:], router_rev).then_inc(loads, 16)
            sp.dma_start(rb[:], router_b_rev.rearrange("(a n) -> a n", a=1)).then_inc(loads, 16)

        @block.scalar
        def _(act):
            act.wait_ge(var_eps, 1)
            act.activation(root[:], shifted[:], ACT.Sqrt).then_inc(rooted, 1)

            def copy_x(t, b):
                act.wait_ge(turned, t + 1)
                after(act, x_used, t - 1)
                act.activation(x_s[:, b, :], ps_x[:, b, 0:P], ACT.Copy).then_inc(x_copied, 1)
                act.activation(x_hi[:, cols(t)], ps_x[:, b, 0:P], ACT.Copy).then_inc(hi_ready, 1)

            def first_exp(t, b):
                act.wait_ge(max_ready, t + 1)
                act.activation(e1[:, b, :], ps_l[:, b, 0:EXPERTS], ACT.Exp, bias=neg_max[:, b, :],
                               accum_out=s1[:, b, :]).then_inc(exp_one, 1)

            def second_exp(t, b):
                act.wait_ge(probs, t + 1)
                act.activation(e2[:, b, :], neg_p[:, b, :], ACT.Exp, bias=neg_r1[:, b, :], scale=-1.0
                               ).then_inc(exp_two, 1)

            def copy_pair(t, b):
                act.wait_ge(pair_turned, t + 1)
                act.activation(comb_t[:, cols(t)], ps_c[:, b, 0:P], ACT.Copy).then_inc(pair_copied, 1)

            def step(t, b):
                copy_x(t, b)
                if not isinstance(t, int) or t >= 2:
                    copy_pair(t - 2, b)
                first_exp(t, b)
                second_exp(t, b)

            in_pairs(act, step, TILES)
            copy_pair(TILES - 2, 0)
            copy_pair(TILES - 1, 1)

        @block.gpsimd
        def _(pool):
            def step(t, b):
                pool.wait_ge(hi_ready, t + 1)
                pool.tensor_tensor(x_lo[:, cols(t)], x_s[:, b, :], x_hi[:, cols(t)].bitcast(F32), ALU.subtract
                                   ).then_inc(x_used, 1)

            in_pairs(pool, step, TILES)

        @block.vector
        def _(dve):
            dve.tensor_scalar(shifted[:], mv[:, :, 1], LN_EPS, None, ALU.add).then_inc(var_eps, 1)
            dve.wait_ge(rooted, 1)
            dve.reciprocal(rstd[:], root[:]).then_inc(rstd_ready, 1)
            dve.wait_ge(rstd_ready, 1)

            def norm(t, b):
                after(dve, turned, t - 1)
                dve.tensor_scalar(xn[:, b, :], h[:, t, :], mv[:, t, 0:1], rstd[:, bass.ds(t, 1)], ALU.subtract,
                                  ALU.mult).then_inc(normed, 1)

            def probabilities(t, b):
                dve.wait_ge(logits, t + 1)
                dve.tensor_reduce(neg_max[:, b, :], ps_l[:, b, 0:EXPERTS], AX.X, ALU.max, negate=True
                                  ).then_inc(max_ready, 1)
                dve.wait_ge(exp_one, t + 1)

            def choose(t, b):
                link = chained(dve, top_step, t * STEPS)
                link(dve.reciprocal(r1[:, b, :], s1[:, b, :]))
                dve.tensor_scalar(neg_r1[:, b, :], r1[:, b, :], -1.0, None, ALU.mult)
                dve.tensor_scalar(neg_p[:, b, :], e1[:, b, :], r1[:, b, :], -1.0, ALU.mult, ALU.mult
                                  ).then_inc(probs, 1)
                hold(dve, probs, t + 1)
                src = neg_p[:, b, :]
                for taken in range(0, DROPPED, 8):
                    link(dve.max(low[:], src))
                    if DROPPED - taken < 8:
                        link(dve.memset(low[:, DROPPED - taken:8], MARK))
                    link(dve.match_replace(left[:], low[:], src, MARK))
                    src = left[:]
                dve.wait_ge(exp_two, t + 1)
                link(dve.scalar_tensor_tensor(out=top[:], in0=left[:], scalar=MARK, in1=e2[:, b, :], op0=ALU.is_gt,
                                              op1=ALU.mult, accum_out=s2[:]))
                link(dve.reciprocal(r2[:], s2[:]))
                link(dve.tensor_scalar(c_hi[:], top[:], r2[:, 0:1], None, ALU.mult))
                after(dve, pair_turned, t - 1)
                dve.tensor_copy(c_pair[:, b, 0:EXPERTS], c_hi[:].bitcast(F32))
                dve.scalar_tensor_tensor(out=c_pair[:, b, EXPERTS:], in0=top[:], scalar=r2[:, 0:1],
                                         in1=c_hi[:].bitcast(F32), op0=ALU.mult, op1=ALU.subtract
                                         ).then_inc(pair_ready, 1)

            STEPS = 1 + 2 * 3 + 1 + 3
            norm(0, 0)

            def step(t, b):
                probabilities(t, b)
                choose(t, b)

            def both(t, b):
                if not isinstance(t, int) or t >= 1:
                    step(t - 1, 1 - b)

            norm(1, 1)
            step(0, 0)
            with dve.Fori(1, TILES // 2) as i:
                for b in range(2):
                    norm(i * 2 + b, b)
                    step(i * 2 + b - 1, 1 - b)
            step(TILES - 1, 1)

        @block.tensor
        def _(pe):
            pe.wait_ge(loads, 32)

            def logit(t, b):
                pe.wait_ge(x_copied, t + 1)
                after(pe, exp_one, t - 1)
                pe.matmul(ps_l[:, b, 0:EXPERTS], x_s[:, b, :], rw[:], start=True, stop=False)
                pe.matmul(ps_l[:, b, 0:EXPERTS], ones_row[:], rb[:], start=False, stop=True).then_inc(logits, 1)

            def turn_pair(t, b):
                pe.wait_ge(pair_ready, t + 1)
                after(pe, pair_copied, t - 1)
                pe.transpose(ps_c[:, b, 0:P], c_pair[:, b, :], ident[:]).then_inc(pair_turned, 1)

            def step(t, r):
                b = r % 2
                pe.wait_ge(normed, t + 1)
                after(pe, hi_ready, t - 1)
                pe.transpose(ps_x[:, b, 0:P], xn[:, b, :], ident[:]).then_inc(turned, 1)
                logit(t, b)
                if not isinstance(t, int) or t >= 2:
                    turn_pair(t - 2, b)

            in_pairs(pe, step, TILES, 4)
            turn_pair(TILES - 2, 0)
            turn_pair(TILES - 1, 1)


def experts(nc, h, ident, pair_ident, x_hi, x_lo, comb_t, w1, b1, w2, b2_rev, out):
    LAG = 4
    STEPS = 2 * EXPERTS
    RING = LAG
    BODY = 2 * WRING
    ROUNDS = EXPERTS // WRING
    HC = HIDDEN // P
    with ExitStack() as ctx:
        def sb(name, shape, dt=F32):
            return ctx.enter_context(nc.sbuf_tensor(name, shape, dt))

        def sem(name):
            return ctx.enter_context(nc.semaphore(name))

        w_raw = sb("w_raw", [P, WRING, 2, HIDDEN])
        w_hi = sb("w_hi", [P, WRING, 2, HIDDEN], F32R)
        w_lo = sb("w_lo", [P, WRING, 2, HIDDEN], F32R)
        sel = sb("sel", [P, WRING, P], F32R)
        b1_rows = sb("b1_rows", [EXPERTS, HIDDEN])
        b1_t = sb("b1_t", [P, HC, EXPERTS])
        b2_raw = sb("b2_raw", [P, DIM])
        b2_hi = sb("b2_hi", [P, DIM], F32R)
        b2_lo = sb("b2_lo", [P, DIM], F32R)
        act_out = sb("act_out", [P, 2, HC, GT])
        scaled = sb("scaled", [P, RING, HC, GT])
        s_hi = sb("s_hi", [P, RING, HC, GT], F32R)
        s_lo = sb("s_lo", [P, RING, HC, GT], F32R)
        y_t = sb("y_t", [P, 2, GT])
        y = sb("y", [P, 2 * GT // P, DIM])
        ps_h = ctx.enter_context(nc.psum_tensor("f_ps_h", [P, 2, HC, GT], F32))
        ps_c = ctx.enter_context(nc.psum_tensor("f_ps_c", [P, 2, GT], F32))
        ps_y = ctx.enter_context(nc.psum_tensor("f_ps_y", [P, 2, GT], F32))
        b_loads = sem("b_loads")
        w_in = [sem(f"w_in{k}") for k in range(WRING)]
        b1_turned = sem("b1_turned")
        b2_step = sem("b2_step")
        w_split = sem("w_split")
        hidden = sem("hidden")
        gelu_done = sem("gelu_done")
        scaled_ready = sem("scaled_ready")
        hi_ready = sem("s_hi_ready")
        lo_ready = sem("s_lo_ready")
        summed = sem("summed")
        hi_copied = sem("hi_copied")
        y_copied = sem("y_copied")
        y_turned = sem("y_turned")
        y_added = sem("f_y_added")
        stored = sem("stored")
        block = ctx.enter_context(nc.Block(name="experts"))
        y_tokens = out.rearrange("b s d -> (b s) d").rearrange("(w t p) d -> w p t d", w=SWEEPS, p=P)

        @block.sync
        def _(sp):
            sp.dma_start(b1_rows[:], b1).then_inc(stored, 16)
            sp.dma_start(b2_raw[0:EXPERTS, :], b2_rev).then_inc(b_loads, 16)
            sp.dma_start(b2_raw[EXPERTS:P, :], b2_rev).then_inc(b_loads, 16)

            def load(in_sweep, r):
                sp.dma_start(w_raw[:, r, 0, :], w1[in_sweep]).then_inc(w_in[r], 16)
                sp.dma_start(w_raw[:, r, 1, :].rearrange("p (c n) -> p c n", c=HC),
                             w2[in_sweep].rearrange("(c p) n -> p c n", p=P)).then_inc(w_in[r], 16)

            def store(w):
                sp.wait_ge(y_added, w + 2)
                sp.dma_start(y_tokens[w], y[:]).then_inc(stored, 16)

            for r in range(WRING):
                load(r, r)
            with sp.Fori(1, ROUNDS) as i:
                for r in range(WRING):
                    sp.wait_ge(w_split, i * WRING + (r - WRING + 1))
                    load(i * WRING + r, r)
            with sp.Fori(1, SWEEPS) as w:
                with sp.Fori(0, ROUNDS) as i:
                    for r in range(WRING):
                        sp.wait_ge(w_split, w * EXPERTS + i * WRING + (r - WRING + 1))
                        load(i * WRING + r, r)
                store(w - 1)
            store(SWEEPS - 1)
            sp.wait_ge(stored, 16 * (SWEEPS + 1))

        @block.gpsimd
        def _(pool):
            def split(e, in_sweep, r, loaded, reuse):
                pool.wait_ge(w_in[r], loaded)
                if reuse:
                    hold(pool, summed, e * 2 - (2 * WRING - 2))
                pool.tensor_copy(w_hi[:, r], w_raw[:, r]).then_inc(hi_copied, 1)
                pool.tensor_copy(sel[:, r, :], pair_ident[:, bass.ds(EXPERTS - 1 - in_sweep, 1)].broadcast_to([P, P]))
                pool.wait_ge(hi_copied, e + 1)
                pool.tensor_tensor(w_lo[:, r], w_raw[:, r], w_hi[:, r].bitcast(F32), ALU.subtract
                                   ).then_inc(w_split, 1)

            for r in range(WRING):
                split(r, r, r, 32, False)
            with pool.Fori(1, ROUNDS) as i:
                for r in range(WRING):
                    split(i * WRING + r, i * WRING + r, r, i * 32 + 32, True)
            with pool.Fori(1, SWEEPS) as w:
                with pool.Fori(0, ROUNDS) as i:
                    for r in range(WRING):
                        split(w * EXPERTS + i * WRING + r, i * WRING + r, r, w * (32 * ROUNDS) + i * 32 + 32, True)

        @block.scalar
        def _(act):
            def gelu(S, e, r):
                hold(act, hidden, S + 1)
                for c in range(HC):
                    last = act.activation(act_out[:, r % 2, c, :], ps_h[:, r % 2, c, :], ACT.Gelu,
                                          bias=b1_t[:, c, bass.ds(e, 1)])
                last.then_inc(gelu_done, 1)

            def high(S, r, reuse):
                act.wait_ge(scaled_ready, S + 1)
                if reuse:
                    act.wait_ge(summed, S - (LAG - 1))
                act.activation(s_hi[:, r % RING], scaled[:, r % RING], ACT.Copy).then_inc(hi_ready, 1)

            act.wait_ge(y_added, 1)
            with act.Fori(0, SWEEPS) as w:
                start = w * STEPS
                for r in range(BODY):
                    gelu(start + r, r // 2, r)
                    if r:
                        high(start + (r - 1), r - 1, r - 1 >= LAG)
                with act.Fori(1, STEPS // BODY) as i:
                    for r in range(BODY):
                        gelu(start + i * BODY + r, i * (BODY // 2) + r // 2, r)
                        high(start + i * BODY + (r - 1), (r - 1) % BODY, True)
                high(start + (STEPS - 1), BODY - 1, True)
                act.wait_ge(summed, start + STEPS)
                for g in range(2):
                    act.activation(y_t[:, g, :], ps_y[:, g, :], ACT.Copy).then_inc(y_copied, 1)

        @block.vector
        def _(dve):
            dve.wait_ge(b_loads, 32)
            dve.tensor_copy(b2_hi[:], b2_raw[:]).then_inc(b2_step, 1)
            dve.wait_ge(b2_step, 1)
            dve.tensor_tensor(b2_lo[:], b2_raw[:], b2_hi[:].bitcast(F32), ALU.subtract).then_inc(b2_step, 1)
            dve.wait_ge(b1_turned, 1)
            dve.tensor_copy(b1_t[:], ps_h[:, 0, 0, 0:HC * EXPERTS].rearrange("p (c e) -> p c e", c=HC)
                            ).then_inc(y_added, 1)

            def scale(S, r, reuse):
                b = r % 2
                if reuse:
                    dve.wait_ge(lo_ready, S - (RING - 1))
                dve.wait_ge(gelu_done, S + 1)
                dve.tensor_tensor(scaled[:, r % RING], act_out[:, b],
                                  ps_c[:, b, :].unsqueeze(1).broadcast_to([P, HC, GT]), ALU.mult
                                  ).then_inc(scaled_ready, 1)

            def low(S, r):
                dve.wait_ge(hi_ready, S + 1)
                dve.tensor_tensor(s_lo[:, r % RING], scaled[:, r % RING], s_hi[:, r % RING].bitcast(F32), ALU.subtract
                                  ).then_inc(lo_ready, 1)

            with dve.Fori(0, SWEEPS) as w:
                start = w * STEPS
                for r in range(BODY):
                    scale(start + r, r, r >= RING)
                    if r:
                        low(start + (r - 1), r - 1)
                with dve.Fori(1, STEPS // BODY) as i:
                    for r in range(BODY):
                        scale(start + i * BODY + r, r, True)
                        low(start + i * BODY + (r - 1), (r - 1) % BODY)
                low(start + (STEPS - 1), BODY - 1)
                dve.wait_ge(stored, w * 16 + 16)
                for g in range(2):
                    dve.wait_ge(y_turned, w * 2 + (g + 1))
                    last = dve.tensor_tensor(y[:, g * GT // P:(g + 1) * GT // P, :],
                                             h[:, bass.ds(w * (2 * GT // P) + g * (GT // P), GT // P), :],
                                             ps_c[:, g, :].rearrange("p (t d) -> p t d", d=DIM), ALU.add)
                last.then_inc(y_added, 1)

        @block.tensor
        def _(pe):
            pe.wait_ge(stored, 16)
            for c in range(HC):
                last = pe.transpose(ps_h[:, 0, 0, c * EXPERTS:(c + 1) * EXPERTS], b1_rows[:, c * P:(c + 1) * P],
                                    ident[0:EXPERTS, 0:EXPERTS])
            last.then_inc(b1_turned, 1)
            pe.wait_ge(b2_step, 2)

            def tokens(w, g):
                return bass.ds(w * SWEEP_TOKENS + g * GT, GT)

            def first(S, e, w, r, reuse):
                g, k = r % 2, r // 2
                if g == 0:
                    pe.wait_ge(w_split, e + 1)
                if reuse:
                    pe.wait_ge(scaled_ready, S - 1)
                pe.matmul(ps_c[:, g, :], sel[:, k, :], comb_t[:, tokens(w, g)], start=True, stop=True)
                for c in range(HC):
                    at = slice(c * P, (c + 1) * P)
                    pe.matmul(ps_h[:, g, c, :], w_hi[:, k, 0, at], x_hi[:, tokens(w, g)], start=True, stop=False)
                    pe.matmul(ps_h[:, g, c, :], w_hi[:, k, 0, at], x_lo[:, tokens(w, g)], start=False, stop=False)
                    last = pe.matmul(ps_h[:, g, c, :], w_lo[:, k, 0, at], x_hi[:, tokens(w, g)], start=False,
                                     stop=True)
                last.then_inc(hidden, 1)

            def second(S, r, last_step):
                g, k, slot = r % 2, r // 2, r % RING
                pe.wait_ge(lo_ready, S + 1)
                for c in range(HC):
                    at = slice(c * P, (c + 1) * P)
                    pe.matmul(ps_y[:, g, :], w_hi[:, k, 1, at], s_hi[:, slot, c, :], start=False, stop=False)
                    pe.matmul(ps_y[:, g, :], w_hi[:, k, 1, at], s_lo[:, slot, c, :], start=False, stop=False)
                    last = pe.matmul(ps_y[:, g, :], w_lo[:, k, 1, at], s_hi[:, slot, c, :], start=False,
                                     stop=last_step and c == HC - 1)
                last.then_inc(summed, 1)

            with pe.Fori(0, SWEEPS) as w:
                start = w * STEPS
                pe.wait_ge(y_added, w + 1)
                for g in range(2):
                    pe.matmul(ps_y[:, g, :], b2_hi[:], comb_t[:, tokens(w, g)], start=True, stop=False)
                    pe.matmul(ps_y[:, g, :], b2_lo[:], comb_t[:, tokens(w, g)], start=False, stop=False)
                for r in range(BODY):
                    if r >= LAG:
                        second(start + (r - LAG), r - LAG, False)
                    first(start + r, w * EXPERTS + r // 2, w, r, r >= 2)
                with pe.Fori(1, STEPS // BODY) as i:
                    for r in range(BODY):
                        at = start + i * BODY
                        second(at + (r - LAG), (r - LAG) % BODY, False)
                        first(at + r, w * EXPERTS + i * (BODY // 2) + r // 2, w, r, True)
                for r in range(LAG):
                    second(start + (STEPS - LAG + r), BODY - LAG + r, r >= LAG - 2)
                for g in range(2):
                    pe.wait_ge(y_copied, w * 2 + (g + 1))
                    for t in range(GT // P):
                        last = pe.transpose(ps_c[:, g, t * P:(t + 1) * P], y_t[:, g, t * P:(t + 1) * P], ident[:])
                    last.then_inc(y_turned, 1)


_OUTS = [((BATCH, SEQ, DIM), "float32")]


def kernel(**inputs):
    import concourse.bacc as _bacc
    from concourse.bass_utils import run_bass_kernel_spmd as _run

    half = DR // 2
    inv_freq = 1.0 / 500000.0 ** (np.arange(0, DR, 2, dtype=np.float32) / DR)
    freqs = np.outer(np.arange(SEQ, dtype=np.float32), inv_freq)
    cos, sin = np.cos(freqs).astype(np.float32), np.sin(freqs).astype(np.float32)
    laid = {
        "tok": inputs["x"],
        "pos": inputs["fside_BS_position"],
        "emb": inputs["L0_tok_embeddings"],
        "centers": inputs["L0_tok_centers"],
        "logvar": inputs["L0_tok_log_variances"],
    }
    for name in ("W_DQ", "W_UQ", "W_QR", "W_DKV", "W_UK", "W_UV", "W_KR", "W_VR", "W_O", "q_ln_w", "kv_ln_w",
                 "q_head_norm_w", "k_head_norm_w"):
        laid[name.lower()] = inputs["L0_attn_" + name]
    laid["w1"] = inputs["L0_ffn_w1"]
    laid["b1"] = inputs["L0_ffn_b1"]
    laid["w2"] = inputs["L0_ffn_w2"]
    laid["b2_rev"] = np.asarray(inputs["L0_ffn_b2"])[::-1]
    laid["router_rev"] = np.asarray(inputs["L0_ffn_router_w"])[:, ::-1]
    laid["router_b_rev"] = np.asarray(inputs["L0_ffn_router_b"])[::-1]
    laid["rope_cos"] = cos
    laid["rope_sin"] = np.stack([-sin, sin])

    nc = _bacc.Bacc("TRN2", target_bir_lowering=False, num_devices=1)
    arrays, args = {}, []
    for name, value in laid.items():
        a = np.ascontiguousarray(value)
        arrays[f"in_{name}"] = a
        args.append(nc.dram_tensor(f"in_{name}", a.shape, mybir.dt.from_np(a.dtype), kind="ExternalInput").ap())
    out = nc.dram_tensor("out_0", _OUTS[0][0], F32, kind="ExternalOutput").ap()
    lm_tower(nc, *args, out)
    r = _run(nc, [arrays], core_ids=[0])
    return r.results[0]["out_0"]
```

```python
from contextlib import ExitStack

import numpy as np

import concourse.bass as bass
from concourse import mybir

F32 = mybir.dt.float32
F32R = mybir.dt.float32r
I32 = mybir.dt.int32
ACT = mybir.ActivationFunctionType
ALU = mybir.AluOpType
AX = mybir.AxisListType

P = 128
BATCH, SEQ, DIM = 16, 256, 128
TOKENS = BATCH * SEQ
TILES = TOKENS // P
CENTERS = 3072
CHUNKS = CENTERS // P
TOPK = 10
CHR_JUMP = 2.0
HEADS, KV, HD, DN, DR = 8, 2, 64, 32, 32
GROUP = HEADS // KV
LQ, LKV = 64, 128
EXPERTS, HIDDEN, ACTIVE = 64, 256, 42
DROPPED = EXPERTS - ACTIVE
RMS_EPS = 1e-6
LN_EPS = 1e-5
MARK = -3.0e38
MASKED = -1.0e30
GT = 512
GROUPS = 4
SWEEP_TOKENS = GROUPS * GT
SWEEPS = TOKENS // SWEEP_TOKENS
WRING = 4
PARTS = 2
CLASSES = 4
LOADS_OF_ATTENTION = 7 + 6 * KV + 4
C_Q, C_KV, C_KR, C_COLS = 0, LQ, LQ + LKV, LQ + LKV + KV * DR + DIM
C_RES = C_COLS - DIM
NH = HEADS + KV


def after(eng, sem, value):
    if not isinstance(value, int) or value > 0:
        eng.wait_ge(sem, value)


def hold(eng, sem, value):
    eng.wait_ge(sem, value)
    if not isinstance(value, int):
        eng.nop(nofuse=True)


def chained(eng, sem, done):
    count = [done]

    def link(instruction):
        instruction.then_inc(sem, 1)
        count[0] = count[0] + 1
        hold(eng, sem, count[0])

    return link


def in_pairs(eng, step, n, body=2):
    for t in range(body):
        step(t, t)
    with eng.Fori(1, n // body) as i:
        for b in range(body):
            step(i * body + b, b)


def in_range(t, n):
    return not isinstance(t, int) or 0 <= t < n


def lm_tower(nc, tok, pos, emb, centers, logvar, w_dq, w_uq, w_qr, w_dkv, w_uk, w_uv, w_kr, w_vr, w_o,
             q_ln, kv_ln, q_hn, k_hn, w1, b1, w2, b2_rev, router_rev, router_b_rev, rope_cos, rope_sin, out):
    comb_rows = nc.dram_tensor("comb_rows", [EXPERTS, TOKENS], F32, kind="Internal").ap()
    with ExitStack() as whole:
        def keep(name, shape, dt=F32):
            return whole.enter_context(nc.sbuf_tensor(name, shape, dt))

        h = keep("h", [P, TILES, DIM])
        ident = keep("ident", [P, P])
        ones_row = keep("ones_row", [1, P])
        mv = keep("mv", [P, TILES, 2])
        rstd = keep("rstd", [P, TILES])
        with ExitStack() as attention:
            def part(name, shape, dt=F32):
                return attention.enter_context(nc.sbuf_tensor(name, shape, dt))

            w = {
                "latent": part("w_latent", [P, C_COLS]),
                "q": part("w_q", [LQ, GROUP, KV, HD]),
                "kv": part("w_kv", [P, KV * DN + KV * HD]),
                "out": part("w_out", [P, GROUP, DIM]),
                "q_in": part("wq_in", [LQ, GROUP, KV, HD]),
                "kv_in": part("wkv_in", [P, KV * DN + KV * HD]),
                "vr_in": part("vr_in", [P, GROUP, KV, HD]),
                "qln": part("qln", [LQ, 1]),
                "kvln": part("kvln", [P, 1]),
                "hn": part("hn", [P, 2]),
                "k_scale": part("k_scale", [P, 1]),
                "cos": part("cos2", [P, SEQ // P, DR]),
                "sin": part("sin2", [P, SEQ // P, DR]),
            }
            causal = part("causal", [P, P])
            w_loaded = attention.enter_context(nc.semaphore("w_loaded"))
            with ExitStack() as tower:
                flag = tower.enter_context(nc.sbuf_tensor("flag", [1, 1], I32))
                e = embed_buffers(nc, tower)
                npos = tower.enter_context(nc.sbuf_tensor("npos", [P, TILES], F32))

                def load_weights(sp):
                    return load_attention(sp, w, w_loaded, w_dq, w_uq, w_qr, w_dkv, w_uk, w_uv, w_kr, w_vr, w_o,
                                          q_ln, kv_ln, q_hn, k_hn, rope_cos, rope_sin)

                setup(nc, tok, pos, centers, logvar, emb, e, ident, ones_row, causal, npos)
                embed(nc, e, h, ident, npos, mv, flag, False, load_weights)
                embed(nc, e, h, ident, npos, mv, flag, True, None)
            with ExitStack() as mid:
                qk = mid.enter_context(nc.sbuf_tensor("qk", [P, TILES, NH, HD], F32))
                v_all = mid.enter_context(nc.sbuf_tensor("v_all", [P, TILES, KV * HD], F32))
                ss = mid.enter_context(nc.sbuf_tensor("ss", [P, TILES, 2], F32))
                hs = mid.enter_context(nc.sbuf_tensor("hs", [P, TILES, NH], F32))
                with ExitStack() as first:
                    c_raw = first.enter_context(nc.sbuf_tensor("c_raw", [P, TILES, C_COLS], F32))
                    project(nc, h, ident, w, w_loaded, mv, rstd, c_raw, ss)
                    heads(nc, ident, w["q"], w["kv"], w["cos"], w["sin"], c_raw, ss, qk, v_all, hs)
                attend(nc, h, ident, causal, w["out"], w["k_scale"], qk, v_all, hs, mv)
        with ExitStack() as last:
            x_hi = last.enter_context(nc.sbuf_tensor("x_hi", [P, TOKENS], F32R))
            x_lo = last.enter_context(nc.sbuf_tensor("x_lo", [P, TOKENS], F32R))
            comb_t = last.enter_context(nc.sbuf_tensor("comb_t", [EXPERTS, TOKENS], F32))
            rows_out = last.enter_context(nc.semaphore("rows_out"))
            route(nc, h, ident, ones_row, router_rev, router_b_rev, mv, rstd, x_hi, x_lo, comb_t, comb_rows, rows_out)
            experts(nc, h, ident, x_hi, x_lo, comb_t, comb_rows, rows_out, w1, b1, w2, b2_rev, out)


def load_attention(sp, w, loaded, w_dq, w_uq, w_qr, w_dkv, w_uk, w_uv, w_kr, w_vr, w_o, q_ln, kv_ln, q_hn, k_hn,
                   rope_cos, rope_sin):
    def load(to, source):
        sp.dma_start(to, source).then_inc(loaded, 16)
        issued.append(to)

    issued = []
    half = DR // 2
    load(w["latent"][:, C_Q:C_KV], w_dq)
    load(w["latent"][:, C_KV:C_KR], w_dkv)
    load(w["latent"][:, C_KR:C_RES], w_kr)
    load(w["kv_in"][:, 0:KV * DN], w_uk)
    load(w["kv_in"][:, KV * DN:], w_uv)
    load(w["qln"][:], q_ln.rearrange("(p a) -> p a", a=1))
    load(w["kvln"][:], kv_ln.rearrange("(p a) -> p a", a=1))
    for g in range(KV):
        heads_of = slice(g * GROUP, (g + 1) * GROUP)
        cols = slice(heads_of.start * DN, heads_of.stop * DN)
        wide = slice(heads_of.start * HD, heads_of.stop * HD)
        rows = slice(g * HD, (g + 1) * HD)
        load(w["vr_in"][:, :, g, :], w_vr[:, wide].rearrange("k (j d) -> k j d", d=HD))
        load(w["out"][rows, :, :], w_o[wide, :].rearrange("(j d) n -> d j n", d=HD))
        load(w["q_in"][:, :, g, 0:DN], w_uq[:, cols].rearrange("k (j n) -> k j n", n=DN))
        load(w["q_in"][:, :, g, DN:HD], w_qr[:, cols].rearrange("k (j n) -> k j n", n=DR))
        load(w["hn"][rows, 0:1], q_hn.rearrange("(p a) -> p a", a=1))
        load(w["hn"][rows, 1:2], k_hn.rearrange("(p a) -> p a", a=1))
    for c in range(2):
        at = slice(c * half, (c + 1) * half)
        load(w["cos"][:, :, at], rope_cos.rearrange("(t p) d -> p t d", p=P))
        load(w["sin"][:, :, at], rope_sin[c].rearrange("(t p) d -> p t d", p=P))
    assert len(issued) == LOADS_OF_ATTENTION


def embed_buffers(nc, ctx):
    def sb(name, shape):
        return ctx.enter_context(nc.sbuf_tensor(name, shape, F32))

    return {
        "cent": sb("cent", [P, CENTERS]),
        "neg_prec": sb("neg_prec", [P, CENTERS]),
        "table": sb("table", [P, CHUNKS, DIM]),
        "z": sb("z", [P, 4, CENTERS]),
        "gauss": sb("gauss", [P, 4, CENTERS]),
        "gauss_t": sb("gauss_t", [P, PARTS, CHUNKS // PARTS, P]),
        "loads": ctx.enter_context(nc.semaphore("e_loads")),
    }


def setup(nc, tok, pos, centers, logvar, emb, e, ident, ones_row, causal, npos):
    with ExitStack() as ctx:
        def sb(name, shape, dt=F32):
            return ctx.enter_context(nc.sbuf_tensor(name, shape, dt))

        def sem(name):
            return ctx.enter_context(nc.semaphore(name))

        tok_rows = sb("tok_rows", [TILES, P], I32)
        pos_rows = sb("pos_rows", [TILES, P])
        tok_f = sb("tok_f", [TILES, P])
        abs_rows = sb("abs_rows", [TILES, P])
        ps_pos = ctx.enter_context(nc.psum_tensor("ps_pos", [P, 512], F32))
        rows_in = sem("rows_in")
        zeroed = sem("zeroed")
        masks = sem("masks")
        posf = sem("posf")
        abs_ready = sem("abs_ready")
        pos_t = sem("pos_t")
        block = ctx.enter_context(nc.Block(name="setup"))

        @block.sync
        def _(sp):
            sp.dma_start(tok_rows[:], tok.rearrange("b (t p) -> (b t) p", p=P)).then_inc(rows_in, 16)
            sp.dma_start(pos_rows[:], pos.rearrange("b (t p) -> (b t) p", p=P)).then_inc(rows_in, 16)
            for to, row in ((e["cent"], centers), (e["neg_prec"], logvar)):
                sp.dma_start(to[:], row.rearrange("(a n) -> a n", a=1).broadcast_to([P, CENTERS])
                             ).then_inc(e["loads"], 16)
            sp.dma_start(e["table"][:], emb.rearrange("(c p) d -> p c d", p=P)).then_inc(e["loads"], 16)

        @block.gpsimd
        def _(pool):
            pool.memset(ident[:], 0.0).then_inc(zeroed, 1)
            pool.memset(causal[:], 0.0).then_inc(zeroed, 1)
            pool.memset(ones_row[:], 1.0).then_inc(zeroed, 1)
            pool.wait_ge(zeroed, 3)
            pool.affine_select(out=ident[:], in_=ident[:], compare_op=ALU.not_equal, fill=1.0, base=0,
                               pattern=[[-1, P]], channel_multiplier=1).then_inc(masks, 1)
            pool.affine_select(out=causal[:], in_=causal[:], compare_op=ALU.is_ge, fill=MASKED, base=0,
                               pattern=[[-1, P]], channel_multiplier=1).then_inc(masks, 1)

        @block.vector
        def _(dve):
            dve.wait_ge(rows_in, 32)
            dve.tensor_copy(tok_f[:], tok_rows[:]).then_inc(posf, 1)
            dve.wait_ge(posf, 1)
            dve.scalar_tensor_tensor(out=abs_rows[:], in0=tok_f[:], scalar=CHR_JUMP, in1=pos_rows[:],
                                     op0=ALU.mult, op1=ALU.add).then_inc(abs_ready, 1)
            dve.wait_ge(pos_t, 1)
            dve.tensor_scalar(npos[:], ps_pos[:, 0:TILES], -1.0, None, ALU.mult)

        @block.tensor
        def _(pe):
            pe.wait_ge(masks, 2)
            pe.wait_ge(abs_ready, 1)
            pe.transpose(ps_pos[:, 0:TILES], abs_rows[:], ident[0:TILES, 0:TILES]).then_inc(pos_t, 1)


def embed(nc, e, h, ident, npos, mv, flag, general, load_weights):
    RING = 4
    PC = CHUNKS // PARTS
    kind = "g_" if general else "e_"
    cent, neg_prec, table, z, gauss, gauss_t = (e[k] for k in ("cent", "neg_prec", "table", "z", "gauss", "gauss_t"))
    with ExitStack() as ctx:
        def sb(name, shape, dt=F32):
            return ctx.enter_context(nc.sbuf_tensor(kind + name, shape, dt))

        def sem(name):
            return ctx.enter_context(nc.semaphore(kind + name))

        found = sb("found", [P, CLASSES, 8])
        left = sb("left", [P, CLASSES, 8])
        eighth = sb("eighth", [P, 1])
        doubt = sb("doubt", [P, TILES])
        doubts = sb("doubts", [P, 1])
        ones_col = sb("ones_col", [P, 1])
        top_a = sb("top_a", [P, 8])
        top_b = sb("top_b", [P, 8])
        wsum = sb("wsum", [P, RING])
        rsum = sb("rsum", [P, RING])
        stats = sb("stats", [P, 6])
        mvt = sb("mvt", [P, 2])
        ps_t = [ctx.enter_context(nc.psum_tensor(f"{kind}ps_t{k}", [P, PC, P], F32)) for k in range(PARTS)]
        ps_h = ctx.enter_context(nc.psum_tensor(kind + "ps_h", [P, 2, 512], F32))
        prec_exp = sem("prec_exp")
        prec = sem("prec")
        squared = sem("squared")
        z_ready = sem("z_ready")
        gauss_ready = sem("gauss_ready")
        sel_step = sem("sel_step")
        fin_step = sem("fin_step")
        chosen = sem("chosen")
        turned = sem("turned")
        copied = sem("copied")
        product = sem("product")
        tile_done = sem("tile_done")
        flag_step = sem("flag_step")
        flag_summed = sem("flag_summed")
        block = ctx.enter_context(nc.Block(name=kind + "embed"))

        def engine_program(eng, body):
            if not general:
                body(eng)
                return
            with eng.If(eng.value_load(flag[0:1, 0:1], min_val=0, max_val=P) > 0):
                body(eng)

        if load_weights is not None:
            @block.sync
            def _(sp):
                load_weights(sp)

        @block.scalar
        def _(act):
            def square(t, r):
                if in_range(t, TILES):
                    after(act, chosen, t - (RING - 1))
                    act.activation(z[:, r, :], cent[:], ACT.Square, bias=npos[:, bass.ds(t, 1)]).then_inc(squared, 1)

            def exponential(t, r):
                if in_range(t, TILES):
                    act.wait_ge(z_ready, t + 1)
                    act.activation(gauss[:, r, :], z[:, r, :], ACT.Exp).then_inc(gauss_ready, 1)

            def copy_out(t):
                if in_range(t, TILES):
                    for k in range(PARTS):
                        act.wait_ge(turned, t * PARTS + (k + 1))
                        after(act, product, t)
                        act.activation(gauss_t[:, k], ps_t[k][:], ACT.Copy).then_inc(copied, 1)

            def step(t, r):
                square(t, r)
                exponential(t - 1, (r - 1) % RING)
                copy_out(t - 3)

            def body(act):
                if not general:
                    act.wait_ge(e["loads"], 48)
                    act.activation(neg_prec[:], neg_prec[:], ACT.Exp, scale=-1.0).then_inc(prec_exp, 1)
                in_pairs(act, step, TILES, RING)
                for t in range(TILES, TILES + 3):
                    step(t, t % RING)

            engine_program(act, body)

        @block.gpsimd
        def _(pool):
            def step(t, r):
                pool.wait_ge(squared, t + 1)
                pool.tensor_tensor(z[:, r, :], z[:, r, :], neg_prec[:], ALU.mult).then_inc(z_ready, 1)

            def body(pool):
                if not general:
                    pool.wait_ge(prec, 1)
                in_pairs(pool, step, TILES, RING)

            engine_program(pool, body)

        @block.vector
        def _(dve):
            def quick_select(t, r):
                link = chained(dve, sel_step, t * 6)
                hold(dve, z_ready, t + 1)
                if r or not isinstance(t, int):
                    hold(dve, chosen, t)
                of_class = z[:, r, :].rearrange("p (n c) -> p c n", c=CLASSES)
                for c in range(CLASSES - 1):
                    dve.max(found[:, c, :], of_class[:, c, :])
                link(dve.max(found[:, CLASSES - 1, :], of_class[:, CLASSES - 1, :]))
                link(dve.max(top_a[:], found[:]))
                link(dve.match_replace(left[:], top_a[:], found[:], MARK))
                link(dve.max(top_b[:], left[:]))
                link(dve.tensor_reduce(eighth[:], found[:, :, 7], AX.X, ALU.max))
                link(dve.tensor_scalar(doubt[:, bass.ds(t, 1)], eighth[:], top_b[:, TOPK - 8:TOPK - 7],
                                       top_b[:, TOPK - 9:TOPK - 8], ALU.max, ALU.is_ge))
                dve.wait_ge(gauss_ready, t + 1)
                dve.scalar_tensor_tensor(out=gauss[:, r, :], in0=z[:, r, :], scalar=top_b[:, TOPK - 9:TOPK - 8],
                                         in1=gauss[:, r, :], op0=ALU.is_ge, op1=ALU.mult,
                                         accum_out=wsum[:, r:r + 1]).then_inc(chosen, 1)

            def general_select(t, r):
                link = chained(dve, sel_step, t * 5)
                hold(dve, gauss_ready, t + 1)
                link(dve.max(top_a[:], z[:, r, :]))
                link(dve.match_replace(z[:, r, :], top_a[:], z[:, r, :], MARK))
                link(dve.max(top_b[:], z[:, r, :]))
                link(dve.memset(top_b[:, TOPK - 8:8], MARK))
                link(dve.match_replace(z[:, r, :], top_b[:], z[:, r, :], MARK))
                dve.scalar_tensor_tensor(out=gauss[:, r, :], in0=z[:, r, :], scalar=MARK, in1=gauss[:, r, :],
                                         op0=ALU.is_le, op1=ALU.mult, accum_out=wsum[:, r:r + 1]
                                         ).then_inc(chosen, 1)
                hold(dve, chosen, t + 1)

            def finish(t, r):
                if not in_range(t, TILES):
                    return
                link = chained(dve, fin_step, t * 4)
                dve.wait_ge(chosen, t + 1)
                link(dve.reciprocal(rsum[:, r:r + 1], wsum[:, r:r + 1]))
                dve.wait_ge(product, t + 1)
                link(dve.tensor_scalar(h[:, t, :], ps_h[:, r % 2, 0:DIM], rsum[:, r:r + 1], None, ALU.mult))
                link(dve.bn_stats(stats[:], h[:, t, :]))
                link(dve.bn_aggr(mvt[:], stats[:]))
                dve.tensor_copy(mv[:, t, :], mvt[:]).then_inc(tile_done, 1)
                hold(dve, tile_done, t + 1)

            def step(t, r):
                (general_select if general else quick_select)(t, r)
                finish(t - 2, (r - 2) % RING)

            def body(dve):
                if not general:
                    dve.memset(ones_col[:], 1.0).then_inc(flag_step, 1)
                    dve.wait_ge(prec_exp, 1)
                    dve.tensor_scalar(neg_prec[:], neg_prec[:], -0.5, None, ALU.mult).then_inc(prec, 1)
                in_pairs(dve, step, TILES, RING)
                for t in (TILES - 2, TILES - 1):
                    finish(t, t % RING)
                if not general:
                    dve.tensor_reduce(doubts[:], doubt[:], AX.X, ALU.max).then_inc(flag_step, 1)
                    dve.wait_ge(flag_summed, 1)
                    dve.tensor_copy(flag[:], ps_h[0:1, 0, 0:1])

            engine_program(dve, body)

        @block.tensor
        def _(pe):
            def step(t, r):
                b = r % 2
                pe.wait_ge(chosen, t + 1)
                for k in range(PARTS):
                    after(pe, copied, (t - 1) * PARTS + (k + 1))
                    for c in range(PC):
                        at = (k * PC + c) * P
                        last = pe.transpose(ps_t[k][:, c, :], gauss[:, r, at:at + P], ident[:])
                    last.then_inc(turned, 1)
                after(pe, tile_done, t - 1)
                for k in range(PARTS):
                    pe.wait_ge(copied, t * PARTS + (k + 1))
                    for c in range(PC):
                        last = pe.matmul(ps_h[:, b, 0:DIM], gauss_t[:, k, c, :], table[:, k * PC + c, :],
                                         start=(k == 0 and c == 0), stop=(k == PARTS - 1 and c == PC - 1))
                last.then_inc(product, 1)

            def body(pe):
                in_pairs(pe, step, TILES, RING)
                if not general:
                    pe.wait_ge(flag_step, 2)
                    pe.wait_ge(tile_done, TILES)
                    pe.matmul(ps_h[0:1, 0, 0:1], doubts[:], ones_col[:], start=True, stop=True
                              ).then_inc(flag_summed, 1)

            engine_program(pe, body)


def project(nc, h, ident, w, w_loaded, mv, rstd, c_raw, ss):
    with ExitStack() as ctx:
        def sb(name, shape, dt=F32):
            return ctx.enter_context(nc.sbuf_tensor(name, shape, dt))

        def sem(name):
            return ctx.enter_context(nc.semaphore(name))

        vr_t = sb("vr_t", [P, GROUP, DIM])
        ps_vr = ctx.enter_context(nc.psum_tensor("ps_vr", [P, GROUP, P], F32))
        ps_m = ctx.enter_context(nc.psum_tensor("ps_m", [P, 512], F32))
        vr_turned = sem("vr_turned")
        vr_copied = sem("vr_copied")
        m_ready = sem("m_ready")
        w_ready = sem("w_ready")
        shifted = sb("p_shifted", [P, TILES])
        root = sb("p_root", [P, TILES])
        xn = sb("xn", [P, 2, DIM])
        x_t = sb("x_t", [P, 2, P])
        junk = sb("junk", [P, LQ + LKV])
        ps_x = ctx.enter_context(nc.psum_tensor("ps_x", [P, 2, 512], F32))
        ps_c = ctx.enter_context(nc.psum_tensor("ps_c", [P, 2, 512], F32))
        var_eps = sem("var_eps")
        rooted = sem("p_rooted")
        rstd_ready = sem("rstd_ready")
        normed = sem("normed")
        turned = sem("p_turned")
        x_copied = sem("x_copied")
        projected = sem("projected")
        c_copied = sem("c_copied")
        squared = sem("p_squared")
        block = ctx.enter_context(nc.Block(name="project"))

        @block.scalar
        def _(act):
            act.wait_ge(var_eps, 1)
            act.activation(root[:], shifted[:], ACT.Sqrt).then_inc(rooted, 1)

            def latents(t, b):
                act.wait_ge(projected, t + 1)
                act.activation(c_raw[:, t, :], ps_c[:, b, 0:C_COLS], ACT.Copy).then_inc(c_copied, 1)
                act.wait_ge(c_copied, t + 1)
                after(act, squared, t)
                act.activation(junk[:, C_Q:C_KV], c_raw[:, t, C_Q:C_KV], ACT.Square, accum_out=ss[:, t, 0:1])
                act.activation(junk[:, C_KV:C_KR], c_raw[:, t, C_KV:C_KR], ACT.Square, accum_out=ss[:, t, 1:2]
                               ).then_inc(squared, 1)

            def step(t, b):
                act.wait_ge(turned, t + 1)
                act.activation(x_t[:, b, :], ps_x[:, b, 0:P], ACT.Copy).then_inc(x_copied, 1)
                if not isinstance(t, int) or t >= 1:
                    latents(t - 1, 1 - b)

            in_pairs(act, step, TILES)
            latents(TILES - 1, 1)

        @block.vector
        def _(dve):
            dve.tensor_scalar(shifted[:], mv[:, :, 1], LN_EPS, None, ALU.add).then_inc(var_eps, 1)
            dve.wait_ge(w_loaded, 16 * LOADS_OF_ATTENTION)
            dve.tensor_scalar(w["q"][:], w["q_in"][:], w["qln"][:, 0:1], None, ALU.mult)
            dve.tensor_scalar(w["kv"][:], w["kv_in"][:], w["kvln"][:, 0:1], None, ALU.mult)
            dve.scalar_tensor_tensor(out=w["k_scale"][:], in0=w["hn"][:, 0:1], scalar=float(HD) ** -0.5,
                                     in1=w["hn"][:, 1:2], op0=ALU.mult, op1=ALU.mult)
            dve.wait_ge(vr_turned, 1)
            dve.tensor_copy(vr_t[:], ps_vr[:]).then_inc(vr_copied, 1)
            dve.wait_ge(m_ready, 1)
            dve.tensor_copy(w["latent"][:, C_RES:C_COLS], ps_m[:, 0:DIM]).then_inc(w_ready, 1)
            dve.wait_ge(rooted, 1)
            dve.reciprocal(rstd[:], root[:]).then_inc(rstd_ready, 1)
            dve.wait_ge(rstd_ready, 1)

            def add_residual(t):
                dve.wait_ge(c_copied, t + 1)
                dve.tensor_tensor(h[:, t, :], h[:, t, :], c_raw[:, t, C_RES:C_COLS], ALU.add)

            def step(t, b):
                after(dve, turned, t - 1)
                dve.tensor_scalar(xn[:, b, :], h[:, t, :], mv[:, t, 0:1], rstd[:, bass.ds(t, 1)], ALU.subtract,
                                  ALU.mult).then_inc(normed, 1)
                if not isinstance(t, int) or t >= 2:
                    add_residual(t - 2)

            in_pairs(dve, step, TILES)
            add_residual(TILES - 2)
            add_residual(TILES - 1)

        @block.tensor
        def _(pe):
            pe.wait_ge(w_loaded, 16 * LOADS_OF_ATTENTION)
            for j in range(GROUP):
                last = pe.transpose(ps_vr[:, j, :], w["vr_in"][:, j].rearrange("k g d -> k (g d)"), ident[:])
            last.then_inc(vr_turned, 1)
            pe.wait_ge(vr_copied, 1)
            for j in range(GROUP):
                last = pe.matmul(ps_m[:, 0:DIM], vr_t[:, j, :], w["out"][:, j, :], start=(j == 0),
                                 stop=(j == GROUP - 1))
            last.then_inc(m_ready, 1)
            pe.wait_ge(w_ready, 1)

            def product(t, b):
                pe.wait_ge(x_copied, t + 1)
                after(pe, c_copied, t - 1)
                pe.matmul(ps_c[:, b, 0:C_COLS], x_t[:, b, :], w["latent"][:], start=True, stop=True
                          ).then_inc(projected, 1)

            def step(t, b):
                pe.wait_ge(normed, t + 1)
                after(pe, x_copied, t - 1)
                pe.transpose(ps_x[:, b, 0:P], xn[:, b, :], ident[:]).then_inc(turned, 1)
                if not isinstance(t, int) or t >= 1:
                    product(t - 1, 1 - b)

            in_pairs(pe, step, TILES)
            product(TILES - 1, 1)


def heads(nc, ident, w_q, w_kv, cos2, sin2, c_raw, ss, qk, v_all, hs):
    with ExitStack() as ctx:
        def sb(name, shape, dt=F32):
            return ctx.enter_context(nc.sbuf_tensor(name, shape, dt))

        def sem(name):
            return ctx.enter_context(nc.semaphore(name))

        mean_sq = sb("mean_sq", [P, 2, TILES])
        root = sb("h_root", [P, 2, TILES])
        rms = sb("rms", [P, 2, TILES])
        cn = sb("cn", [P, 2, LQ + LKV])
        c_t = sb("c_t", [P, 2, 2 * P])
        turned_cos = sb("turned_cos", [P, NH, DR])
        turned_sin = sb("turned_sin", [P, NH, DR])
        sq = sb("sq", [P, 2, NH, HD])
        ps_ct = ctx.enter_context(nc.psum_tensor("ps_ct", [P, 2, 512], F32))
        ps_q = ctx.enter_context(nc.psum_tensor("ps_q", [P, 2, 512], F32))
        ps_kv = ctx.enter_context(nc.psum_tensor("ps_kv", [P, 2, 512], F32))
        mean_ready = sem("mean_ready")
        rooted = sem("h_rooted")
        rms_ready = sem("rms_ready")
        normed = sem("c_normed")
        turned = sem("c_turned")
        c_copied = sem("ct_copied")
        projected = sem("qkv_projected")
        out_copied = sem("qkv_copied")
        rope_step = sem("rope_step")
        roped = sem("roped")
        squares = sem("squares")
        head_sums = sem("head_sums")
        block = ctx.enter_context(nc.Block(name="heads"))
        half = DR // 2

        @block.scalar
        def _(act):
            act.wait_ge(mean_ready, 2)
            act.activation(root[:], mean_sq[:], ACT.Sqrt).then_inc(rooted, 1)

            def copy_out(t, b):
                act.wait_ge(projected, t + 1)
                act.activation(qk[:, t, 0:HEADS, :], ps_q[:, b, :].rearrange("p (n d) -> p n d", d=HD), ACT.Copy)
                act.activation(qk[:, t, HEADS:NH, 0:DN], ps_kv[:, b, 0:KV * DN].rearrange("p (n d) -> p n d", d=DN),
                               ACT.Copy)
                act.activation(v_all[:, t, :], ps_kv[:, b, KV * DN:KV * (DN + HD)], ACT.Copy)
                act.activation(qk[:, t, HEADS:NH, DN:HD], c_raw[:, t, C_KR:C_RES].rearrange("p (n d) -> p n d", d=DR),
                               ACT.Copy).then_inc(out_copied, 1)

            def step(t, b):
                act.wait_ge(turned, t + 1)
                act.activation(c_t[0:LQ, b, 0:P], ps_ct[0:LQ, b, 0:P], ACT.Copy)
                act.activation(c_t[:, b, P:2 * P], ps_ct[:, b, P:2 * P], ACT.Copy).then_inc(c_copied, 1)
                if not isinstance(t, int) or t >= 1:
                    copy_out(t - 1, 1 - b)

            in_pairs(act, step, TILES)
            copy_out(TILES - 1, 1)

        @block.vector
        def _(dve):
            for k, n in enumerate((LQ, LKV)):
                dve.tensor_scalar(mean_sq[:, k, :], ss[:, :, k], 1.0 / n, RMS_EPS, ALU.mult, ALU.add
                                  ).then_inc(mean_ready, 1)
            dve.wait_ge(rooted, 1)
            dve.reciprocal(rms[:], root[:]).then_inc(rms_ready, 1)
            dve.wait_ge(rms_ready, 1)

            def cn_of(t, b):
                if in_range(t, TILES):
                    after(dve, turned, t - 1)
                    dve.tensor_scalar(cn[:, b, 0:LQ], c_raw[:, t, C_Q:C_KV], rms[:, 0, bass.ds(t, 1)], None, ALU.mult)
                    dve.tensor_scalar(cn[:, b, LQ:], c_raw[:, t, C_KV:C_KR], rms[:, 1, bass.ds(t, 1)], None, ALU.mult
                                      ).then_inc(normed, 1)

            def rope(t, b):
                if in_range(t, TILES):
                    dve.wait_ge(out_copied, t + 1)
                    link = chained(dve, rope_step, t)
                    x = qk[:, t, :, DN:HD]
                    cos = cos2[:, b:b + 1, :].broadcast_to([P, NH, DR])
                    sin = sin2[:, b:b + 1, :].broadcast_to([P, NH, DR])
                    if not isinstance(t, int) or t >= 1:
                        hold(dve, roped, t)
                    dve.tensor_tensor(turned_sin[:, :, 0:half], qk[:, t, :, DN + half:HD], sin[:, :, 0:half],
                                      ALU.mult)
                    dve.tensor_tensor(turned_sin[:, :, half:DR], qk[:, t, :, DN:DN + half], sin[:, :, half:DR],
                                      ALU.mult)
                    link(dve.tensor_tensor(turned_cos[:], x, cos, ALU.mult))
                    dve.tensor_tensor(x, turned_cos[:], turned_sin[:], ALU.add).then_inc(roped, 1)

            def sum_up(t, b):
                if in_range(t, TILES):
                    dve.wait_ge(squares, t + 1)
                    dve.tensor_reduce(hs[:, t, :], sq[:, b], AX.X, ALU.add).then_inc(head_sums, 1)

            def step(t, r):
                cn_of(t, r % 2)
                rope(t - 3, (r - 3) % 2)
                sum_up(t - 4, r % 2)

            in_pairs(dve, step, TILES, 4)
            for t in range(TILES, TILES + 4):
                step(t, t)

        @block.gpsimd
        def _(pool):
            def step(t, b):
                pool.wait_ge(roped, t + 1)
                after(pool, head_sums, t - 1)
                pool.tensor_tensor(sq[:, b], qk[:, t], qk[:, t], ALU.mult).then_inc(squares, 1)

            in_pairs(pool, step, TILES)

        @block.tensor
        def _(pe):
            def product(t, b):
                pe.wait_ge(c_copied, t + 1)
                after(pe, out_copied, t - 1)
                pe.matmul(ps_q[:, b, :], c_t[0:LQ, b, 0:P], w_q[:].rearrange("k j g d -> k (j g d)"), start=True,
                          stop=True)
                pe.matmul(ps_kv[:, b, 0:KV * (DN + HD)], c_t[:, b, P:2 * P], w_kv[:], start=True, stop=True
                          ).then_inc(projected, 1)

            def step(t, b):
                pe.wait_ge(normed, t + 1)
                if not isinstance(t, int) or t >= 2:
                    hold(pe, c_copied, t - 1)
                pe.transpose(ps_ct[0:LQ, b, 0:P], cn[:, b, 0:LQ], ident[:])
                pe.transpose(ps_ct[:, b, P:2 * P], cn[:, b, LQ:], ident[:]).then_inc(turned, 1)
                if not isinstance(t, int) or t >= 1:
                    product(t - 1, 1 - b)

            in_pairs(pe, step, TILES)
            product(TILES - 1, 1)


def attend(nc, h, ident, causal, w_out, k_scale, qk, v_all, hs, mv):
    UNITS = 2 * BATCH
    with ExitStack() as ctx:
        def sb(name, shape, dt=F32):
            return ctx.enter_context(nc.sbuf_tensor(name, shape, dt))

        def sem(name):
            return ctx.enter_context(nc.semaphore(name))

        mean_sq = sb("a_mean_sq", [P, TILES, NH])
        rms = sb("a_rms", [P, TILES, NH])
        qkn = sb("qkn", [P, 2, NH, HD])
        v_s = sb("v_s", [P, 2, 2, KV * HD])
        q_t = sb("q_t", [P, 2, GROUP, P])
        k_t = sb("k_t", [P, 2, SEQ])
        sm = sb("sm", [P, 4, HEADS, SEQ])
        neg_max = sb("neg_max", [P, 4, HEADS])
        rowsum = sb("rowsum", [P, 4, HEADS])
        rinv = sb("rinv", [P, 4, HEADS])
        p_t = sb("p_t", [P, 2, HEADS, P])
        o_n = sb("o_n", [P, GROUP, KV, HD])
        o_t = sb("o_t", [P, GROUP, P])
        stats = sb("a_stats", [P, 6])
        mvt = sb("a_mvt", [P, 2])
        ps_s = ctx.enter_context(nc.psum_tensor("ps_s", [P, HEADS, SEQ], F32))
        ps_p = ctx.enter_context(nc.psum_tensor("ps_p", [P, HEADS, P], F32))
        ps_qy = ctx.enter_context(nc.psum_tensor("ps_qy", [P, GROUP, P], F32))
        ps_ko = ctx.enter_context(nc.psum_tensor("ps_ko", [P, GROUP, P], F32))
        mean_ready = sem("a_mean_ready")
        rooted = sem("a_rooted")
        rms_ready = sem("a_rms_ready")
        qk_normed = sem("qk_normed")
        q_turned = sem("q_turned")
        k_turned = sem("k_turned")
        q_copied = sem("q_copied")
        k_copied = sem("k_copied")
        scored = sem("scored")
        masked = sem("masked")
        max_ready = sem("max_ready")
        exp_done = sem("exp_done")
        rinv_ready = sem("rinv_ready")
        v_ready = sem("v_ready")
        o_normed = sem("o_normed")
        o_turned = sem("o_turned")
        p_turned = sem("p_turned")
        p_copied = sem("p_copied")
        mixed = sem("mixed")
        o_copied = sem("o_copied")
        y_ready = sem("y_ready")
        y_added = sem("y_added")
        mv_step = sem("mv_step")
        block = ctx.enter_context(nc.Block(name="attend"))

        def blocks_before(u, r):
            whole = u // 2 if isinstance(u, int) else (u - r % 2) // 2
            return whole * 3 + r % 2

        def all_steps(eng, step):
            in_pairs(eng, step, UNITS - 4, 4)
            for u in range(UNITS - 4, UNITS + 4):
                step(u, u % 4)

        @block.scalar
        def _(act):
            act.wait_ge(mean_ready, 1)
            act.activation(mean_sq[:], mean_sq[:], ACT.Sqrt).then_inc(rooted, 1)

            def copy_q(u, r):
                if in_range(u, UNITS):
                    act.wait_ge(q_turned, u + 1)
                    act.activation(q_t[:, r % 2], ps_qy[:], ACT.Copy).then_inc(q_copied, 1)

            def copy_k(u, r):
                if in_range(u, UNITS):
                    q, s = r % 2, r // 2 % 2
                    act.wait_ge(k_turned, u + 1)
                    act.activation(k_t[:, s, q * P:(q + 1) * P], ps_ko[:, 0, :], ACT.Copy, scale=k_scale[:, 0:1]
                                   ).then_inc(k_copied, 1)

            def copy_p(u, r, k):
                if in_range(u, UNITS):
                    act.wait_ge(p_turned, blocks_before(u, r) + k + 1)
                    act.activation(p_t[:, k], ps_p[:], ACT.Copy).then_inc(p_copied, 1)

            def copy_o(u):
                if in_range(u, UNITS):
                    act.wait_ge(o_turned, u + 1)
                    act.activation(o_t[:], ps_qy[:], ACT.Copy).then_inc(o_copied, 1)

            def exps(u, r):
                if in_range(u, UNITS):
                    keys = (r % 2 + 1) * P
                    act.wait_ge(max_ready, u + 1)
                    for n in range(HEADS):
                        last = act.activation(sm[:, r, n, 0:keys], sm[:, r, n, 0:keys], ACT.Exp,
                                              bias=neg_max[:, r, n:n + 1], accum_out=rowsum[:, r, n:n + 1])
                    last.then_inc(exp_done, 1)

            def step(u, r):
                copy_p(u - 3, (r - 3) % 4, 0)
                copy_o(u - 4)
                if (r - 3) % 2:
                    copy_p(u - 3, (r - 3) % 4, 1)
                copy_q(u + 1, (r + 1) % 4)
                copy_k(u + 1, (r + 1) % 4)
                exps(u - 1, (r - 1) % 4)

            copy_q(0, 0)
            copy_k(0, 0)
            all_steps(act, step)

        @block.gpsimd
        def _(pool):
            pool.wait_ge(rms_ready, 1)

            def norm_qk(u, r):
                if in_range(u, UNITS):
                    after(pool, k_turned, u - 1)
                    pool.tensor_tensor(qkn[:, r % 2], qk[:, u], rms[:, bass.ds(u, 1), :]
                                       .rearrange("p a n -> p (a n)").unsqueeze(2).broadcast_to([P, NH, HD]),
                                       ALU.mult).then_inc(qk_normed, 1)

            def copy_v(u, r):
                if in_range(u, UNITS):
                    q, s = r % 2, r // 2 % 2
                    after(pool, mixed, u - 2 - q)
                    pool.tensor_copy(v_s[:, s, q, :], v_all[:, u, :]).then_inc(v_ready, 1)

            def step(u, r):
                norm_qk(u, r)
                copy_v(u - 2, (r - 2) % 4)

            in_pairs(pool, step, UNITS - 4, 4)
            for u in range(UNITS - 4, UNITS + 2):
                step(u, u % 4)

        @block.vector
        def _(dve):
            dve.tensor_scalar(mean_sq[:], hs[:], 1.0 / HD, RMS_EPS, ALU.mult, ALU.add).then_inc(mean_ready, 1)
            dve.wait_ge(rooted, 1)
            dve.reciprocal(rms[:], mean_sq[:]).then_inc(rms_ready, 1)

            def add_y(u):
                if in_range(u, UNITS):
                    dve.wait_ge(y_ready, u + 1)
                    dve.tensor_tensor(h[:, u, :], h[:, u, :], ps_ko[:, 0, :], ALU.add).then_inc(y_added, 1)

            def mask(u, r):
                if in_range(u, UNITS):
                    q = r % 2
                    dve.wait_ge(scored, u + 1)
                    if q:
                        dve.tensor_copy(sm[:, r, :, 0:P], ps_s[:, :, 0:P])
                    dve.tensor_tensor(sm[:, r, :, q * P:(q + 1) * P], ps_s[:, :, q * P:(q + 1) * P],
                                      causal[:].unsqueeze(1).broadcast_to([P, HEADS, P]), ALU.add
                                      ).then_inc(masked, 1)

            def maximum(u, r):
                if in_range(u, UNITS):
                    dve.wait_ge(masked, u + 1)
                    dve.tensor_reduce(neg_max[:, r, :], sm[:, r, :, 0:(r % 2 + 1) * P], AX.X, ALU.max, negate=True
                                      ).then_inc(max_ready, 1)

            def norm_o(u, r):
                if in_range(u, UNITS):
                    dve.wait_ge(exp_done, u + 1)
                    dve.reciprocal(rinv[:, r, :], rowsum[:, r, :]).then_inc(rinv_ready, 1)
                    hold(dve, rinv_ready, u + 1)
                    dve.wait_ge(mixed, u + 1)
                    dve.tensor_tensor(o_n[:].rearrange("p j g d -> p g j d"),
                                      ps_ko[:].rearrange("p a b -> p (a b)").rearrange("p (g j d) -> p g j d", g=KV,
                                                                                       j=GROUP),
                                      rinv[:, r, :].rearrange("p (g j) -> p g j", g=KV).unsqueeze(3)
                                      .broadcast_to([P, KV, GROUP, HD]), ALU.mult).then_inc(o_normed, 1)

            def statistics(u):
                if in_range(u, UNITS):
                    link = chained(dve, mv_step, u * 3)
                    hold(dve, y_added, u + 1)
                    link(dve.bn_stats(stats[:], h[:, u, :]))
                    link(dve.bn_aggr(mvt[:], stats[:]))
                    link(dve.tensor_copy(mv[:, u, :], mvt[:]))

            def step(u, r):
                mask(u - 1, (r - 1) % 4)
                norm_o(u - 4, r)
                maximum(u - 1, (r - 1) % 4)
                add_y(u - 4)
                statistics(u - 4)

            all_steps(dve, step)

        @block.tensor
        def _(pe):
            def project_out(u):
                if in_range(u, UNITS):
                    pe.wait_ge(o_copied, u + 1)
                    for j in range(GROUP):
                        last = pe.matmul(ps_ko[:, 0, :], o_t[:, j, :], w_out[:, j, :], start=(j == 0),
                                         stop=(j == GROUP - 1))
                    last.then_inc(y_ready, 1)

            def turn_p(u, r, k):
                if in_range(u, UNITS):
                    if k == 0:
                        pe.wait_ge(exp_done, u + 1)
                    after(pe, p_copied, blocks_before(u, r) + k)
                    for n in range(HEADS):
                        last = pe.transpose(ps_p[:, n, :], sm[:, r, n, k * P:(k + 1) * P], ident[:])
                    last.then_inc(p_turned, 1)

            def turn_q(u, r):
                if in_range(u, UNITS):
                    pe.wait_ge(qk_normed, u + 1)
                    if isinstance(u, int):
                        after(pe, q_copied, u)
                    for j in range(GROUP):
                        last = pe.transpose(ps_qy[:, j, :], qkn[:, r % 2, KV * j:KV * (j + 1), :]
                                            .rearrange("p n d -> p (n d)"), ident[:])
                    last.then_inc(q_turned, 1)

            def turn_k(u, r):
                if in_range(u, UNITS):
                    if isinstance(u, int):
                        after(pe, k_copied, u)
                    after(pe, y_added, u - 4)
                    pe.transpose(ps_ko[:, 0, :], qkn[:, r % 2, HEADS:NH, :].rearrange("p n d -> p (n d)"), ident[:]
                                 ).then_inc(k_turned, 1)

            def mix(u, r, turning):
                if in_range(u, UNITS):
                    q, s = r % 2, r // 2 % 2
                    if turning:
                        pe.wait_ge(k_copied, u + 5)
                    else:
                        pe.wait_ge(y_added, u)
                    pe.wait_ge(v_ready, u + 1)
                    pe.wait_ge(p_copied, blocks_before(u, r) + q + 1)
                    for n in range(HEADS):
                        at = slice(n // GROUP * HD, (n // GROUP + 1) * HD)
                        for k in range(q + 1):
                            last = pe.matmul(ps_o[:, n, :], p_t[:, k, n, :], v_s[:, s, k, at], start=(k == 0),
                                             stop=(k == q))
                    last.then_inc(mixed, 1)

            def score(u, r, banks):
                if in_range(u, UNITS):
                    q, s = r % 2, r // 2 % 2
                    if 0 in banks:
                        pe.wait_ge(q_copied, u + 1)
                        pe.wait_ge(k_copied, u + 1)
                        after(pe, masked, u)
                    for n in (n for bank in banks for n in (2 * bank, 2 * bank + 1)):
                        at = slice(n // GROUP * HD, (n // GROUP + 1) * HD)
                        last = pe.matmul(ps_s[:, n, 0:(q + 1) * P], q_t[at, q, n % GROUP, :],
                                         k_t[at, s, 0:(q + 1) * P], start=True, stop=True)
                    if HEADS // 2 - 1 in banks:
                        last.then_inc(scored, 1)

            def turn_o(u):
                if in_range(u, UNITS):
                    if in_range(u + 4, UNITS):
                        pe.wait_ge(q_copied, u + 5)
                    pe.wait_ge(o_normed, u + 1)
                    for j in range(GROUP):
                        last = pe.transpose(ps_qy[:, j, :], o_n[:, j].rearrange("p g d -> p (g d)"), ident[:])
                    last.then_inc(o_turned, 1)

            def step(u, r):
                v, rv = u - 3, (r - 3) % 4
                turn_p(v, rv, 0)
                turn_o(u - 4)
                score(u, r, (0, 1))
                project_out(u - 4)
                if rv % 2:
                    turn_p(v, rv, 1)
                turn_q(u + 1, (r + 1) % 4)
                score(u, r, (2,))
                turn_k(u + 1, (r + 1) % 4)
                score(u, r, (3,))
                mix(v, rv, in_range(u + 1, UNITS))

            ps_o = ps_ko[:].rearrange("p a b -> p (a b)").rearrange("p (n d) -> p n d", d=HD)
            turn_q(0, 0)
            turn_k(0, 0)
            all_steps(pe, step)


def route(nc, h, ident, ones_row, router_rev, router_b_rev, mv, rstd, x_hi, x_lo, comb_t, comb_rows, rows_out):
    QT = GT // P
    QUADS = TILES // QT
    with ExitStack() as ctx:
        def sb(name, shape, dt=F32):
            return ctx.enter_context(nc.sbuf_tensor(name, shape, dt))

        def sem(name):
            return ctx.enter_context(nc.semaphore(name))

        rw = sb("rw", [P, EXPERTS])
        rb = sb("rb", [1, EXPERTS])
        shifted = sb("r_shifted", [P, TILES])
        root = sb("r_root", [P, TILES])
        xn = sb("r_xn", [P, 2, QT, DIM])
        x_s = sb("x_s", [P, 2, GT])
        neg_max = sb("r_neg_max", [P, QT])
        d1 = sb("d1", [P, QT, EXPERTS])
        e1 = sb("e1", [P, QT, EXPERTS])
        neg_s1 = sb("neg_s1", [P, QT])
        neg_r1 = sb("neg_r1", [P, QT])
        neg_p = sb("neg_p", [P, QT, EXPERTS])
        d2 = sb("d2", [P, QT, EXPERTS])
        e2 = sb("e2", [P, QT, EXPERTS])
        left = sb("left", [P, QT, EXPERTS])
        low = sb("low", [P, QT, 8])
        top = sb("top", [P, QT, EXPERTS])
        s2 = sb("s2", [P, QT])
        r2 = sb("r2", [P, QT])
        comb = sb("comb", [P, 2, QT, EXPERTS])
        ps_x = ctx.enter_context(nc.psum_tensor("r_ps_x", [P, 2, GT], F32))
        ps_l = ctx.enter_context(nc.psum_tensor("ps_l", [P, 2, 512], F32))
        ps_c = ctx.enter_context(nc.psum_tensor("r_ps_c", [P, 2, GT], F32))
        loads = sem("r_loads")
        var_eps = sem("r_var_eps")
        rooted = sem("r_rooted")
        rstd_ready = sem("r_rstd_ready")
        normed = sem("r_normed")
        turned = sem("r_turned")
        x_copied = sem("r_x_copied")
        hi_ready = sem("hi_ready")
        x_used = sem("x_used")
        logits = sem("logits")
        max_ready = sem("r_max_ready")
        d1_ready = sem("d1_ready")
        exp_one = sem("exp_one")
        d2_ready = sem("d2_ready")
        exp_two = sem("exp_two")
        sum_step = sem("sum_step")
        top_step = sem("top_step")
        comb_ready = sem("comb_ready")
        comb_turned = sem("comb_turned")
        comb_copied = sem("comb_copied")
        block = ctx.enter_context(nc.Block(name="route"))

        def cols(q):
            return bass.ds(q * GT, GT)

        def spread(of_tile):
            return of_tile[:].unsqueeze(2).broadcast_to([P, QT, EXPERTS])

        @block.sync
        def _(sp):
            sp.dma_start(rw[:], router_rev).then_inc(loads, 16)
            sp.dma_start(rb[:], router_b_rev.rearrange("(a n) -> a n", a=1)).then_inc(loads, 16)

            def write_rows(q, b):
                sp.wait_ge(comb_copied, q + 1)
                sp.dma_start(comb_rows[:, cols(q)], comb_t[:, cols(q)]).then_inc(rows_out, 16)

            in_pairs(sp, write_rows, QUADS)

        @block.scalar
        def _(act):
            act.wait_ge(var_eps, 1)
            act.activation(root[:], shifted[:], ACT.Sqrt).then_inc(rooted, 1)

            def copy_x(q, b):
                act.wait_ge(turned, q + 1)
                after(act, x_used, q - 1)
                act.activation(x_s[:, b], ps_x[:, b], ACT.Copy).then_inc(x_copied, 1)
                act.activation(x_hi[:, cols(q)], ps_x[:, b], ACT.Copy).then_inc(hi_ready, 1)

            def copy_comb(q, b):
                if in_range(q, QUADS):
                    hold(act, comb_turned, q + 1)
                    act.activation(comb_t[:, cols(q)], ps_c[0:EXPERTS, b], ACT.Copy).then_inc(comb_copied, 1)

            def step(q, b):
                copy_x(q, b)
                act.wait_ge(d1_ready, q + 1)
                act.activation(e1[:], d1[:], ACT.Exp).then_inc(exp_one, 1)
                copy_comb(q - 1, 1 - b)
                act.wait_ge(d2_ready, q + 1)
                act.activation(e2[:], d2[:], ACT.Exp, scale=-1.0).then_inc(exp_two, 1)

            in_pairs(act, step, QUADS)
            copy_comb(QUADS - 1, 1)

        @block.gpsimd
        def _(pool):
            def step(q, b):
                pool.wait_ge(hi_ready, q + 1)
                pool.tensor_tensor(x_lo[:, cols(q)], x_s[:, b], x_hi[:, cols(q)].bitcast(F32), ALU.subtract
                                   ).then_inc(x_used, 1)

            in_pairs(pool, step, QUADS)

        @block.vector
        def _(dve):
            dve.tensor_scalar(shifted[:], mv[:, :, 1], LN_EPS, None, ALU.add).then_inc(var_eps, 1)
            dve.wait_ge(rooted, 1)
            dve.reciprocal(rstd[:], root[:]).then_inc(rstd_ready, 1)
            dve.wait_ge(rstd_ready, 1)

            def norm(q, b):
                if in_range(q, QUADS):
                    after(dve, turned, q - 1)
                    for k in range(QT):
                        t = q * QT + k
                        last = dve.tensor_scalar(xn[:, b, k, :], h[:, t, :], mv[:, t, 0:1], rstd[:, bass.ds(t, 1)],
                                                 ALU.subtract, ALU.mult)
                    last.then_inc(normed, 1)

            def probabilities(q, b):
                of_quad = ps_l[:, b, 0:QT * EXPERTS].rearrange("p (k e) -> p k e", k=QT)
                link = chained(dve, sum_step, q * 3)
                dve.wait_ge(logits, q + 1)
                dve.tensor_reduce(neg_max[:], of_quad, AX.X, ALU.max, negate=True).then_inc(max_ready, 1)
                hold(dve, max_ready, q + 1)
                dve.tensor_tensor(d1[:], of_quad, spread(neg_max), ALU.add).then_inc(d1_ready, 1)
                norm(q + 1, 1 - b)
                dve.wait_ge(exp_one, q + 1)
                link(dve.tensor_reduce(neg_s1[:], e1[:], AX.X, ALU.add, negate=True))
                link(dve.reciprocal(neg_r1[:], neg_s1[:]))
                link(dve.tensor_tensor(neg_p[:], e1[:], spread(neg_r1), ALU.mult))
                dve.tensor_tensor(d2[:], neg_p[:], spread(neg_r1), ALU.subtract).then_inc(d2_ready, 1)

            def choose(q, b):
                link = chained(dve, top_step, q * (2 * ROUNDS + 1 + 3))
                source = neg_p
                for taken in range(0, DROPPED, 8):
                    for k in range(QT):
                        last = dve.max(low[:, k, :], source[:, k, :])
                    link(last)
                    if DROPPED - taken < 8:
                        link(dve.memset(low[:, :, DROPPED - taken:8], MARK))
                    for k in range(QT):
                        last = dve.match_replace(left[:, k, :], low[:, k, :], source[:, k, :], MARK)
                    link(last)
                    source = left
                dve.wait_ge(exp_two, q + 1)
                link(dve.scalar_tensor_tensor(out=top[:], in0=left[:], scalar=MARK, in1=e2[:], op0=ALU.is_gt,
                                              op1=ALU.mult))
                link(dve.tensor_reduce(s2[:], top[:], AX.X, ALU.add))
                link(dve.reciprocal(r2[:], s2[:]))
                after(dve, comb_turned, q - 1)
                dve.tensor_tensor(comb[:, b], top[:], spread(r2), ALU.mult).then_inc(comb_ready, 1)

            def step(q, b):
                if not isinstance(q, int) or q > 0:
                    hold(dve, comb_ready, q)
                probabilities(q, b)
                choose(q, b)

            ROUNDS = -(-DROPPED // 8)
            norm(0, 0)
            in_pairs(dve, step, QUADS - 2)
            for q in (QUADS - 2, QUADS - 1):
                step(q, q % 2)

        @block.tensor
        def _(pe):
            pe.wait_ge(loads, 32)

            def turn_x(q, b):
                pe.wait_ge(normed, q + 1)
                after(pe, hi_ready, q - 1)
                for k in range(QT):
                    last = pe.transpose(ps_x[:, b, k * P:(k + 1) * P], xn[:, b, k, :], ident[:])
                last.then_inc(turned, 1)

            def logit(q, b):
                pe.wait_ge(x_copied, q + 1)
                after(pe, d1_ready, q - 1)
                for k in range(QT):
                    of_tile = ps_l[:, b, k * EXPERTS:(k + 1) * EXPERTS]
                    pe.matmul(of_tile, x_s[:, b, k * P:(k + 1) * P], rw[:], start=True, stop=False)
                    last = pe.matmul(of_tile, ones_row[:], rb[:], start=False, stop=True)
                last.then_inc(logits, 1)

            def turn_comb(q, b):
                if in_range(q, QUADS):
                    after(pe, comb_copied, q - 1)
                    hold(pe, comb_ready, q + 1)
                    for k in range(QT):
                        last = pe.transpose(ps_c[0:EXPERTS, b, k * P:(k + 1) * P], comb[:, b, k, :], ident[:])
                    last.then_inc(comb_turned, 1)

            def step(q, r):
                turn_x(q, r % 2)
                logit(q, r % 2)
                turn_comb(q - 1, (r - 1) % 2)

            in_pairs(pe, step, QUADS, 4)
            turn_comb(QUADS - 1, 1)


def experts(nc, h, ident, x_hi, x_lo, comb_t, comb_rows, rows_out, w1, b1, w2, b2_rev, out):
    LAG = 4
    RING = LAG
    STEPS = GROUPS * EXPERTS
    BODY = GROUPS * WRING
    ROUNDS = EXPERTS // WRING
    HC = HIDDEN // P
    GTILES = GT // P
    with ExitStack() as ctx:
        def sb(name, shape, dt=F32):
            return ctx.enter_context(nc.sbuf_tensor(name, shape, dt))

        def sem(name):
            return ctx.enter_context(nc.semaphore(name))

        w_raw = sb("w_raw", [P, WRING, 2, HIDDEN])
        w_hi = sb("w_hi", [P, WRING, 2, HIDDEN], F32R)
        w_lo = sb("w_lo", [P, WRING, 2, HIDDEN], F32R)
        c_row = sb("c_row", [P, WRING, SWEEP_TOKENS])
        b1_rows = sb("b1_rows", [EXPERTS, HIDDEN])
        b1_t = sb("b1_t", [P, HC, EXPERTS])
        b2_rows = sb("b2_rows", [EXPERTS, DIM])
        act_out = sb("act_out", [P, 2, HC, GT])
        scaled = sb("scaled", [P, RING, HC, GT])
        s_hi = sb("s_hi", [P, RING, HC, GT], F32R)
        s_lo = sb("s_lo", [P, RING, HC, GT], F32R)
        y_t = sb("y_t", [P, GROUPS, GT])
        ps_h = ctx.enter_context(nc.psum_tensor("f_ps_h", [P, 2, HC, GT], F32))
        ps_y = ctx.enter_context(nc.psum_tensor("f_ps_y", [P, GROUPS, GT], F32))
        b1_in = sem("b1_in")
        b2_in = sem("b2_in")
        w_in = [sem(f"w_in{k}") for k in range(WRING)]
        row_in = [sem(f"row_in{k}") for k in range(WRING)]
        b1_turned = sem("b1_turned")
        hi_copied = sem("hi_copied")
        w_split = sem("w_split")
        hidden = sem("hidden")
        gelu_done = sem("gelu_done")
        scaled_ready = sem("scaled_ready")
        hi_ready = sem("s_hi_ready")
        lo_ready = sem("s_lo_ready")
        summed = sem("summed")
        y_copied = sem("y_copied")
        y_turned = sem("y_turned")
        y_added = sem("f_y_added")
        stored = sem("stored")
        block = ctx.enter_context(nc.Block(name="experts"))
        y_tokens = out.rearrange("b s d -> (b s) d").rearrange("(w t p) d -> w p t d", w=SWEEPS, p=P)

        @block.sync
        def _(sp):
            def load_weights(e, r):
                sp.dma_start(w_raw[:, r, 0, :], w1[e]).then_inc(w_in[r], 16)
                sp.dma_start(w_raw[:, r, 1, :].rearrange("p (c n) -> p c n", c=HC),
                             w2[e].rearrange("(c p) n -> p c n", p=P)).then_inc(w_in[r], 16)

            def load_row(w, e, r):
                row = comb_rows[bass.ds(EXPERTS - 1 - e, 1), bass.ds(w * SWEEP_TOKENS, SWEEP_TOKENS)]
                sp.dma_start(c_row[:, r, :], row.broadcast_to([P, SWEEP_TOKENS])).then_inc(row_in[r], 16)

            def load(w, e, r):
                hold(sp, w_split, w * EXPERTS + e - (WRING - 1))
                load_weights(e, r)
                hold(sp, scaled_ready, (w * EXPERTS + e) * GROUPS - (WRING - 1) * GROUPS)
                load_row(w, e, r)

            def store(w):
                sp.wait_ge(y_added, w + 2)
                tiles = slice(w * GROUPS * GTILES, (w + 1) * GROUPS * GTILES)
                sp.dma_start(y_tokens[w], h[:, tiles, :]).then_inc(stored, 16)

            sp.dma_start(b1_rows[:], b1).then_inc(b1_in, 16)
            for r in range(WRING):
                load_weights(r, r)
            sp.dma_start(b2_rows[:], b2_rev).then_inc(b2_in, 16)
            sp.wait_ge(rows_out, 16 * (TOKENS // GT))
            for r in range(WRING):
                load_row(0, r, r)
            with sp.Fori(1, ROUNDS) as i:
                for r in range(WRING):
                    load(0, i * WRING + r, r)
            for w in range(1, SWEEPS):
                with sp.Fori(0, ROUNDS) as i:
                    for r in range(WRING):
                        load(w, i * WRING + r, r)
                store(w - 1)
            store(SWEEPS - 1)
            sp.wait_ge(stored, 16 * SWEEPS)

        @block.gpsimd
        def _(pool):
            def split(e, r, loaded, reuse):
                pool.wait_ge(w_in[r], loaded)
                if reuse:
                    hold(pool, summed, e * GROUPS - (WRING - 1) * GROUPS)
                pool.tensor_copy(w_hi[:, r], w_raw[:, r]).then_inc(hi_copied, 1)
                pool.wait_ge(hi_copied, e + 1)
                pool.tensor_tensor(w_lo[:, r], w_raw[:, r], w_hi[:, r].bitcast(F32), ALU.subtract
                                   ).then_inc(w_split, 1)

            for r in range(WRING):
                split(r, r, 32, False)
            with pool.Fori(1, SWEEPS * ROUNDS) as i:
                for r in range(WRING):
                    split(i * WRING + r, r, i * 32 + 32, True)

        @block.scalar
        def _(act):
            def gelu(S, e, r):
                hold(act, hidden, S + 1)
                for c in range(HC):
                    last = act.activation(act_out[:, r % 2, c, :], ps_h[:, r % 2, c, :], ACT.Gelu,
                                          bias=b1_t[:, c, bass.ds(e, 1)])
                last.then_inc(gelu_done, 1)

            def high(S, r, reuse):
                act.wait_ge(scaled_ready, S + 1)
                if reuse:
                    act.wait_ge(summed, S - (LAG - 1))
                act.activation(s_hi[:, r % RING], scaled[:, r % RING], ACT.Copy).then_inc(hi_ready, 1)

            act.wait_ge(y_added, 1)
            with act.Fori(0, SWEEPS) as w:
                start = w * STEPS
                for r in range(BODY):
                    gelu(start + r, r // GROUPS, r)
                    if r:
                        high(start + (r - 1), r - 1, r - 1 >= LAG)
                with act.Fori(1, STEPS // BODY) as i:
                    for r in range(BODY):
                        gelu(start + i * BODY + r, i * WRING + r // GROUPS, r)
                        high(start + i * BODY + (r - 1), (r - 1) % BODY, True)
                high(start + (STEPS - 1), BODY - 1, True)
                act.wait_ge(summed, start + STEPS)
                for g in range(GROUPS):
                    act.activation(y_t[:, g, :], ps_y[:, g, :], ACT.Copy).then_inc(y_copied, 1)

        @block.vector
        def _(dve):
            dve.wait_ge(b1_turned, 1)
            dve.tensor_copy(b1_t[:], ps_h[:, 0, 0, 0:HC * EXPERTS].rearrange("p (c e) -> p c e", c=HC)
                            ).then_inc(y_added, 1)

            def scale(S, rows_loaded, r, reuse):
                g, k = r % GROUPS, r // GROUPS
                if g == 0:
                    dve.wait_ge(row_in[k], rows_loaded)
                if reuse:
                    dve.wait_ge(lo_ready, S - (RING - 1))
                dve.wait_ge(gelu_done, S + 1)
                dve.tensor_tensor(scaled[:, r % RING], act_out[:, r % 2],
                                  c_row[:, k, g * GT:(g + 1) * GT].unsqueeze(1).broadcast_to([P, HC, GT]), ALU.mult
                                  ).then_inc(scaled_ready, 1)

            def low(S, r):
                dve.wait_ge(hi_ready, S + 1)
                dve.tensor_tensor(s_lo[:, r % RING], scaled[:, r % RING], s_hi[:, r % RING].bitcast(F32), ALU.subtract
                                  ).then_inc(lo_ready, 1)

            with dve.Fori(0, SWEEPS) as w:
                start = w * STEPS
                rows = w * (16 * ROUNDS)
                for r in range(BODY):
                    scale(start + r, rows + 16, r, r >= RING)
                    if r:
                        low(start + (r - 1), r - 1)
                with dve.Fori(1, STEPS // BODY) as i:
                    for r in range(BODY):
                        scale(start + i * BODY + r, rows + i * 16 + 16, r, True)
                        low(start + i * BODY + (r - 1), (r - 1) % BODY)
                low(start + (STEPS - 1), BODY - 1)
                for g in range(GROUPS):
                    hold(dve, y_turned, w * GROUPS + (g + 1))
                    tiles = bass.ds(w * (GROUPS * GTILES) + g * GTILES, GTILES)
                    last = dve.tensor_tensor(h[:, tiles, :], h[:, tiles, :],
                                             ps_h[:, g // HC, g % HC, :].rearrange("p (t d) -> p t d", d=DIM),
                                             ALU.add)
                last.then_inc(y_added, 1)

        @block.tensor
        def _(pe):
            pe.wait_ge(b1_in, 16)
            for c in range(HC):
                last = pe.transpose(ps_h[:, 0, 0, c * EXPERTS:(c + 1) * EXPERTS], b1_rows[:, c * P:(c + 1) * P],
                                    ident[0:EXPERTS, 0:EXPERTS])
            last.then_inc(b1_turned, 1)
            pe.wait_ge(b2_in, 16)

            def tokens(w, g):
                return bass.ds(w * SWEEP_TOKENS + g * GT, GT)

            def first(S, e, w, r, reuse):
                g, k = r % GROUPS, r // GROUPS
                if g == 0:
                    pe.wait_ge(w_split, e + 1)
                if reuse:
                    pe.wait_ge(gelu_done, S - 1)
                for c in range(HC):
                    at = slice(c * P, (c + 1) * P)
                    to = ps_h[:, r % 2, c, :]
                    pe.matmul(to, w_hi[:, k, 0, at], x_hi[:, tokens(w, g)], start=True, stop=False)
                    pe.matmul(to, w_hi[:, k, 0, at], x_lo[:, tokens(w, g)], start=False, stop=False)
                    last = pe.matmul(to, w_lo[:, k, 0, at], x_hi[:, tokens(w, g)], start=False, stop=True)
                last.then_inc(hidden, 1)

            def second(S, r, last_step):
                g, k, slot = r % GROUPS, r // GROUPS, r % RING
                pe.wait_ge(lo_ready, S + 1)
                for c in range(HC):
                    at = slice(c * P, (c + 1) * P)
                    pe.matmul(ps_y[:, g, :], w_hi[:, k, 1, at], s_hi[:, slot, c, :], start=False, stop=False)
                    pe.matmul(ps_y[:, g, :], w_hi[:, k, 1, at], s_lo[:, slot, c, :], start=False, stop=False)
                    last = pe.matmul(ps_y[:, g, :], w_lo[:, k, 1, at], s_hi[:, slot, c, :], start=False,
                                     stop=last_step and c == HC - 1)
                last.then_inc(summed, 1)

            with pe.Fori(0, SWEEPS) as w:
                start = w * STEPS
                pe.wait_ge(y_added, w + 1)
                for g in range(GROUPS):
                    pe.matmul(ps_y[:, g, :], b2_rows[:], comb_t[:, tokens(w, g)], start=True, stop=False)
                for r in range(BODY):
                    if r >= LAG:
                        second(start + (r - LAG), r - LAG, False)
                    first(start + r, w * EXPERTS + r // GROUPS, w, r, r >= 2)
                with pe.Fori(1, STEPS // BODY) as i:
                    for r in range(BODY):
                        at = start + i * BODY
                        second(at + (r - LAG), (r - LAG) % BODY, False)
                        first(at + r, w * EXPERTS + i * WRING + r // GROUPS, w, r, True)
                for r in range(LAG):
                    second(start + (STEPS - LAG + r), BODY - LAG + r, True)
                for g in range(GROUPS):
                    pe.wait_ge(y_copied, w * GROUPS + (g + 1))
                    for t in range(GTILES):
                        last = pe.transpose(ps_h[:, g // HC, g % HC, t * P:(t + 1) * P],
                                            y_t[:, g, t * P:(t + 1) * P], ident[:])
                    last.then_inc(y_turned, 1)


_OUTS = [((BATCH, SEQ, DIM), "float32")]


def kernel(**inputs):
    import concourse.bacc as _bacc
    from concourse.bass_utils import run_bass_kernel_spmd as _run

    half = DR // 2
    inv_freq = 1.0 / 500000.0 ** (np.arange(0, DR, 2, dtype=np.float32) / DR)
    freqs = np.outer(np.arange(SEQ, dtype=np.float32), inv_freq)
    cos, sin = np.cos(freqs).astype(np.float32), np.sin(freqs).astype(np.float32)
    laid = {
        "tok": inputs["x"],
        "pos": inputs["fside_BS_position"],
        "emb": inputs["L0_tok_embeddings"],
        "centers": inputs["L0_tok_centers"],
        "logvar": inputs["L0_tok_log_variances"],
    }
    for name in ("W_DQ", "W_UQ", "W_QR", "W_DKV", "W_UK", "W_UV", "W_KR", "W_VR", "W_O", "q_ln_w", "kv_ln_w",
                 "q_head_norm_w", "k_head_norm_w"):
        laid[name.lower()] = inputs["L0_attn_" + name]
    laid["w1"] = inputs["L0_ffn_w1"]
    laid["b1"] = inputs["L0_ffn_b1"]
    laid["w2"] = inputs["L0_ffn_w2"]
    laid["b2_rev"] = np.asarray(inputs["L0_ffn_b2"])[::-1]
    laid["router_rev"] = np.asarray(inputs["L0_ffn_router_w"])[:, ::-1]
    laid["router_b_rev"] = np.asarray(inputs["L0_ffn_router_b"])[::-1]
    laid["rope_cos"] = cos
    laid["rope_sin"] = np.stack([-sin, sin])

    nc = _bacc.Bacc("TRN2", target_bir_lowering=False, num_devices=1)
    arrays, args = {}, []
    for name, value in laid.items():
        a = np.ascontiguousarray(value)
        arrays[f"in_{name}"] = a
        args.append(nc.dram_tensor(f"in_{name}", a.shape, mybir.dt.from_np(a.dtype), kind="ExternalInput").ap())
    out = nc.dram_tensor("out_0", _OUTS[0][0], F32, kind="ExternalOutput").ap()
    lm_tower(nc, *args, out)
    r = _run(nc, [arrays], core_ids=[0])
    return r.results[0]["out_0"]
```

```python
from contextlib import ExitStack

import numpy as np

import concourse.bass as bass
from concourse import mybir

F32 = mybir.dt.float32
F32R = mybir.dt.float32r
I32 = mybir.dt.int32
ACT = mybir.ActivationFunctionType
ALU = mybir.AluOpType
AX = mybir.AxisListType

P = 128
BATCH, SEQ, DIM = 16, 256, 128
TOKENS = BATCH * SEQ
TILES = TOKENS // P
CENTERS = 3072
CHUNKS = CENTERS // P
TOPK = 10
CHR_JUMP = 2.0
HEADS, KV, HD, DN, DR = 8, 2, 64, 32, 32
GROUP = HEADS // KV
LQ, LKV = 64, 128
EXPERTS, HIDDEN, ACTIVE = 64, 256, 42
DROPPED = EXPERTS - ACTIVE
RMS_EPS = 1e-6
LN_EPS = 1e-5
MARK = -3.0e38
MASKED = -1.0e30
GT = 512
GROUPS = 4
SWEEP_TOKENS = GROUPS * GT
SWEEPS = TOKENS // SWEEP_TOKENS
WRING = 4
SPLIT_EARLY = 2
PARTS = 2
CLASSES = 4
LOADS_OF_ATTENTION = 7 + 6 * KV + 4
C_Q, C_KV, C_KR, C_COLS = 0, LQ, LQ + LKV, LQ + LKV + KV * DR + DIM
C_RES = C_COLS - DIM
NH = HEADS + KV


def after(eng, sem, value):
    if not isinstance(value, int) or value > 0:
        eng.wait_ge(sem, value)


def hold(eng, sem, value):
    eng.wait_ge(sem, value)
    if not isinstance(value, int):
        eng.nop(nofuse=True)


def chain(eng, sem, done):
    count = [done]

    def mark(instruction):
        instruction.then_inc(sem, 1)
        count[0] = count[0] + 1

    def settle():
        hold(eng, sem, count[0])

    def link(instruction):
        mark(instruction)
        settle()

    return mark, settle, link


def chained(eng, sem, done):
    return chain(eng, sem, done)[2]


def repeat(eng, step, n, body=2):
    for t in range(body):
        step(t, t)
    with eng.Fori(1, n // body) as i:
        for b in range(body):
            step(i * body + b, b)


def in_range(t, n):
    return not isinstance(t, int) or 0 <= t < n


def lm_tower(nc, tok, pos, emb, centers, logvar, w_dq, w_uq, w_qr, w_dkv, w_uk, w_uv, w_kr, w_vr, w_o,
             q_ln, kv_ln, q_hn, k_hn, w1, b1, w2, b2_rev, router_rev, router_b_rev, rope_cos, rope_sin, out):
    comb_rows = nc.dram_tensor("comb_rows", [EXPERTS, TOKENS], F32, kind="Internal").ap()
    with ExitStack() as whole:
        def keep(name, shape, dt=F32):
            return whole.enter_context(nc.sbuf_tensor(name, shape, dt))

        h = keep("h", [P, TILES, DIM])
        ident = keep("ident", [P, P])
        ones_row = keep("ones_row", [1, P])
        mv = keep("mv", [P, TILES, 2])
        rstd = keep("rstd", [P, TILES])
        with ExitStack() as attention:
            def part(name, shape, dt=F32):
                return attention.enter_context(nc.sbuf_tensor(name, shape, dt))

            w = {
                "latent": part("w_latent", [P, C_COLS]),
                "q": part("w_q", [LQ, GROUP, KV, HD]),
                "kv": part("w_kv", [P, KV * DN + KV * HD]),
                "out": part("w_out", [P, GROUP, DIM]),
                "q_in": part("wq_in", [LQ, GROUP, KV, HD]),
                "kv_in": part("wkv_in", [P, KV * DN + KV * HD]),
                "vr_in": part("vr_in", [P, GROUP, KV, HD]),
                "qln": part("qln", [LQ, 1]),
                "kvln": part("kvln", [P, 1]),
                "hn": part("hn", [P, 2]),
                "k_scale": part("k_scale", [P, 1]),
                "cos": part("cos2", [P, SEQ // P, DR]),
                "sin": part("sin2", [P, SEQ // P, DR]),
            }
            causal = part("causal", [P, P])
            w_loaded = attention.enter_context(nc.semaphore("w_loaded"))
            with ExitStack() as tower:
                flag = tower.enter_context(nc.sbuf_tensor("flag", [1, 1], I32))
                e = embed_buffers(nc, tower)
                npos = tower.enter_context(nc.sbuf_tensor("npos", [P, TILES], F32))

                def load_weights(sp):
                    return load_attention(sp, w, w_loaded, w_dq, w_uq, w_qr, w_dkv, w_uk, w_uv, w_kr, w_vr, w_o,
                                          q_ln, kv_ln, q_hn, k_hn, rope_cos, rope_sin)

                setup(nc, tok, pos, centers, logvar, emb, e, ident, ones_row, causal, npos)
                embed(nc, e, h, ident, npos, mv, flag, False, load_weights)
                embed(nc, e, h, ident, npos, mv, flag, True, None)
            with ExitStack() as mid:
                qk = mid.enter_context(nc.sbuf_tensor("qk", [P, TILES, NH, HD], F32))
                v_all = mid.enter_context(nc.sbuf_tensor("v_all", [P, TILES, KV * HD], F32))
                ss = mid.enter_context(nc.sbuf_tensor("ss", [P, TILES, 2], F32))
                hs = mid.enter_context(nc.sbuf_tensor("hs", [P, TILES, NH], F32))
                with ExitStack() as first:
                    c_raw = first.enter_context(nc.sbuf_tensor("c_raw", [P, TILES, C_COLS], F32))
                    project(nc, h, ident, w, w_loaded, mv, rstd, c_raw, ss)
                    heads(nc, ident, w["q"], w["kv"], w["cos"], w["sin"], c_raw, ss, qk, v_all, hs)
                attend(nc, h, ident, causal, w["out"], w["k_scale"], qk, v_all, hs, mv)
        with ExitStack() as last:
            x_hi = last.enter_context(nc.sbuf_tensor("x_hi", [P, TOKENS], F32R))
            x_lo = last.enter_context(nc.sbuf_tensor("x_lo", [P, TOKENS], F32R))
            comb_t = last.enter_context(nc.sbuf_tensor("comb_t", [EXPERTS, TOKENS], F32))
            f = expert_buffers(nc, last)
            loader = ExpertLoads(f, comb_rows, w1, b1, w2, b2_rev)
            route(nc, h, ident, ones_row, router_rev, router_b_rev, mv, rstd, x_hi, x_lo, comb_t, comb_rows, f, loader)
            experts(nc, h, ident, x_hi, x_lo, comb_t, f, loader, out)


def load_attention(sp, w, loaded, w_dq, w_uq, w_qr, w_dkv, w_uk, w_uv, w_kr, w_vr, w_o, q_ln, kv_ln, q_hn, k_hn,
                   rope_cos, rope_sin):
    def load(to, source):
        sp.dma_start(to, source).then_inc(loaded, 16)
        issued.append(to)

    issued = []
    half = DR // 2
    load(w["latent"][:, C_Q:C_KV], w_dq)
    load(w["latent"][:, C_KV:C_KR], w_dkv)
    load(w["latent"][:, C_KR:C_RES], w_kr)
    load(w["kv_in"][:, 0:KV * DN], w_uk)
    load(w["kv_in"][:, KV * DN:], w_uv)
    load(w["qln"][:], q_ln.rearrange("(p a) -> p a", a=1))
    load(w["kvln"][:], kv_ln.rearrange("(p a) -> p a", a=1))
    for g in range(KV):
        heads_of = slice(g * GROUP, (g + 1) * GROUP)
        cols = slice(heads_of.start * DN, heads_of.stop * DN)
        wide = slice(heads_of.start * HD, heads_of.stop * HD)
        rows = slice(g * HD, (g + 1) * HD)
        load(w["vr_in"][:, :, g, :], w_vr[:, wide].rearrange("k (j d) -> k j d", d=HD))
        load(w["out"][rows, :, :], w_o[wide, :].rearrange("(j d) n -> d j n", d=HD))
        load(w["q_in"][:, :, g, 0:DN], w_uq[:, cols].rearrange("k (j n) -> k j n", n=DN))
        load(w["q_in"][:, :, g, DN:HD], w_qr[:, cols].rearrange("k (j n) -> k j n", n=DR))
        load(w["hn"][rows, 0:1], q_hn.rearrange("(p a) -> p a", a=1))
        load(w["hn"][rows, 1:2], k_hn.rearrange("(p a) -> p a", a=1))
    for c in range(2):
        at = slice(c * half, (c + 1) * half)
        load(w["cos"][:, :, at], rope_cos.rearrange("(t p) d -> p t d", p=P))
        load(w["sin"][:, :, at], rope_sin[c].rearrange("(t p) d -> p t d", p=P))
    assert len(issued) == LOADS_OF_ATTENTION


def embed_buffers(nc, ctx):
    def sb(name, shape):
        return ctx.enter_context(nc.sbuf_tensor(name, shape, F32))

    return {
        "cent": sb("cent", [P, CENTERS]),
        "neg_prec": sb("neg_prec", [P, CENTERS]),
        "table": sb("table", [P, CHUNKS, DIM]),
        "z": sb("z", [P, 4, CENTERS]),
        "gauss": sb("gauss", [P, 4, CENTERS]),
        "gauss_t": sb("gauss_t", [P, PARTS, CHUNKS // PARTS, P]),
        "cent_in": ctx.enter_context(nc.semaphore("cent_in")),
        "logvar_in": ctx.enter_context(nc.semaphore("logvar_in")),
        "table_in": ctx.enter_context(nc.semaphore("table_in")),
    }


def setup(nc, tok, pos, centers, logvar, emb, e, ident, ones_row, causal, npos):
    with ExitStack() as ctx:
        def sb(name, shape, dt=F32):
            return ctx.enter_context(nc.sbuf_tensor(name, shape, dt))

        def sem(name):
            return ctx.enter_context(nc.semaphore(name))

        tok_rows = sb("tok_rows", [TILES, P], I32)
        pos_rows = sb("pos_rows", [TILES, P])
        tok_f = sb("tok_f", [TILES, P])
        abs_rows = sb("abs_rows", [TILES, P])
        ps_pos = ctx.enter_context(nc.psum_tensor("ps_pos", [P, 512], F32))
        rows_in = sem("rows_in")
        zeroed = sem("zeroed")
        masks = sem("masks")
        posf = sem("posf")
        abs_ready = sem("abs_ready")
        pos_t = sem("pos_t")
        block = ctx.enter_context(nc.Block(name="setup"))

        @block.sync
        def _(sp):
            sp.dma_start(tok_rows[:], tok.rearrange("b (t p) -> (b t) p", p=P)).then_inc(rows_in, 16)
            sp.dma_start(pos_rows[:], pos.rearrange("b (t p) -> (b t) p", p=P)).then_inc(rows_in, 16)
            for to, row, there in ((e["cent"], centers, e["cent_in"]), (e["neg_prec"], logvar, e["logvar_in"])):
                sp.dma_start(to[:], row.rearrange("(a n) -> a n", a=1).broadcast_to([P, CENTERS])).then_inc(there, 16)
            sp.dma_start(e["table"][:], emb.rearrange("(c p) d -> p c d", p=P)).then_inc(e["table_in"], 16)

        @block.gpsimd
        def _(pool):
            pool.memset(ident[:], 0.0).then_inc(zeroed, 1)
            pool.memset(causal[:], 0.0).then_inc(zeroed, 1)
            pool.memset(ones_row[:], 1.0).then_inc(zeroed, 1)
            pool.wait_ge(zeroed, 3)
            pool.affine_select(out=ident[:], in_=ident[:], compare_op=ALU.not_equal, fill=1.0, base=0,
                               pattern=[[-1, P]], channel_multiplier=1).then_inc(masks, 1)
            pool.affine_select(out=causal[:], in_=causal[:], compare_op=ALU.is_ge, fill=MASKED, base=0,
                               pattern=[[-1, P]], channel_multiplier=1).then_inc(masks, 1)

        @block.vector
        def _(dve):
            dve.wait_ge(rows_in, 32)
            dve.tensor_copy(tok_f[:], tok_rows[:]).then_inc(posf, 1)
            dve.wait_ge(posf, 1)
            dve.scalar_tensor_tensor(out=abs_rows[:], in0=tok_f[:], scalar=CHR_JUMP, in1=pos_rows[:],
                                     op0=ALU.mult, op1=ALU.add).then_inc(abs_ready, 1)
            dve.wait_ge(pos_t, 1)
            dve.tensor_scalar(npos[:], ps_pos[:, 0:TILES], -1.0, None, ALU.mult)

        @block.tensor
        def _(pe):
            pe.wait_ge(masks, 2)
            pe.wait_ge(abs_ready, 1)
            pe.transpose(ps_pos[:, 0:TILES], abs_rows[:], ident[0:TILES, 0:TILES]).then_inc(pos_t, 1)


def embed(nc, e, h, ident, npos, mv, flag, general, load_weights):
    RING = 4
    PC = CHUNKS // PARTS
    kind = "g_" if general else "e_"
    cent, neg_prec, table, z, gauss, gauss_t = (e[k] for k in ("cent", "neg_prec", "table", "z", "gauss", "gauss_t"))
    with ExitStack() as ctx:
        def sb(name, shape, dt=F32):
            return ctx.enter_context(nc.sbuf_tensor(kind + name, shape, dt))

        def sem(name):
            return ctx.enter_context(nc.semaphore(kind + name))

        found = sb("found", [P, CLASSES, 8])
        left = sb("left", [P, CLASSES, 8])
        eighth = sb("eighth", [P, 1])
        doubt = sb("doubt", [P, TILES])
        doubts = sb("doubts", [P, 1])
        ones_col = sb("ones_col", [P, 1])
        top_a = sb("top_a", [P, 8])
        top_b = sb("top_b", [P, 8])
        wsum = sb("wsum", [P, RING])
        rsum = sb("rsum", [P, RING])
        stats = sb("stats", [P, 6])
        mvt = sb("mvt", [P, 2])
        ps_t = [ctx.enter_context(nc.psum_tensor(f"{kind}ps_t{k}", [P, PC, P], F32)) for k in range(PARTS)]
        ps_h = ctx.enter_context(nc.psum_tensor(kind + "ps_h", [P, 2, 512], F32))
        prec_exp = sem("prec_exp")
        prec = sem("prec")
        squared = sem("squared")
        z_ready = sem("z_ready")
        gauss_ready = sem("gauss_ready")
        sel_step = sem("sel_step")
        fin_step = sem("fin_step")
        chosen = sem("chosen")
        turned = sem("turned")
        copied = sem("copied")
        product = sem("product")
        tile_done = sem("tile_done")
        flag_step = sem("flag_step")
        flag_summed = sem("flag_summed")
        block = ctx.enter_context(nc.Block(name=kind + "embed"))

        def engine_program(eng, body):
            if not general:
                body(eng)
                return
            with eng.If(eng.value_load(flag[0:1, 0:1], min_val=0, max_val=P) > 0):
                body(eng)

        if load_weights is not None:
            @block.sync
            def _(sp):
                load_weights(sp)

        @block.scalar
        def _(act):
            def square(t, r):
                if in_range(t, TILES):
                    after(act, chosen, t - (RING - 1))
                    act.activation(z[:, r, :], cent[:], ACT.Square, bias=npos[:, bass.ds(t, 1)]).then_inc(squared, 1)

            def exponential(t, r):
                if in_range(t, TILES):
                    act.wait_ge(z_ready, t + 1)
                    act.activation(gauss[:, r, :], z[:, r, :], ACT.Exp).then_inc(gauss_ready, 1)

            def copy_out(t, k):
                if in_range(t, TILES):
                    act.wait_ge(turned, t * PARTS + (k + 1))
                    after(act, product, (t - 1) * PARTS + (k + 1))
                    act.activation(gauss_t[:, k], ps_t[k][:], ACT.Copy).then_inc(copied, 1)

            def step(t, r):
                copy_out(t - 3, 0)
                square(t, r)
                if isinstance(t, int) and t == 0 and not general:
                    act.wait_ge(e["logvar_in"], 16)
                    act.activation(neg_prec[:], neg_prec[:], ACT.Exp, scale=-1.0).then_inc(prec_exp, 1)
                copy_out(t - 3, 1)
                exponential(t - 1, (r - 1) % RING)

            def body(act):
                if not general:
                    act.wait_ge(e["cent_in"], 16)
                repeat(act, step, TILES, RING)
                for t in range(TILES, TILES + 3):
                    step(t, t % RING)

            engine_program(act, body)

        @block.gpsimd
        def _(pool):
            def step(t, r):
                pool.wait_ge(squared, t + 1)
                pool.tensor_tensor(z[:, r, :], z[:, r, :], neg_prec[:], ALU.mult).then_inc(z_ready, 1)

            def body(pool):
                if not general:
                    pool.wait_ge(prec, 1)
                repeat(pool, step, TILES, RING)

            engine_program(pool, body)

        @block.vector
        def _(dve):
            def quick_step(t, r):
                now, old = in_range(t, TILES), in_range(t - 3, TILES)
                mark, settle, _ = chain(dve, sel_step, t * 5)
                done, ro = t - 3, (r - 3) % RING
                mark_old, settle_old, _ = chain(dve, fin_step, done * 4)
                if now:
                    hold(dve, z_ready, t + 1)
                    if not isinstance(t, int) or t > 0:
                        hold(dve, chosen, t)
                    of_class = z[:, r, :].rearrange("p (n c) -> p c n", c=CLASSES)
                    for c in range(CLASSES):
                        last = dve.max(found[:, c, :], of_class[:, c, :])
                    mark(last)
                if old:
                    dve.wait_ge(chosen, done + 1)
                    mark_old(dve.reciprocal(rsum[:, ro:ro + 1], wsum[:, ro:ro + 1]))
                if now:
                    settle()
                    dve.tensor_reduce(eighth[:], found[:, :, 7], AX.X, ALU.max)
                    mark(dve.max(top_a[:], found[:]))
                if old:
                    settle_old()
                    dve.wait_ge(product, (done + 1) * PARTS)
                    mark_old(dve.tensor_scalar(h[:, done, :], ps_h[:, ro % 2, 0:DIM], rsum[:, ro:ro + 1], None,
                                               ALU.mult))
                if now:
                    settle()
                    mark(dve.match_replace(left[:], top_a[:], found[:], MARK))
                if old:
                    settle_old()
                    mark_old(dve.bn_stats(stats[:], h[:, done, :]))
                if now:
                    settle()
                    mark(dve.max(top_b[:], left[:]))
                if old:
                    settle_old()
                    mark_old(dve.bn_aggr(mvt[:], stats[:]))
                if now:
                    settle()
                    mark(dve.tensor_scalar(doubt[:, bass.ds(t, 1)], eighth[:], top_b[:, TOPK - 8:TOPK - 7],
                                           top_b[:, TOPK - 9:TOPK - 8], ALU.max, ALU.is_ge))
                if old:
                    settle_old()
                    dve.tensor_copy(mv[:, done, :], mvt[:]).then_inc(tile_done, 1)
                if now:
                    settle()
                    dve.wait_ge(gauss_ready, t + 1)
                    dve.scalar_tensor_tensor(out=gauss[:, r, :], in0=z[:, r, :], scalar=top_b[:, TOPK - 9:TOPK - 8],
                                             in1=gauss[:, r, :], op0=ALU.is_ge, op1=ALU.mult,
                                             accum_out=wsum[:, r:r + 1]).then_inc(chosen, 1)

            def general_select(t, r):
                link = chained(dve, sel_step, t * 5)
                hold(dve, gauss_ready, t + 1)
                link(dve.max(top_a[:], z[:, r, :]))
                link(dve.match_replace(z[:, r, :], top_a[:], z[:, r, :], MARK))
                link(dve.max(top_b[:], z[:, r, :]))
                link(dve.memset(top_b[:, TOPK - 8:8], MARK))
                link(dve.match_replace(z[:, r, :], top_b[:], z[:, r, :], MARK))
                dve.scalar_tensor_tensor(out=gauss[:, r, :], in0=z[:, r, :], scalar=MARK, in1=gauss[:, r, :],
                                         op0=ALU.is_le, op1=ALU.mult, accum_out=wsum[:, r:r + 1]
                                         ).then_inc(chosen, 1)
                hold(dve, chosen, t + 1)

            def general_step(t, r):
                if in_range(t, TILES):
                    general_select(t, r)
                done, ro = t - 3, (r - 3) % RING
                if in_range(done, TILES):
                    link = chained(dve, fin_step, done * 4)
                    link(dve.reciprocal(rsum[:, ro:ro + 1], wsum[:, ro:ro + 1]))
                    dve.wait_ge(product, (done + 1) * PARTS)
                    link(dve.tensor_scalar(h[:, done, :], ps_h[:, ro % 2, 0:DIM], rsum[:, ro:ro + 1], None, ALU.mult))
                    link(dve.bn_stats(stats[:], h[:, done, :]))
                    link(dve.bn_aggr(mvt[:], stats[:]))
                    dve.tensor_copy(mv[:, done, :], mvt[:]).then_inc(tile_done, 1)

            def step(t, r):
                (general_step if general else quick_step)(t, r)
                if not isinstance(t, int) or t >= 3:
                    hold(dve, tile_done, t - 2)

            def body(dve):
                if not general:
                    dve.memset(ones_col[:], 1.0).then_inc(flag_step, 1)
                    dve.wait_ge(prec_exp, 1)
                    dve.tensor_scalar(neg_prec[:], neg_prec[:], -0.5, None, ALU.mult).then_inc(prec, 1)
                repeat(dve, step, TILES, RING)
                for t in range(TILES, TILES + 3):
                    step(t, t % RING)
                if not general:
                    dve.tensor_reduce(doubts[:], doubt[:], AX.X, ALU.max).then_inc(flag_step, 1)
                    dve.wait_ge(flag_summed, 1)
                    dve.tensor_copy(flag[:], ps_h[0:1, 0, 0:1])

            engine_program(dve, body)

        @block.tensor
        def _(pe):
            def turn(t, r, k):
                if in_range(t, TILES):
                    pe.wait_ge(chosen, t + 1)
                    after(pe, copied, (t - 1) * PARTS + (k + 1))
                    for c in range(PC):
                        at = (k * PC + c) * P
                        last = pe.transpose(ps_t[k][:, c, :], gauss[:, r, at:at + P], ident[:])
                    last.then_inc(turned, 1)

            def multiply(t, b, k):
                if in_range(t, TILES):
                    if k == 0:
                        after(pe, tile_done, t - 1)
                    pe.wait_ge(copied, t * PARTS + (k + 1))
                    for c in range(PC):
                        last = pe.matmul(ps_h[:, b, 0:DIM], gauss_t[:, k, c, :], table[:, k * PC + c, :],
                                         start=(k == 0 and c == 0), stop=(k == PARTS - 1 and c == PC - 1))
                    last.then_inc(product, 1)

            def step(t, r):
                for k in range(PARTS):
                    turn(t, r, k)
                    multiply(t - 1, (r - 1) % 2, k)

            def body(pe):
                if not general:
                    pe.wait_ge(e["table_in"], 16)
                repeat(pe, step, TILES, RING)
                step(TILES, 0)
                if not general:
                    pe.wait_ge(flag_step, 2)
                    pe.wait_ge(tile_done, TILES)
                    pe.matmul(ps_h[0:1, 0, 0:1], doubts[:], ones_col[:], start=True, stop=True
                              ).then_inc(flag_summed, 1)

            engine_program(pe, body)


def project(nc, h, ident, w, w_loaded, mv, rstd, c_raw, ss):
    with ExitStack() as ctx:
        def sb(name, shape, dt=F32):
            return ctx.enter_context(nc.sbuf_tensor(name, shape, dt))

        def sem(name):
            return ctx.enter_context(nc.semaphore(name))

        vr_t = sb("vr_t", [P, GROUP, DIM])
        ps_vr = ctx.enter_context(nc.psum_tensor("ps_vr", [P, GROUP, P], F32))
        ps_m = ctx.enter_context(nc.psum_tensor("ps_m", [P, 512], F32))
        vr_turned = sem("vr_turned")
        vr_copied = sem("vr_copied")
        m_ready = sem("m_ready")
        w_ready = sem("w_ready")
        shifted = sb("p_shifted", [P, TILES])
        root = sb("p_root", [P, TILES])
        XN = 4
        xn = sb("xn", [P, XN, DIM])
        x_t = sb("x_t", [P, 2, P])
        junk = sb("junk", [P, LQ + LKV])
        ps_x = ctx.enter_context(nc.psum_tensor("ps_x", [P, 2, 512], F32))
        ps_c = ctx.enter_context(nc.psum_tensor("ps_c", [P, 2, 512], F32))
        var_eps = sem("var_eps")
        rooted = sem("p_rooted")
        rstd_ready = sem("rstd_ready")
        normed = sem("normed")
        turned = sem("p_turned")
        x_copied = sem("x_copied")
        projected = sem("projected")
        c_copied = sem("c_copied")
        squared = sem("p_squared")
        block = ctx.enter_context(nc.Block(name="project"))

        @block.scalar
        def _(act):
            act.wait_ge(var_eps, 1)
            act.activation(root[:], shifted[:], ACT.Sqrt).then_inc(rooted, 1)

            def copy_latents(t, b):
                if in_range(t, TILES):
                    act.wait_ge(projected, t + 1)
                    act.activation(c_raw[:, t, :], ps_c[:, b, 0:C_COLS], ACT.Copy).then_inc(c_copied, 1)

            def step(t, b):
                act.wait_ge(turned, t + 1)
                act.activation(x_t[:, b, :], ps_x[:, b, 0:P], ACT.Copy).then_inc(x_copied, 1)
                copy_latents(t - 1, 1 - b)

            repeat(act, step, TILES)
            copy_latents(TILES - 1, 1)

        @block.vector
        def _(dve):
            dve.tensor_scalar(shifted[:], mv[:, :, 1], LN_EPS, None, ALU.add).then_inc(var_eps, 1)
            dve.wait_ge(w_loaded, 16 * LOADS_OF_ATTENTION)
            dve.tensor_scalar(w["q"][:], w["q_in"][:], w["qln"][:, 0:1], None, ALU.mult)
            dve.tensor_scalar(w["kv"][:], w["kv_in"][:], w["kvln"][:, 0:1], None, ALU.mult)
            dve.scalar_tensor_tensor(out=w["k_scale"][:], in0=w["hn"][:, 0:1], scalar=float(HD) ** -0.5,
                                     in1=w["hn"][:, 1:2], op0=ALU.mult, op1=ALU.mult)
            dve.wait_ge(vr_turned, 1)
            dve.tensor_copy(vr_t[:], ps_vr[:]).then_inc(vr_copied, 1)
            dve.wait_ge(m_ready, 1)
            dve.tensor_copy(w["latent"][:, C_RES:C_COLS], ps_m[:, 0:DIM]).then_inc(w_ready, 1)
            dve.wait_ge(rooted, 1)
            dve.reciprocal(rstd[:], root[:]).then_inc(rstd_ready, 1)
            dve.wait_ge(rstd_ready, 1)

            def finish(t):
                if in_range(t, TILES):
                    hold(dve, c_copied, t + 1)
                    for k, at in enumerate((slice(C_Q, C_KV), slice(C_KV, C_KR))):
                        dve.scalar_tensor_tensor(out=junk[:, at], in0=c_raw[:, t, at], scalar=1.0,
                                                 in1=c_raw[:, t, at], op0=ALU.mult, op1=ALU.mult,
                                                 accum_out=ss[:, t, k:k + 1])
                    dve.tensor_tensor(h[:, t, :], h[:, t, :], c_raw[:, t, C_RES:C_COLS], ALU.add
                                      ).then_inc(squared, 1)

            def norm(t, r):
                if in_range(t, TILES):
                    after(dve, turned, t - (XN - 1))
                    dve.tensor_scalar(xn[:, r, :], h[:, t, :], mv[:, t, 0:1], rstd[:, bass.ds(t, 1)], ALU.subtract,
                                      ALU.mult).then_inc(normed, 1)

            def step(t, r):
                norm(t, r)
                after(dve, squared, t - 3)
                finish(t - 3)

            repeat(dve, step, TILES, XN)
            for t in range(TILES, TILES + 3):
                step(t, t % XN)

        @block.tensor
        def _(pe):
            pe.wait_ge(w_loaded, 16 * LOADS_OF_ATTENTION)
            for j in range(GROUP):
                last = pe.transpose(ps_vr[:, j, :], w["vr_in"][:, j].rearrange("k g d -> k (g d)"), ident[:])
            last.then_inc(vr_turned, 1)
            pe.wait_ge(vr_copied, 1)
            for j in range(GROUP):
                last = pe.matmul(ps_m[:, 0:DIM], vr_t[:, j, :], w["out"][:, j, :], start=(j == 0),
                                 stop=(j == GROUP - 1))
            last.then_inc(m_ready, 1)
            pe.wait_ge(w_ready, 1)

            def product(t, b):
                pe.wait_ge(x_copied, t + 1)
                after(pe, c_copied, t - 1)
                pe.matmul(ps_c[:, b, 0:C_COLS], x_t[:, b, :], w["latent"][:], start=True, stop=True
                          ).then_inc(projected, 1)

            def step(t, r):
                b = r % 2
                pe.wait_ge(normed, t + 1)
                after(pe, x_copied, t - 1)
                pe.transpose(ps_x[:, b, 0:P], xn[:, r, :], ident[:]).then_inc(turned, 1)
                if not isinstance(t, int) or t >= 1:
                    product(t - 1, 1 - b)

            repeat(pe, step, TILES, XN)
            product(TILES - 1, 1)


def heads(nc, ident, w_q, w_kv, cos2, sin2, c_raw, ss, qk, v_all, hs):
    with ExitStack() as ctx:
        def sb(name, shape, dt=F32):
            return ctx.enter_context(nc.sbuf_tensor(name, shape, dt))

        def sem(name):
            return ctx.enter_context(nc.semaphore(name))

        mean_sq = sb("mean_sq", [P, 2, TILES])
        root = sb("h_root", [P, 2, TILES])
        rms = sb("rms", [P, 2, TILES])
        cn = sb("cn", [P, 2, LQ + LKV])
        c_t = sb("c_t", [P, 2, 2 * P])
        turned_cos = sb("turned_cos", [P, 2, NH, DR])
        turned_sin = sb("turned_sin", [P, 2, NH, DR])
        sq = sb("sq", [P, 2, NH, HD])
        ps_ct = ctx.enter_context(nc.psum_tensor("ps_ct", [P, 2, 512], F32))
        ps_q = ctx.enter_context(nc.psum_tensor("ps_q", [P, 2, 512], F32))
        ps_kv = ctx.enter_context(nc.psum_tensor("ps_kv", [P, 2, 512], F32))
        mean_ready = sem("mean_ready")
        rooted = sem("h_rooted")
        rms_ready = sem("rms_ready")
        normed = sem("c_normed")
        turned = sem("c_turned")
        c_copied = sem("ct_copied")
        projected = sem("qkv_projected")
        out_copied = sem("qkv_copied")
        rotated = sem("rotated")
        roped = sem("roped")
        squares = sem("squares")
        head_sums = sem("head_sums")
        block = ctx.enter_context(nc.Block(name="heads"))
        half = DR // 2

        @block.scalar
        def _(act):
            act.wait_ge(mean_ready, 2)
            act.activation(root[:], mean_sq[:], ACT.Sqrt).then_inc(rooted, 1)

            def copy_out(t, b):
                if in_range(t, TILES):
                    act.wait_ge(projected, t + 1)
                    act.activation(qk[:, t, 0:HEADS, :], ps_q[:, b, :].rearrange("p (n d) -> p n d", d=HD), ACT.Copy)
                    act.activation(qk[:, t, HEADS:NH, 0:DN],
                                   ps_kv[:, b, 0:KV * DN].rearrange("p (n d) -> p n d", d=DN), ACT.Copy)
                    act.activation(v_all[:, t, :], ps_kv[:, b, KV * DN:KV * (DN + HD)], ACT.Copy)
                    act.activation(qk[:, t, HEADS:NH, DN:HD],
                                   c_raw[:, t, C_KR:C_RES].rearrange("p (n d) -> p n d", d=DR), ACT.Copy
                                   ).then_inc(out_copied, 1)

            def norm(t, b):
                if in_range(t, TILES):
                    after(act, turned, t - 1)
                    act.activation(cn[:, b, 0:LQ], c_raw[:, t, C_Q:C_KV], ACT.Copy, scale=rms[:, 0, bass.ds(t, 1)])
                    act.activation(cn[:, b, LQ:], c_raw[:, t, C_KV:C_KR], ACT.Copy, scale=rms[:, 1, bass.ds(t, 1)]
                                   ).then_inc(normed, 1)

            def step(t, r):
                b = r % 2
                if in_range(t, TILES):
                    act.wait_ge(turned, t + 1)
                    act.activation(c_t[0:LQ, b, 0:P], ps_ct[0:LQ, b, 0:P], ACT.Copy)
                    act.activation(c_t[:, b, P:2 * P], ps_ct[:, b, P:2 * P], ACT.Copy).then_inc(c_copied, 1)
                norm(t + 2, b)
                copy_out(t - 1, 1 - b)

            act.wait_ge(rms_ready, 1)
            norm(0, 0)
            norm(1, 1)
            repeat(act, step, TILES - 4, 4)
            for t in range(TILES - 4, TILES + 1):
                step(t, t)

        @block.vector
        def _(dve):
            for k, n in enumerate((LQ, LKV)):
                dve.tensor_scalar(mean_sq[:, k, :], ss[:, :, k], 1.0 / n, RMS_EPS, ALU.mult, ALU.add
                                  ).then_inc(mean_ready, 1)
            dve.wait_ge(rooted, 1)
            dve.reciprocal(rms[:], root[:]).then_inc(rms_ready, 1)
            dve.wait_ge(rms_ready, 1)

            def sum_up(t, b):
                if in_range(t, TILES):
                    dve.wait_ge(squares, t + 1)
                    dve.tensor_reduce(hs[:, t, :], sq[:, b], AX.X, ALU.add).then_inc(head_sums, 1)

            def step(t, r):
                b = r % 2
                x = qk[:, t, :, DN:HD]
                cos = cos2[:, b:b + 1, :].broadcast_to([P, NH, DR])
                sin = sin2[:, b:b + 1, :].broadcast_to([P, NH, DR])
                dve.wait_ge(out_copied, t + 1)
                if not isinstance(t, int) or t >= 2:
                    hold(dve, roped, t - 1)
                dve.tensor_tensor(turned_sin[:, b, :, 0:half], qk[:, t, :, DN + half:HD], sin[:, :, 0:half],
                                  ALU.mult)
                dve.tensor_tensor(turned_sin[:, b, :, half:DR], qk[:, t, :, DN:DN + half], sin[:, :, half:DR],
                                  ALU.mult)
                dve.tensor_tensor(turned_cos[:, b], x, cos, ALU.mult).then_inc(rotated, 1)
                sum_up(t - 2, b)
                hold(dve, rotated, t + 1)
                dve.tensor_tensor(x, turned_cos[:, b], turned_sin[:, b], ALU.add).then_inc(roped, 1)

            repeat(dve, step, TILES, 4)
            sum_up(TILES - 2, 0)
            sum_up(TILES - 1, 1)

        @block.gpsimd
        def _(pool):
            def step(t, b):
                pool.wait_ge(roped, t + 1)
                after(pool, head_sums, t - 1)
                pool.tensor_tensor(sq[:, b], qk[:, t], qk[:, t], ALU.mult).then_inc(squares, 1)

            repeat(pool, step, TILES)

        @block.tensor
        def _(pe):
            def product(t, b):
                pe.wait_ge(c_copied, t + 1)
                after(pe, out_copied, t - 1)
                pe.matmul(ps_q[:, b, :], c_t[0:LQ, b, 0:P], w_q[:].rearrange("k j g d -> k (j g d)"), start=True,
                          stop=True)
                pe.matmul(ps_kv[:, b, 0:KV * (DN + HD)], c_t[:, b, P:2 * P], w_kv[:], start=True, stop=True
                          ).then_inc(projected, 1)

            def step(t, b):
                pe.wait_ge(normed, t + 1)
                if not isinstance(t, int) or t >= 2:
                    hold(pe, c_copied, t - 1)
                pe.transpose(ps_ct[0:LQ, b, 0:P], cn[:, b, 0:LQ], ident[:])
                pe.transpose(ps_ct[:, b, P:2 * P], cn[:, b, LQ:], ident[:]).then_inc(turned, 1)
                if not isinstance(t, int) or t >= 1:
                    product(t - 1, 1 - b)

            repeat(pe, step, TILES)
            product(TILES - 1, 1)


def attend(nc, h, ident, causal, w_out, k_scale, qk, v_all, hs, mv):
    UNITS = 2 * BATCH
    with ExitStack() as ctx:
        def sb(name, shape, dt=F32):
            return ctx.enter_context(nc.sbuf_tensor(name, shape, dt))

        def sem(name):
            return ctx.enter_context(nc.semaphore(name))

        mean_sq = sb("a_mean_sq", [P, TILES, NH])
        rms = sb("a_rms", [P, TILES, NH])
        qkn = sb("qkn", [P, 2, NH, HD])
        v_s = sb("v_s", [P, 2, 2, KV * HD])
        q_t = sb("q_t", [P, 2, GROUP, P])
        k_t = sb("k_t", [P, 2, SEQ])
        sm = sb("sm", [P, 4, HEADS, SEQ])
        neg_max = sb("neg_max", [P, 4, HEADS])
        rowsum = sb("rowsum", [P, 4, HEADS])
        rinv = sb("rinv", [P, 4, HEADS])
        p_t = sb("p_t", [P, 2, HEADS, P])
        o_n = sb("o_n", [P, GROUP, KV, HD])
        o_t = sb("o_t", [P, GROUP, P])
        stats = sb("a_stats", [P, 6])
        mvt = sb("a_mvt", [P, 2])
        ps_s = ctx.enter_context(nc.psum_tensor("ps_s", [P, HEADS, SEQ], F32))
        ps_p = ctx.enter_context(nc.psum_tensor("ps_p", [P, HEADS, P], F32))
        ps_qy = ctx.enter_context(nc.psum_tensor("ps_qy", [P, GROUP, P], F32))
        ps_ko = ctx.enter_context(nc.psum_tensor("ps_ko", [P, GROUP, P], F32))
        mean_ready = sem("a_mean_ready")
        rooted = sem("a_rooted")
        rms_ready = sem("a_rms_ready")
        qk_normed = sem("qk_normed")
        q_turned = sem("q_turned")
        k_turned = sem("k_turned")
        q_copied = sem("q_copied")
        k_copied = sem("k_copied")
        scored = sem("scored")
        masked = sem("masked")
        max_ready = sem("max_ready")
        exp_done = sem("exp_done")
        rinv_ready = sem("rinv_ready")
        v_ready = sem("v_ready")
        o_normed = sem("o_normed")
        o_turned = sem("o_turned")
        p_turned = sem("p_turned")
        p_copied = sem("p_copied")
        mixed = sem("mixed")
        o_copied = sem("o_copied")
        y_ready = sem("y_ready")
        y_added = sem("y_added")
        mv_step = sem("mv_step")
        block = ctx.enter_context(nc.Block(name="attend"))

        def blocks_before(u, r):
            whole = u // 2 if isinstance(u, int) else (u - r % 2) // 2
            return whole * 3 + r % 2

        def all_steps(eng, step):
            repeat(eng, step, UNITS - 4, 4)
            for u in range(UNITS - 4, UNITS + 4):
                step(u, u % 4)

        @block.scalar
        def _(act):
            act.wait_ge(mean_ready, 1)
            act.activation(mean_sq[:], mean_sq[:], ACT.Sqrt).then_inc(rooted, 1)

            def copy_q(u, r):
                if in_range(u, UNITS):
                    act.wait_ge(q_turned, u + 1)
                    act.activation(q_t[:, r % 2], ps_qy[:], ACT.Copy).then_inc(q_copied, 1)

            def copy_k(u, r):
                if in_range(u, UNITS):
                    q, s = r % 2, r // 2 % 2
                    act.wait_ge(k_turned, u + 1)
                    act.activation(k_t[:, s, q * P:(q + 1) * P], ps_ko[:, 0, :], ACT.Copy, scale=k_scale[:, 0:1]
                                   ).then_inc(k_copied, 1)

            def copy_p(u, r, k):
                if in_range(u, UNITS):
                    act.wait_ge(p_turned, blocks_before(u, r) + k + 1)
                    act.activation(p_t[:, k], ps_p[:], ACT.Copy).then_inc(p_copied, 1)

            def copy_o(u):
                if in_range(u, UNITS):
                    act.wait_ge(o_turned, u + 1)
                    act.activation(o_t[:], ps_qy[:], ACT.Copy).then_inc(o_copied, 1)

            def exps(u, r):
                if in_range(u, UNITS):
                    keys = (r % 2 + 1) * P
                    act.wait_ge(max_ready, u + 1)
                    for n in range(HEADS):
                        last = act.activation(sm[:, r, n, 0:keys], sm[:, r, n, 0:keys], ACT.Exp,
                                              bias=neg_max[:, r, n:n + 1], accum_out=rowsum[:, r, n:n + 1])
                    last.then_inc(exp_done, 1)

            def step(u, r):
                copy_p(u - 3, (r - 3) % 4, 0)
                copy_o(u - 4)
                copy_q(u + 1, (r + 1) % 4)
                if (r - 3) % 2:
                    copy_p(u - 3, (r - 3) % 4, 1)
                copy_k(u + 1, (r + 1) % 4)
                exps(u - 1, (r - 1) % 4)

            copy_q(0, 0)
            copy_k(0, 0)
            all_steps(act, step)

        @block.gpsimd
        def _(pool):
            pool.wait_ge(rms_ready, 1)

            def norm_qk(u, r):
                if in_range(u, UNITS):
                    after(pool, k_turned, u - 1)
                    pool.tensor_tensor(qkn[:, r % 2], qk[:, u], rms[:, bass.ds(u, 1), :]
                                       .rearrange("p a n -> p (a n)").unsqueeze(2).broadcast_to([P, NH, HD]),
                                       ALU.mult).then_inc(qk_normed, 1)

            def copy_v(u, r):
                if in_range(u, UNITS):
                    q, s = r % 2, r // 2 % 2
                    after(pool, mixed, u - 2 - q)
                    pool.tensor_copy(v_s[:, s, q, :], v_all[:, u, :]).then_inc(v_ready, 1)

            def step(u, r):
                norm_qk(u, r)
                copy_v(u - 2, (r - 2) % 4)

            repeat(pool, step, UNITS - 4, 4)
            for u in range(UNITS - 4, UNITS + 2):
                step(u, u % 4)

        @block.vector
        def _(dve):
            dve.tensor_scalar(mean_sq[:], hs[:], 1.0 / HD, RMS_EPS, ALU.mult, ALU.add).then_inc(mean_ready, 1)
            dve.wait_ge(rooted, 1)
            dve.reciprocal(rms[:], mean_sq[:]).then_inc(rms_ready, 1)

            def add_y(u):
                if in_range(u, UNITS):
                    dve.wait_ge(y_ready, u + 1)
                    dve.tensor_tensor(h[:, u, :], h[:, u, :], ps_ko[:, 0, :], ALU.add).then_inc(y_added, 1)

            def copy_far(u, r):
                if in_range(u, UNITS) and r % 2:
                    dve.wait_ge(scored, u + 1)
                    dve.tensor_copy(sm[:, r, :, 0:P], ps_s[:, :, 0:P])

            def mask(u, r):
                if in_range(u, UNITS):
                    q = r % 2
                    dve.wait_ge(scored, u + 1)
                    dve.tensor_tensor(sm[:, r, :, q * P:(q + 1) * P], ps_s[:, :, q * P:(q + 1) * P],
                                      causal[:].unsqueeze(1).broadcast_to([P, HEADS, P]), ALU.add
                                      ).then_inc(masked, 1)

            def maximum(u, r):
                if in_range(u, UNITS):
                    dve.wait_ge(masked, u + 1)
                    dve.tensor_reduce(neg_max[:, r, :], sm[:, r, :, 0:(r % 2 + 1) * P], AX.X, ALU.max, negate=True
                                      ).then_inc(max_ready, 1)

            def invert(u, r):
                if in_range(u, UNITS):
                    dve.wait_ge(exp_done, u + 1)
                    dve.reciprocal(rinv[:, r, :], rowsum[:, r, :]).then_inc(rinv_ready, 1)

            def norm_o(u, r):
                if in_range(u, UNITS):
                    hold(dve, rinv_ready, u + 1)
                    dve.wait_ge(mixed, u + 1)
                    dve.tensor_tensor(o_n[:].rearrange("p j g d -> p g j d"),
                                      ps_ko[:].rearrange("p a b -> p (a b)").rearrange("p (g j d) -> p g j d", g=KV,
                                                                                       j=GROUP),
                                      rinv[:, r, :].rearrange("p (g j) -> p g j", g=KV).unsqueeze(3)
                                      .broadcast_to([P, KV, GROUP, HD]), ALU.mult).then_inc(o_normed, 1)

            def statistics(u):
                if in_range(u, UNITS):
                    link = chained(dve, mv_step, u * 3)
                    hold(dve, y_added, u + 1)
                    link(dve.bn_stats(stats[:], h[:, u, :]))
                    link(dve.bn_aggr(mvt[:], stats[:]))
                    link(dve.tensor_copy(mv[:, u, :], mvt[:]))

            def step(u, r):
                new = (r - 1) % 4
                invert(u - 4, r)
                if new % 2:
                    copy_far(u - 1, new)
                    norm_o(u - 4, r)
                    mask(u - 1, new)
                else:
                    mask(u - 1, new)
                    norm_o(u - 4, r)
                maximum(u - 1, new)
                add_y(u - 4)
                statistics(u - 4)

            all_steps(dve, step)

        @block.tensor
        def _(pe):
            def project_out(u):
                if in_range(u, UNITS):
                    pe.wait_ge(o_copied, u + 1)
                    for j in range(GROUP):
                        last = pe.matmul(ps_ko[:, 0, :], o_t[:, j, :], w_out[:, j, :], start=(j == 0),
                                         stop=(j == GROUP - 1))
                    last.then_inc(y_ready, 1)

            def turn_p(u, r, k):
                if in_range(u, UNITS):
                    if k == 0:
                        pe.wait_ge(exp_done, u + 1)
                    after(pe, p_copied, blocks_before(u, r) + k)
                    for n in range(HEADS):
                        last = pe.transpose(ps_p[:, n, :], sm[:, r, n, k * P:(k + 1) * P], ident[:])
                    last.then_inc(p_turned, 1)

            def turn_q(u, r):
                if in_range(u, UNITS):
                    pe.wait_ge(qk_normed, u + 1)
                    if isinstance(u, int):
                        after(pe, q_copied, u)
                    for j in range(GROUP):
                        last = pe.transpose(ps_qy[:, j, :], qkn[:, r % 2, KV * j:KV * (j + 1), :]
                                            .rearrange("p n d -> p (n d)"), ident[:])
                    last.then_inc(q_turned, 1)

            def turn_k(u, r):
                if in_range(u, UNITS):
                    if isinstance(u, int):
                        after(pe, k_copied, u)
                    after(pe, y_added, u - 4)
                    pe.transpose(ps_ko[:, 0, :], qkn[:, r % 2, HEADS:NH, :].rearrange("p n d -> p (n d)"), ident[:]
                                 ).then_inc(k_turned, 1)

            def mix(u, r, turning):
                if in_range(u, UNITS):
                    q, s = r % 2, r // 2 % 2
                    if turning:
                        pe.wait_ge(k_copied, u + 5)
                    else:
                        pe.wait_ge(y_added, u)
                    pe.wait_ge(v_ready, u + 1)
                    pe.wait_ge(p_copied, blocks_before(u, r) + q + 1)
                    for n in range(HEADS):
                        at = slice(n // GROUP * HD, (n // GROUP + 1) * HD)
                        for k in range(q + 1):
                            last = pe.matmul(ps_o[:, n, :], p_t[:, k, n, :], v_s[:, s, k, at], start=(k == 0),
                                             stop=(k == q))
                    last.then_inc(mixed, 1)

            def score(u, r, banks):
                if in_range(u, UNITS):
                    q, s = r % 2, r // 2 % 2
                    if 0 in banks:
                        pe.wait_ge(q_copied, u + 1)
                        pe.wait_ge(k_copied, u + 1)
                        after(pe, masked, u)
                    for n in (n for bank in banks for n in (2 * bank, 2 * bank + 1)):
                        at = slice(n // GROUP * HD, (n // GROUP + 1) * HD)
                        last = pe.matmul(ps_s[:, n, 0:(q + 1) * P], q_t[at, q, n % GROUP, :],
                                         k_t[at, s, 0:(q + 1) * P], start=True, stop=True)
                    if HEADS // 2 - 1 in banks:
                        last.then_inc(scored, 1)

            def turn_o(u):
                if in_range(u, UNITS):
                    if in_range(u + 4, UNITS):
                        pe.wait_ge(q_copied, u + 5)
                    pe.wait_ge(o_normed, u + 1)
                    for j in range(GROUP):
                        last = pe.transpose(ps_qy[:, j, :], o_n[:, j].rearrange("p g d -> p (g d)"), ident[:])
                    last.then_inc(o_turned, 1)

            def step(u, r):
                v, rv = u - 3, (r - 3) % 4
                turn_p(v, rv, 0)
                turn_o(u - 4)
                score(u, r, (0, 1))
                project_out(u - 4)
                turn_q(u + 1, (r + 1) % 4)
                if rv % 2:
                    turn_p(v, rv, 1)
                score(u, r, (2,))
                turn_k(u + 1, (r + 1) % 4)
                score(u, r, (3,))
                mix(v, rv, in_range(u + 1, UNITS))

            ps_o = ps_ko[:].rearrange("p a b -> p (a b)").rearrange("p (n d) -> p n d", d=HD)
            turn_q(0, 0)
            turn_k(0, 0)
            all_steps(pe, step)


def route(nc, h, ident, ones_row, router_rev, router_b_rev, mv, rstd, x_hi, x_lo, comb_t, comb_rows, f, loader):
    QT = GT // P
    QUADS = TILES // QT
    with ExitStack() as ctx:
        def sb(name, shape, dt=F32):
            return ctx.enter_context(nc.sbuf_tensor(name, shape, dt))

        def sem(name):
            return ctx.enter_context(nc.semaphore(name))

        rw = sb("rw", [P, EXPERTS])
        rb = sb("rb", [1, EXPERTS])
        shifted = sb("r_shifted", [P, TILES])
        root = sb("r_root", [P, TILES])
        xn = sb("r_xn", [P, 2, QT, DIM])
        x_s = sb("x_s", [P, 2, GT])
        neg_max = sb("r_neg_max", [P, QT])
        d1 = sb("d1", [P, QT, EXPERTS])
        e1 = sb("e1", [P, QT, EXPERTS])
        neg_s1 = sb("neg_s1", [P, QT])
        neg_r1 = sb("neg_r1", [P, QT])
        neg_p = sb("neg_p", [P, QT, EXPERTS])
        d2 = sb("d2", [P, QT, EXPERTS])
        e2 = sb("e2", [P, QT, EXPERTS])
        left = sb("left", [P, QT, EXPERTS])
        low = sb("low", [P, QT, 8])
        top = sb("top", [P, QT, EXPERTS])
        s2 = sb("s2", [P, QT])
        r2 = sb("r2", [P, QT])
        comb = sb("comb", [P, 2, QT, EXPERTS])
        ps_x = ctx.enter_context(nc.psum_tensor("r_ps_x", [P, 2, GT], F32))
        ps_l = ctx.enter_context(nc.psum_tensor("ps_l", [P, 2, 512], F32))
        ps_c = ctx.enter_context(nc.psum_tensor("r_ps_c", [P, 2, GT], F32))
        loads = sem("r_loads")
        var_eps = sem("r_var_eps")
        rooted = sem("r_rooted")
        rstd_ready = sem("r_rstd_ready")
        normed = sem("r_normed")
        turned = sem("r_turned")
        x_copied = sem("r_x_copied")
        hi_ready = sem("hi_ready")
        x_used = sem("x_used")
        logits = sem("logits")
        max_ready = sem("r_max_ready")
        d1_ready = sem("d1_ready")
        exp_one = sem("exp_one")
        d2_ready = sem("d2_ready")
        exp_two = sem("exp_two")
        sum_step = sem("sum_step")
        top_step = sem("top_step")
        comb_ready = sem("comb_ready")
        comb_turned = sem("comb_turned")
        comb_copied = sem("comb_copied")
        block = ctx.enter_context(nc.Block(name="route"))

        def cols(q):
            return bass.ds(q * GT, GT)

        def spread(of_tile):
            return of_tile[:].unsqueeze(2).broadcast_to([P, QT, EXPERTS])

        @block.sync
        def _(sp):
            sp.dma_start(rw[:], router_rev).then_inc(loads, 16)
            sp.dma_start(rb[:], router_b_rev.rearrange("(a n) -> a n", a=1)).then_inc(loads, 16)

            def write_rows(q):
                sp.wait_ge(comb_copied, q + 1)
                sp.dma_start(comb_rows[:, cols(q)], comb_t[:, cols(q)]).then_inc(f["rows_out"], 16)

            loader.biases(sp)
            for r in range(WRING):
                loader.weights(sp, r, r)
            for q in range(GROUPS):
                write_rows(q)
            sp.wait_ge(f["rows_out"], 16 * GROUPS)
            for r in range(WRING):
                loader.row(sp, 0, r, r)
            for q in range(GROUPS, QUADS):
                write_rows(q)

        @block.scalar
        def _(act):
            act.wait_ge(var_eps, 1)
            act.activation(root[:], shifted[:], ACT.Sqrt).then_inc(rooted, 1)

            def copy_x(q, b):
                act.wait_ge(turned, q + 1)
                after(act, x_used, q - 1)
                act.activation(x_s[:, b], ps_x[:, b], ACT.Copy).then_inc(x_copied, 1)
                act.activation(x_hi[:, cols(q)], ps_x[:, b], ACT.Copy).then_inc(hi_ready, 1)

            def copy_comb(q, b):
                if in_range(q, QUADS):
                    hold(act, comb_turned, q + 1)
                    act.activation(comb_t[:, cols(q)], ps_c[0:EXPERTS, b], ACT.Copy).then_inc(comb_copied, 1)

            def step(q, b):
                copy_x(q, b)
                act.wait_ge(d1_ready, q + 1)
                act.activation(e1[:], d1[:], ACT.Exp).then_inc(exp_one, 1)
                copy_comb(q - 1, 1 - b)
                act.wait_ge(d2_ready, q + 1)
                act.activation(e2[:], d2[:], ACT.Exp, scale=-1.0).then_inc(exp_two, 1)

            repeat(act, step, QUADS)
            copy_comb(QUADS - 1, 1)

        @block.gpsimd
        def _(pool):
            def step(q, b):
                pool.wait_ge(hi_ready, q + 1)
                pool.tensor_tensor(x_lo[:, cols(q)], x_s[:, b], x_hi[:, cols(q)].bitcast(F32), ALU.subtract
                                   ).then_inc(x_used, 1)

            repeat(pool, step, QUADS)
            for r in range(SPLIT_EARLY):
                split_weights(pool, f, r, r, 32)

        @block.vector
        def _(dve):
            dve.tensor_scalar(shifted[:], mv[:, :, 1], LN_EPS, None, ALU.add).then_inc(var_eps, 1)
            dve.wait_ge(rooted, 1)
            dve.reciprocal(rstd[:], root[:]).then_inc(rstd_ready, 1)
            dve.wait_ge(rstd_ready, 1)

            def norm(q, b):
                if in_range(q, QUADS):
                    after(dve, turned, q - 1)
                    for k in range(QT):
                        t = q * QT + k
                        last = dve.tensor_scalar(xn[:, b, k, :], h[:, t, :], mv[:, t, 0:1], rstd[:, bass.ds(t, 1)],
                                                 ALU.subtract, ALU.mult)
                    last.then_inc(normed, 1)

            def probabilities(q, b):
                of_quad = ps_l[:, b, 0:QT * EXPERTS].rearrange("p (k e) -> p k e", k=QT)
                link = chained(dve, sum_step, q * 3)
                dve.wait_ge(logits, q + 1)
                dve.tensor_reduce(neg_max[:], of_quad, AX.X, ALU.max, negate=True).then_inc(max_ready, 1)
                hold(dve, max_ready, q + 1)
                dve.tensor_tensor(d1[:], of_quad, spread(neg_max), ALU.add).then_inc(d1_ready, 1)
                norm(q + 1, 1 - b)
                dve.wait_ge(exp_one, q + 1)
                link(dve.tensor_reduce(neg_s1[:], e1[:], AX.X, ALU.add, negate=True))
                link(dve.reciprocal(neg_r1[:], neg_s1[:]))
                link(dve.tensor_tensor(neg_p[:], e1[:], spread(neg_r1), ALU.mult))
                dve.tensor_tensor(d2[:], neg_p[:], spread(neg_r1), ALU.subtract).then_inc(d2_ready, 1)

            def choose(q, b):
                halves = (range(0, QT // 2), range(QT // 2, QT))
                before = q * STEPS
                rounds = [(taken, op) for taken in range(0, DROPPED, 8) for op in ("max", "marks", "take")
                          if op != "marks" or DROPPED - taken < 8]
                for n, (taken, op) in enumerate(rounds):
                    source = left if taken else neg_p
                    for half, tiles in enumerate(halves):
                        if n:
                            hold(dve, top_step, before + (2 * (n - 1) + half + 1))
                        if op == "marks":
                            last = dve.memset(low[:, tiles.start:tiles.stop, DROPPED - taken:8], MARK)
                        for k in tiles:
                            if op == "max":
                                last = dve.max(low[:, k, :], source[:, k, :])
                            if op == "take":
                                last = dve.match_replace(left[:, k, :], low[:, k, :], source[:, k, :], MARK)
                        last.then_inc(top_step, 1)
                link = chained(dve, top_step, before + 2 * len(rounds))
                hold(dve, top_step, before + 2 * len(rounds))
                dve.wait_ge(exp_two, q + 1)
                link(dve.scalar_tensor_tensor(out=top[:], in0=left[:], scalar=MARK, in1=e2[:], op0=ALU.is_gt,
                                              op1=ALU.mult))
                link(dve.tensor_reduce(s2[:], top[:], AX.X, ALU.add))
                link(dve.reciprocal(r2[:], s2[:]))
                after(dve, comb_turned, q - 1)
                dve.tensor_tensor(comb[:, b], top[:], spread(r2), ALU.mult).then_inc(comb_ready, 1)

            def step(q, b):
                if not isinstance(q, int) or q > 0:
                    hold(dve, comb_ready, q)
                probabilities(q, b)
                choose(q, b)

            ROUNDS = -(-DROPPED // 8)
            STEPS = 2 * (2 * ROUNDS + 1) + 3
            norm(0, 0)
            repeat(dve, step, QUADS - 2)
            for q in (QUADS - 2, QUADS - 1):
                step(q, q % 2)

        @block.tensor
        def _(pe):
            pe.wait_ge(loads, 32)

            def turn_x(q, b):
                pe.wait_ge(normed, q + 1)
                after(pe, hi_ready, q - 1)
                for k in range(QT):
                    last = pe.transpose(ps_x[:, b, k * P:(k + 1) * P], xn[:, b, k, :], ident[:])
                last.then_inc(turned, 1)

            def logit(q, b):
                pe.wait_ge(x_copied, q + 1)
                after(pe, d1_ready, q - 1)
                for k in range(QT):
                    of_tile = ps_l[:, b, k * EXPERTS:(k + 1) * EXPERTS]
                    pe.matmul(of_tile, x_s[:, b, k * P:(k + 1) * P], rw[:], start=True, stop=False)
                    last = pe.matmul(of_tile, ones_row[:], rb[:], start=False, stop=True)
                last.then_inc(logits, 1)

            def turn_comb(q, b):
                if in_range(q, QUADS):
                    after(pe, comb_copied, q - 1)
                    hold(pe, comb_ready, q + 1)
                    for k in range(QT):
                        last = pe.transpose(ps_c[0:EXPERTS, b, k * P:(k + 1) * P], comb[:, b, k, :], ident[:])
                    last.then_inc(comb_turned, 1)

            def step(q, r):
                turn_x(q, r % 2)
                logit(q, r % 2)
                turn_comb(q - 1, (r - 1) % 2)

            repeat(pe, step, QUADS, 4)
            turn_comb(QUADS - 1, 1)


def expert_buffers(nc, ctx):
    def sb(name, shape, dt=F32):
        return ctx.enter_context(nc.sbuf_tensor(name, shape, dt))

    def sem(name):
        return ctx.enter_context(nc.semaphore(name))

    return {
        "w_raw": sb("w_raw", [P, WRING, 2, HIDDEN]),
        "w_hi": sb("w_hi", [P, WRING, 2, HIDDEN], F32R),
        "w_lo": sb("w_lo", [P, WRING, 2, HIDDEN], F32R),
        "c_row": sb("c_row", [P, WRING, SWEEP_TOKENS]),
        "b1_rows": sb("b1_rows", [EXPERTS, HIDDEN]),
        "b2_rows": sb("b2_rows", [EXPERTS, DIM]),
        "b1_in": sem("b1_in"),
        "b2_in": sem("b2_in"),
        "w_in": [sem(f"w_in{k}") for k in range(WRING)],
        "row_in": [sem(f"row_in{k}") for k in range(WRING)],
        "rows_out": sem("rows_out"),
        "hi_copied": sem("hi_copied"),
        "w_split": sem("w_split"),
    }


class ExpertLoads:

    def __init__(self, f, comb_rows, w1, b1, w2, b2_rev):
        self.f, self.comb_rows, self.w1, self.b1, self.w2, self.b2_rev = f, comb_rows, w1, b1, w2, b2_rev

    def biases(self, sp):
        sp.dma_start(self.f["b1_rows"][:], self.b1).then_inc(self.f["b1_in"], 16)
        sp.dma_start(self.f["b2_rows"][:], self.b2_rev).then_inc(self.f["b2_in"], 16)

    def weights(self, sp, e, r):
        w_raw, w_in = self.f["w_raw"], self.f["w_in"][r]
        sp.dma_start(w_raw[:, r, 0, :], self.w1[e]).then_inc(w_in, 16)
        sp.dma_start(w_raw[:, r, 1, :].rearrange("p (c n) -> p c n", n=DIM),
                     self.w2[e].rearrange("(c p) n -> p c n", p=P)).then_inc(w_in, 16)

    def row(self, sp, w, e, r):
        row = self.comb_rows[bass.ds(EXPERTS - 1 - e, 1), bass.ds(w * SWEEP_TOKENS, SWEEP_TOKENS)]
        sp.dma_start(self.f["c_row"][:, r, :], row.broadcast_to([P, SWEEP_TOKENS])).then_inc(self.f["row_in"][r], 16)


def split_weights(pool, f, e, r, loaded, free=None):
    w_raw, w_hi, w_lo = f["w_raw"], f["w_hi"], f["w_lo"]
    pool.wait_ge(f["w_in"][r], loaded)
    if free is not None:
        free()
    pool.tensor_copy(w_hi[:, r], w_raw[:, r]).then_inc(f["hi_copied"], 1)
    pool.wait_ge(f["hi_copied"], e + 1)
    pool.tensor_tensor(w_lo[:, r], w_raw[:, r], w_hi[:, r].bitcast(F32), ALU.subtract).then_inc(f["w_split"], 1)


def experts(nc, h, ident, x_hi, x_lo, comb_t, f, loader, out):
    LAG = 4
    RING = LAG
    STEPS = GROUPS * EXPERTS
    BODY = GROUPS * WRING
    ROUNDS = EXPERTS // WRING
    HC = HIDDEN // P
    GTILES = GT // P
    with ExitStack() as ctx:
        def sb(name, shape, dt=F32):
            return ctx.enter_context(nc.sbuf_tensor(name, shape, dt))

        def sem(name):
            return ctx.enter_context(nc.semaphore(name))

        w_hi, w_lo, c_row, b1_rows, b2_rows, b1_in, b2_in, row_in, w_split = (
            f[k] for k in ("w_hi", "w_lo", "c_row", "b1_rows", "b2_rows", "b1_in", "b2_in", "row_in", "w_split"))
        b1_t = sb("b1_t", [P, HC, EXPERTS])
        act_out = sb("act_out", [P, 2, HC, GT])
        scaled = sb("scaled", [P, RING, HC, GT])
        s_hi = sb("s_hi", [P, RING, HC, GT], F32R)
        s_lo = sb("s_lo", [P, RING, HC, GT], F32R)
        y_t = sb("y_t", [P, GROUPS, GT])
        ps_h = ctx.enter_context(nc.psum_tensor("f_ps_h", [P, 2, HC, GT], F32))
        ps_y = ctx.enter_context(nc.psum_tensor("f_ps_y", [P, GROUPS, GT], F32))
        b1_turned = sem("b1_turned")
        hidden = sem("hidden")
        gelu_done = sem("gelu_done")
        scaled_ready = sem("scaled_ready")
        hi_ready = sem("s_hi_ready")
        lo_ready = sem("s_lo_ready")
        summed = sem("summed")
        y_copied = sem("y_copied")
        y_turned = sem("y_turned")
        y_added = sem("f_y_added")
        stored = sem("stored")
        block = ctx.enter_context(nc.Block(name="experts"))
        y_tokens = out.rearrange("b s d -> (b s) d").rearrange("(w t p) d -> w p t d", w=SWEEPS, p=P)

        @block.sync
        def _(sp):
            def load(w, e, r):
                hold(sp, w_split, w * EXPERTS + e - (WRING - 1))
                loader.weights(sp, e, r)
                hold(sp, scaled_ready, (w * EXPERTS + e) * GROUPS - (WRING - 1) * GROUPS)
                loader.row(sp, w, e, r)

            def store(w):
                for g in range(GROUPS):
                    sp.wait_ge(y_added, (w + 1) * GROUPS + g + 1)
                    tiles = slice(g * GTILES, (g + 1) * GTILES)
                    sp.dma_start(y_tokens[w, :, tiles, :], h[:, w * GROUPS * GTILES:(w + 1) * GROUPS * GTILES, :]
                                 [:, tiles, :]).then_inc(stored, 16)

            with sp.Fori(1, ROUNDS) as i:
                for r in range(WRING):
                    load(0, i * WRING + r, r)
            sp.wait_ge(f["rows_out"], 16 * (TOKENS // GT))
            for w in range(1, SWEEPS):
                with sp.Fori(0, ROUNDS) as i:
                    for r in range(WRING):
                        load(w, i * WRING + r, r)
                store(w - 1)
            store(SWEEPS - 1)
            sp.wait_ge(stored, 16 * SWEEPS * GROUPS)

        @block.gpsimd
        def _(pool):
            def split(e, r, loaded):
                def free():
                    hold(pool, summed, e * GROUPS - (WRING - 1) * GROUPS)

                split_weights(pool, f, e, r, loaded, free)

            for r in range(SPLIT_EARLY, WRING):
                split_weights(pool, f, r, r, 32)
            with pool.Fori(1, SWEEPS * ROUNDS) as i:
                for r in range(WRING):
                    split(i * WRING + r, r, i * 32 + 32)

        @block.scalar
        def _(act):
            def gelu(S, e, r):
                hold(act, hidden, S + 1)
                for c in range(HC):
                    last = act.activation(act_out[:, r % 2, c, :], ps_h[:, r % 2, c, :], ACT.Gelu,
                                          bias=b1_t[:, c, bass.ds(e, 1)])
                last.then_inc(gelu_done, 1)

            def high(S, r, reuse):
                act.wait_ge(scaled_ready, S + 1)
                if reuse:
                    act.wait_ge(summed, S - (LAG - 1))
                act.activation(s_hi[:, r % RING], scaled[:, r % RING], ACT.Copy).then_inc(hi_ready, 1)

            act.wait_ge(y_added, GROUPS)
            with act.Fori(0, SWEEPS) as w:
                start = w * STEPS
                for r in range(BODY):
                    gelu(start + r, r // GROUPS, r)
                    if r:
                        high(start + (r - 1), r - 1, r - 1 >= LAG)
                with act.Fori(1, STEPS // BODY) as i:
                    for r in range(BODY):
                        gelu(start + i * BODY + r, i * WRING + r // GROUPS, r)
                        high(start + i * BODY + (r - 1), (r - 1) % BODY, True)
                high(start + (STEPS - 1), BODY - 1, True)
                act.wait_ge(summed, start + STEPS)
                for g in range(GROUPS):
                    act.activation(y_t[:, g, :], ps_y[:, g, :], ACT.Copy).then_inc(y_copied, 1)

        @block.vector
        def _(dve):
            dve.wait_ge(b1_turned, 1)
            dve.tensor_copy(b1_t[:], ps_h[:, 0, 0, 0:HC * EXPERTS].rearrange("p (c e) -> p c e", c=HC)
                            ).then_inc(y_added, GROUPS)

            def scale(S, rows_loaded, r, reuse):
                g, k = r % GROUPS, r // GROUPS
                if g == 0:
                    dve.wait_ge(row_in[k], rows_loaded)
                if reuse:
                    dve.wait_ge(lo_ready, S - (RING - 1))
                dve.wait_ge(gelu_done, S + 1)
                dve.tensor_tensor(scaled[:, r % RING], act_out[:, r % 2],
                                  c_row[:, k, g * GT:(g + 1) * GT].unsqueeze(1).broadcast_to([P, HC, GT]), ALU.mult
                                  ).then_inc(scaled_ready, 1)

            def low(S, r):
                dve.wait_ge(hi_ready, S + 1)
                dve.tensor_tensor(s_lo[:, r % RING], scaled[:, r % RING], s_hi[:, r % RING].bitcast(F32), ALU.subtract
                                  ).then_inc(lo_ready, 1)

            with dve.Fori(0, SWEEPS) as w:
                start = w * STEPS
                rows = w * (16 * ROUNDS)
                for r in range(BODY):
                    scale(start + r, rows + 16, r, r >= RING)
                    if r:
                        low(start + (r - 1), r - 1)
                with dve.Fori(1, STEPS // BODY) as i:
                    for r in range(BODY):
                        scale(start + i * BODY + r, rows + i * 16 + 16, r, True)
                        low(start + i * BODY + (r - 1), (r - 1) % BODY)
                low(start + (STEPS - 1), BODY - 1)
                for g in range(GROUPS):
                    hold(dve, y_turned, w * GROUPS + (g + 1))
                    tiles = bass.ds(w * (GROUPS * GTILES) + g * GTILES, GTILES)
                    dve.tensor_tensor(h[:, tiles, :], h[:, tiles, :],
                                      ps_h[:, g // HC, g % HC, :].rearrange("p (t d) -> p t d", d=DIM), ALU.add
                                      ).then_inc(y_added, 1)

        @block.tensor
        def _(pe):
            pe.wait_ge(b1_in, 16)
            for c in range(HC):
                last = pe.transpose(ps_h[:, 0, 0, c * EXPERTS:(c + 1) * EXPERTS], b1_rows[:, c * P:(c + 1) * P],
                                    ident[0:EXPERTS, 0:EXPERTS])
            last.then_inc(b1_turned, 1)
            pe.wait_ge(b2_in, 16)

            def tokens(w, g):
                return bass.ds(w * SWEEP_TOKENS + g * GT, GT)

            def first(S, e, w, r, reuse):
                g, k = r % GROUPS, r // GROUPS
                if g == 0:
                    pe.wait_ge(w_split, e + 1)
                if reuse:
                    pe.wait_ge(gelu_done, S - 1)
                for c in range(HC):
                    at = slice(c * P, (c + 1) * P)
                    to = ps_h[:, r % 2, c, :]
                    pe.matmul(to, w_hi[:, k, 0, at], x_hi[:, tokens(w, g)], start=True, stop=False)
                    pe.matmul(to, w_hi[:, k, 0, at], x_lo[:, tokens(w, g)], start=False, stop=False)
                    last = pe.matmul(to, w_lo[:, k, 0, at], x_hi[:, tokens(w, g)], start=False, stop=True)
                last.then_inc(hidden, 1)

            def second(S, r, last_step):
                g, k, slot = r % GROUPS, r // GROUPS, r % RING
                pe.wait_ge(lo_ready, S + 1)
                for c in range(HC):
                    at = slice(c * P, (c + 1) * P)
                    pe.matmul(ps_y[:, g, :], w_hi[:, k, 1, at], s_hi[:, slot, c, :], start=False, stop=False)
                    pe.matmul(ps_y[:, g, :], w_hi[:, k, 1, at], s_lo[:, slot, c, :], start=False, stop=False)
                    last = pe.matmul(ps_y[:, g, :], w_lo[:, k, 1, at], s_hi[:, slot, c, :], start=False,
                                     stop=last_step and c == HC - 1)
                last.then_inc(summed, 1)

            with pe.Fori(0, SWEEPS) as w:
                start = w * STEPS
                pe.wait_ge(y_added, w * GROUPS + GROUPS)
                for r in range(BODY):
                    if r >= LAG:
                        second(start + (r - LAG), r - LAG, False)
                    first(start + r, w * EXPERTS + r // GROUPS, w, r, r >= 2)
                    if r == 1:
                        for g in range(GROUPS):
                            pe.matmul(ps_y[:, g, :], b2_rows[:], comb_t[:, tokens(w, g)], start=True, stop=False)
                with pe.Fori(1, STEPS // BODY) as i:
                    for r in range(BODY):
                        at = start + i * BODY
                        second(at + (r - LAG), (r - LAG) % BODY, False)
                        first(at + r, w * EXPERTS + i * WRING + r // GROUPS, w, r, True)
                for r in range(LAG):
                    second(start + (STEPS - LAG + r), BODY - LAG + r, True)
                for g in range(GROUPS):
                    pe.wait_ge(y_copied, w * GROUPS + (g + 1))
                    for t in range(GTILES):
                        last = pe.transpose(ps_h[:, g // HC, g % HC, t * P:(t + 1) * P],
                                            y_t[:, g, t * P:(t + 1) * P], ident[:])
                    last.then_inc(y_turned, 1)


_OUTS = [((BATCH, SEQ, DIM), "float32")]


def kernel(**inputs):
    import concourse.bacc as _bacc
    from concourse.bass_utils import run_bass_kernel_spmd as _run

    half = DR // 2
    inv_freq = 1.0 / 500000.0 ** (np.arange(0, DR, 2, dtype=np.float32) / DR)
    freqs = np.outer(np.arange(SEQ, dtype=np.float32), inv_freq)
    cos, sin = np.cos(freqs).astype(np.float32), np.sin(freqs).astype(np.float32)
    laid = {
        "tok": inputs["x"],
        "pos": inputs["fside_BS_position"],
        "emb": inputs["L0_tok_embeddings"],
        "centers": inputs["L0_tok_centers"],
        "logvar": inputs["L0_tok_log_variances"],
    }
    for name in ("W_DQ", "W_UQ", "W_QR", "W_DKV", "W_UK", "W_UV", "W_KR", "W_VR", "W_O", "q_ln_w", "kv_ln_w",
                 "q_head_norm_w", "k_head_norm_w"):
        laid[name.lower()] = inputs["L0_attn_" + name]
    laid["w1"] = inputs["L0_ffn_w1"]
    laid["b1"] = inputs["L0_ffn_b1"]
    laid["w2"] = inputs["L0_ffn_w2"]
    laid["b2_rev"] = np.asarray(inputs["L0_ffn_b2"])[::-1]
    laid["router_rev"] = np.asarray(inputs["L0_ffn_router_w"])[:, ::-1]
    laid["router_b_rev"] = np.asarray(inputs["L0_ffn_router_b"])[::-1]
    laid["rope_cos"] = cos
    laid["rope_sin"] = np.stack([-sin, sin])

    nc = _bacc.Bacc("TRN2", target_bir_lowering=False, num_devices=1)
    arrays, args = {}, []
    for name, value in laid.items():
        a = np.ascontiguousarray(value)
        arrays[f"in_{name}"] = a
        args.append(nc.dram_tensor(f"in_{name}", a.shape, mybir.dt.from_np(a.dtype), kind="ExternalInput").ap())
    out = nc.dram_tensor("out_0", _OUTS[0][0], F32, kind="ExternalOutput").ap()
    lm_tower(nc, *args, out)
    r = _run(nc, [arrays], core_ids=[0])
    return r.results[0]["out_0"]
```
